# Optimizing a Trainium2 kernel written in Bass

```python
import numpy as np
import jax
import jax.numpy as jnp

def _softmax(x, axis=-1):
    return jax.nn.softmax(x, axis=axis)

def _gelu(x):
    return jax.nn.gelu(x, approximate=True)

def _silu(x):
    return jax.nn.silu(x)

def _sigmoid(x):
    return jax.nn.sigmoid(x)

def _layernorm(x, axis=-1, eps=1e-05):
    m = jnp.mean(x, axis=axis, keepdims=True)
    v = jnp.var(x, axis=axis, keepdims=True)
    return (x - m) / jnp.sqrt(v + eps)

def _scatter_add(tgt, idx, src, axis=0):
    return tgt.at[idx].add(src)

def _segment_sum(src, seg, n):
    return jax.ops.segment_sum(src, seg, n)
kernel_name = 'mk_decoder_preln_d1_seqx_r4_e13d2f'

def setup_inputs(seed: int=0):
    np.random.seed(seed)
    _w = jnp.asarray

    def _rec_inputs():
        import jax
        import jax.numpy as jnp
        _rk = jax.random.key(seed)
        x = 7.22e-05 + 1 * jax.random.normal(jax.random.fold_in(_rk, 1), (32, 256, 256), jnp.float32)
        _lenS = 256 - jax.random.randint(jax.random.fold_in(_rk, 7), (32,), 0, max(1, 256 // 4) + 1, jnp.int32)
        _lenS2 = 77 - jax.random.randint(jax.random.fold_in(_rk, 8), (32,), 0, max(1, 77 // 4) + 1, jnp.int32)
        _ctx_1024P = jax.random.normal(jax.random.fold_in(_rk, 11), (32, 16, 256), jnp.float32)
        _ctx_1024c = jax.random.dirichlet(jax.random.fold_in(_rk, 511), 0.3 * jnp.ones((16,), jnp.float32), (32, 77))
        _ctx_1024t = jnp.einsum('bsk,bkd->bsd', _ctx_1024c, _ctx_1024P)
        _ctx_1024t = _ctx_1024t * jax.lax.rsqrt(jnp.mean(jnp.square(_ctx_1024t)) + 1e-12) * 0.953939
        ctx_1024 = 4.13588e-05 + 0.999923 * (_ctx_1024t + 0.3 * jax.random.normal(jax.random.fold_in(_rk, 611), (32, 77, 256), jnp.float32))
        _validS = jnp.arange(256)[None, :] < _lenS[:, None]
        _validS2 = jnp.arange(77)[None, :] < _lenS2[:, None]
        _causal = jnp.tril(jnp.ones((256, 256), dtype=bool))
        mask_Bx1xSxS2_bk0 = jnp.logical_not(jnp.broadcast_to(_validS2[:, None, None, :], (32, 1, 256, 77)))
        return (x, ctx_1024, mask_Bx1xSxS2_bk0)
    x, ctx_1024, mask_Bx1xSxS2_bk0 = _rec_inputs()

    def _L0_attn_setup():
        import jax, jax.numpy as jnp
        import numpy as np
        H = 4
        M = 64
        KS = 4
        EPS = 1e-05
        BASE = 10000.0

        def _short_conv(x, w):
            B, T, D = x.shape
            xp = jnp.pad(x.transpose(0, 2, 1), ((0, 0), (0, 0), (w.shape[-1] - 1, 0)))
            y = jax.lax.conv_general_dilated(xp, w, (1,), 'VALID', dimension_numbers=('NCH', 'OIH', 'NCH'), feature_group_count=D)
            return jax.nn.silu(y).transpose(0, 2, 1)

        def _rope(q, k):
            T, hk = (q.shape[1], q.shape[-1])
            inv_freq = 1.0 / BASE ** (jnp.arange(0, hk, 2, dtype=jnp.float32) / hk)
            freqs = jnp.arange(T, dtype=jnp.float32)[:, None] * inv_freq[None, :]
            emb = jnp.concatenate([freqs, freqs], -1)
            cos = jnp.cos(emb)[None, :, None, :]
            sin = jnp.sin(emb)[None, :, None, :]

            def rot(x):
                x1, x2 = jnp.split(x, 2, -1)
                return jnp.concatenate([-x2, x1], -1)
            return (q * cos + rot(q) * sin, k * cos + rot(k) * sin)

        def _chunk_abc(q, k, v, s):
            B, T, Hn, Kd = q.shape
            scale = Kd ** (-0.5)
            to_t = lambda x: x.transpose(1, 0, 2, 3)
            q = to_t(q) * scale
            k = to_t(k)
            v = to_t(v)
            s = to_t(s)
            z = jax.lax.cumlogsumexp(s, axis=0)
            z_prev = jnp.concatenate([jnp.zeros_like(z[:1]), z[:-1]], 0)
            g = jnp.exp(z_prev - z)
            s_norm = jnp.exp(s - z)
            Mn, Vd = (s.shape[-1], v.shape[-1])
            hk0 = jnp.zeros((B, Hn, Kd, Mn), jnp.float32)

            def step1(hk, inp):
                qi, ki, si, gi = inp
                hk = hk * gi[:, :, None, :] + ki[..., None] * si[:, :, None, :]
                return (hk, jnp.einsum('bhk,bhkm->bhm', qi, hk))
            _, ok = jax.lax.scan(step1, hk0, (q, k, s_norm, g))
            qv = jax.nn.softmax(ok, -1)
            hv0 = jnp.zeros((B, Hn, Mn, Vd), jnp.float32)

            def step2(hv, inp):
                qvi, si, vi, gi = inp
                hv = hv * gi[..., None] + si[..., None] * vi[:, :, None, :]
                return (hv, jnp.einsum('bhm,bhmv->bhv', qvi, hv))
            _, ov = jax.lax.scan(step2, hv0, (qv, s_norm, v, g))
            return ov.transpose(1, 0, 2, 3)
        key = jax.random.key(seed)
        ks = jax.random.split(key, 11)
        B, T, D = (4, 512, 256)
        Kd, Vd = (128, 256)
        w = lambda k, shape: jax.random.normal(k, shape, jnp.float32) * 0.02
        return {'hidden_states': jax.random.normal(ks[0], (B, T, D), jnp.float32), 'Wq': w(ks[1], (D, Kd)), 'Wk': w(ks[2], (D, Kd)), 'Wv': w(ks[3], (D, Vd)), 'Ws': w(ks[4], (D, H * M)), 'Wg': w(ks[5], (D, Vd)), 'Wo': w(ks[6], (Vd, D)), 'qconv_w': w(ks[7], (Kd, 1, KS)), 'kconv_w': w(ks[8], (Kd, 1, KS)), 'vconv_w': w(ks[9], (Vd, 1, KS)), 'gnorm_w': jnp.ones((Vd // H,), jnp.float32)}
    _L0_attn_all = _L0_attn_setup()
    _L0_attn_in = {k: v for k, v in _L0_attn_all.items() if k in ('Wq', 'Wk', 'Wv', 'Ws', 'Wg', 'Wo', 'qconv_w', 'kconv_w', 'vconv_w', 'gnorm_w')}
    del _L0_attn_all

    def _L0_xattn_setup():
        import jax, jax.numpy as jnp
        import numpy as np
        D_MODEL = 256
        N_HEADS = 16
        D_HEAD = D_MODEL // N_HEADS
        B = 4
        S = 512
        NEG_INF = -10000000000.0
        key = jax.random.key(seed)
        ks = jax.random.split(key, 8)
        queries = jax.random.normal(ks[0], (B, S, D_MODEL), dtype=jnp.float32)
        keys = jax.random.normal(ks[1], (B, S, D_MODEL), dtype=jnp.float32)
        values = jax.random.normal(ks[2], (B, S, D_MODEL), dtype=jnp.float32)
        causal = jnp.tril(jnp.ones((S, S), dtype=bool))
        mask = jnp.broadcast_to(causal[None, None, :, :], (B, 1, S, S))
        sc = 1.0 / np.sqrt(D_MODEL)
        W_q = jax.random.normal(ks[3], (D_MODEL, D_MODEL), dtype=jnp.float32) * sc
        W_k = jax.random.normal(ks[4], (D_MODEL, D_MODEL), dtype=jnp.float32) * sc
        W_v = jax.random.normal(ks[5], (D_MODEL, D_MODEL), dtype=jnp.float32) * sc
        W_proj = jax.random.normal(ks[6], (D_MODEL, D_MODEL), dtype=jnp.float32) * sc
        b_proj = jnp.zeros((D_MODEL,), dtype=jnp.float32)
        return {'queries': queries, 'keys': keys, 'values': values, 'mask': mask, 'W_q': W_q, 'W_k': W_k, 'W_v': W_v, 'W_proj': W_proj, 'b_proj': b_proj}
    _L0_xattn_all = _L0_xattn_setup()
    _L0_xattn_in = {k: v for k, v in _L0_xattn_all.items() if k in ('W_q', 'W_k', 'W_v', 'W_proj', 'b_proj')}
    del _L0_xattn_all

    def _L0_ffn_setup():
        import jax, jax.numpy as jnp
        import numpy as np
        B, N, D, E, R, K = (4, 512, 256, 8, 64, 2)
        key = jax.random.key(seed)
        ks = jax.random.split(key, 5)
        scale = 0.02
        return {'x': jax.random.normal(ks[0], (B, N, D), dtype=jnp.float32), 'gate_w': jax.random.normal(ks[1], (D, E), dtype=jnp.float32) * scale, 'Wu': jax.random.normal(ks[2], (E, D, R), dtype=jnp.float32) * scale, 'Wv': jax.random.normal(ks[3], (E, D, R), dtype=jnp.float32) * scale, 'Wo': jax.random.normal(ks[4], (E, R, D), dtype=jnp.float32) * scale}
    _L0_ffn_all = _L0_ffn_setup()
    _L0_ffn_in = {k: v for k, v in _L0_ffn_all.items() if k in ('gate_w', 'Wu', 'Wv', 'Wo')}
    del _L0_ffn_all
    return {'x': x, 'ctx_1024': ctx_1024, 'mask_Bx1xSxS2_bk0': mask_Bx1xSxS2_bk0, 'L0_attn_Wq': _L0_attn_in['Wq'], 'L0_attn_Wk': _L0_attn_in['Wk'], 'L0_attn_Wv': _L0_attn_in['Wv'], 'L0_attn_Ws': _L0_attn_in['Ws'], 'L0_attn_Wg': _L0_attn_in['Wg'], 'L0_attn_Wo': _L0_attn_in['Wo'], 'L0_attn_qconv_w': _L0_attn_in['qconv_w'], 'L0_attn_kconv_w': _L0_attn_in['kconv_w'], 'L0_attn_vconv_w': _L0_attn_in['vconv_w'], 'L0_attn_gnorm_w': _L0_attn_in['gnorm_w'], 'L0_xattn_W_q': _L0_xattn_in['W_q'], 'L0_xattn_W_k': _L0_xattn_in['W_k'], 'L0_xattn_W_v': _L0_xattn_in['W_v'], 'L0_xattn_W_proj': _L0_xattn_in['W_proj'], 'L0_xattn_b_proj': _L0_xattn_in['b_proj'], 'L0_ffn_gate_w': _L0_ffn_in['gate_w'], 'L0_ffn_Wu': _L0_ffn_in['Wu'], 'L0_ffn_Wv': _L0_ffn_in['Wv'], 'L0_ffn_Wo': _L0_ffn_in['Wo']}

def reference(x, ctx_1024, mask_Bx1xSxS2_bk0, L0_attn_Wq, L0_attn_Wk, L0_attn_Wv, L0_attn_Ws, L0_attn_Wg, L0_attn_Wo, L0_attn_qconv_w, L0_attn_kconv_w, L0_attn_vconv_w, L0_attn_gnorm_w, L0_xattn_W_q, L0_xattn_W_k, L0_xattn_W_v, L0_xattn_W_proj, L0_xattn_b_proj, L0_ffn_gate_w, L0_ffn_Wu, L0_ffn_Wv, L0_ffn_Wo):
    import jax
    import jax.numpy as jnp

    def _L0_attn_ref(hidden_states, Wq, Wk, Wv, Ws, Wg, Wo, qconv_w, kconv_w, vconv_w, gnorm_w):
        import jax, jax.numpy as jnp
        import numpy as np
        H = 4
        M = 64
        KS = 4
        EPS = 1e-05
        BASE = 10000.0

        def _short_conv(x, w):
            B, T, D = x.shape
            xp = jnp.pad(x.transpose(0, 2, 1), ((0, 0), (0, 0), (w.shape[-1] - 1, 0)))
            y = jax.lax.conv_general_dilated(xp, w, (1,), 'VALID', dimension_numbers=('NCH', 'OIH', 'NCH'), feature_group_count=D)
            return jax.nn.silu(y).transpose(0, 2, 1)

        def _rope(q, k):
            T, hk = (q.shape[1], q.shape[-1])
            inv_freq = 1.0 / BASE ** (jnp.arange(0, hk, 2, dtype=jnp.float32) / hk)
            freqs = jnp.arange(T, dtype=jnp.float32)[:, None] * inv_freq[None, :]
            emb = jnp.concatenate([freqs, freqs], -1)
            cos = jnp.cos(emb)[None, :, None, :]
            sin = jnp.sin(emb)[None, :, None, :]

            def rot(x):
                x1, x2 = jnp.split(x, 2, -1)
                return jnp.concatenate([-x2, x1], -1)
            return (q * cos + rot(q) * sin, k * cos + rot(k) * sin)

        def _chunk_abc(q, k, v, s):
            B, T, Hn, Kd = q.shape
            scale = Kd ** (-0.5)
            to_t = lambda x: x.transpose(1, 0, 2, 3)
            q = to_t(q) * scale
            k = to_t(k)
            v = to_t(v)
            s = to_t(s)
            z = jax.lax.cumlogsumexp(s, axis=0)
            z_prev = jnp.concatenate([jnp.zeros_like(z[:1]), z[:-1]], 0)
            g = jnp.exp(z_prev - z)
            s_norm = jnp.exp(s - z)
            Mn, Vd = (s.shape[-1], v.shape[-1])
            hk0 = jnp.zeros((B, Hn, Kd, Mn), jnp.float32)

            def step1(hk, inp):
                qi, ki, si, gi = inp
                hk = hk * gi[:, :, None, :] + ki[..., None] * si[:, :, None, :]
                return (hk, jnp.einsum('bhk,bhkm->bhm', qi, hk))
            _, ok = jax.lax.scan(step1, hk0, (q, k, s_norm, g))
            qv = jax.nn.softmax(ok, -1)
            hv0 = jnp.zeros((B, Hn, Mn, Vd), jnp.float32)

            def step2(hv, inp):
                qvi, si, vi, gi = inp
                hv = hv * gi[..., None] + si[..., None] * vi[:, :, None, :]
                return (hv, jnp.einsum('bhm,bhmv->bhv', qvi, hv))
            _, ov = jax.lax.scan(step2, hv0, (qv, s_norm, v, g))
            return ov.transpose(1, 0, 2, 3)
        B, T, D = hidden_states.shape
        q = _short_conv(hidden_states @ Wq, qconv_w)
        k = _short_conv(hidden_states @ Wk, kconv_w)
        v = _short_conv(hidden_states @ Wv, vconv_w)
        hk = q.shape[-1] // H
        hv = v.shape[-1] // H
        q = q.reshape(B, T, H, hk)
        k = k.reshape(B, T, H, hk)
        v = v.reshape(B, T, H, hv)
        q, k = _rope(q, k)
        s = jnp.clip((hidden_states @ Ws).reshape(B, T, H, M), -32.0, 32.0)
        o = _chunk_abc(q, k, v, s)
        g = (hidden_states @ Wg).reshape(B, T, H, hv)
        var = jnp.mean(o * o, -1, keepdims=True)
        o = o * jax.lax.rsqrt(var + EPS) * gnorm_w
        o = o * jax.nn.silu(g)
        return o.reshape(B, T, H * hv) @ Wo

    def _L0_xattn_ref(queries, keys, values, mask, W_q, W_k, W_v, W_proj, b_proj):
        import jax, jax.numpy as jnp
        import numpy as np
        D_MODEL = 256
        N_HEADS = 16
        D_HEAD = D_MODEL // N_HEADS
        B = 4
        S = 512
        NEG_INF = -10000000000.0
        b, sq, _ = queries.shape
        Q = (queries @ W_q.T).reshape(b, sq, N_HEADS, D_HEAD).transpose(0, 2, 1, 3)
        K = (keys @ W_k.T).reshape(b, -1, N_HEADS, D_HEAD).transpose(0, 2, 1, 3)
        V = (values @ W_v.T).reshape(b, -1, N_HEADS, D_HEAD).transpose(0, 2, 1, 3)
        scale = jnp.sqrt(jnp.float32(D_HEAD))
        scores = jnp.einsum('bhqd,bhkd->bhqk', Q, K) / scale
        scores = jnp.where(mask, scores, NEG_INF)
        attention = jax.nn.softmax(scores, axis=-1)
        heads_out = jnp.einsum('bhqk,bhkd->bhqd', attention, V)
        heads_out = heads_out.transpose(0, 2, 1, 3).reshape(b, sq, D_MODEL)
        out = heads_out @ W_proj.T + b_proj
        return out

    def _L0_ffn_ref(x, gate_w, Wu, Wv, Wo):
        import jax, jax.numpy as jnp
        import numpy as np
        B, N, D, E, R, K = (4, 512, 256, 8, 64, 2)
        logits = jnp.einsum('bnd,de->bne', x, gate_w)
        topv, topi = jax.lax.top_k(logits, K)
        w = jax.nn.softmax(topv, axis=-1)
        u = jnp.einsum('bnd,edr->bner', x, Wu)
        v = jnp.einsum('bnd,edr->bner', x, Wv)
        s = jax.nn.silu(u) * v
        Y = jnp.einsum('bner,erd->bned', s, Wo)
        y_sel = jnp.take_along_axis(Y, topi[..., None], axis=2)
        out = jnp.einsum('bnkd,bnk->bnd', y_sel, w)
        return out
    x = x + _L0_attn_ref(_layernorm(x, axis=-1), L0_attn_Wq, L0_attn_Wk, L0_attn_Wv, L0_attn_Ws, L0_attn_Wg, L0_attn_Wo, L0_attn_qconv_w, L0_attn_kconv_w, L0_attn_vconv_w, L0_attn_gnorm_w)
    x = x + _L0_xattn_ref(_layernorm(x, axis=-1), ctx_1024, ctx_1024, mask_Bx1xSxS2_bk0, L0_xattn_W_q, L0_xattn_W_k, L0_xattn_W_v, L0_xattn_W_proj, L0_xattn_b_proj)
    x = x + _L0_ffn_ref(_layernorm(x, axis=-1), L0_ffn_gate_w, L0_ffn_Wu, L0_ffn_Wv, L0_ffn_Wo)
    return x

_drawn_inputs = setup_inputs


def setup_inputs(seed=0):
    import zlib

    import numpy as np

    out = dict(_drawn_inputs(seed))
    spreads = {'L0_attn_gnorm_w': (1.0, 0.6), 'L0_xattn_b_proj': (0.0, 0.1)}
    factors = {'L0_attn_Wq': 8.0,
     'L0_attn_Wk': 8.0,
     'L0_attn_Wv': 4.95,
     'L0_attn_Ws': 8.0,
     'L0_attn_Wg': 5.068,
     'L0_attn_Wo': 4.921,
     'L0_attn_qconv_w': 8.0,
     'L0_attn_kconv_w': 8.0,
     'L0_attn_vconv_w': 4.746,
     'L0_ffn_gate_w': 8.0,
     'L0_ffn_Wu': 8.0,
     'L0_ffn_Wv': 8.0,
     'L0_ffn_Wo': 8.0}
    for name, (base, spread) in spreads.items():
        noise = np.random.default_rng([zlib.crc32(name.encode()), seed]).standard_normal(out[name].shape)
        drawn = base * np.exp(spread * noise) if base else spread * noise
        out[name] = jnp.asarray(drawn.astype(out[name].dtype))
    for name, factor in factors.items():
        out[name] = (out[name] * factor).astype(out[name].dtype)
    return out
```

```python
from collections import namedtuple
from contextlib import ExitStack

import numpy as np

import concourse.bass as bass
from concourse import mybir

F32 = mybir.dt.float32
BF16 = mybir.dt.bfloat16
U8 = mybir.dt.uint8
U32 = mybir.dt.uint32
ALU = mybir.AluOpType
ACT = mybir.ActivationFunctionType
AX = mybir.AxisListType

P = 128
B, T, D = 32, 256, 256
TC = T // P
KC = D // P
H, M, KD, VD = 4, 64, 32, 64
TAPS = 4
S2, NH, HD = 77, 16, 16
UH = 4
QU = NH // UH
NU = TC * QU
HB = P // HD
NE, R, TOPK = 8, 64, 2
RC = NE * R // P
EPS = 1e-5
CLIP = 32.0
MASKED = -(2.0 ** 100)

Row = namedtuple("Row", "half parity")


STEPS = (
    "a_qk_ps a_v_ps a_s_ps a_g_ps a_qk_raw a_v_raw a_tap0 a_conv a_convt a_qk a_v a_rot a_cos "
    "a_sin a_kr a_qbd a_sc a_E a_C_ps a_rC a_ET_ps a_ET a_tok_ps a_ktok a_vtok a_gt a_gate "
    "a_A_ps a_A a_state_ps a_state a_ok_ps a_okn a_max a_oks a_oke a_sum a_ssq a_qn a_qnT_ps "
    "a_qnT a_P_ps a_P a_o_ps a_osq a_oss a_ove a_orinv a_o1 a_o2 a_oT_ps a_oT a_wo_ps a_x1 "
    "x_k_ps x_v_ps x_q_ps x_k x_kbd x_v x_q x_neg x_s_ps x_max x_sub x_prob x_pT_ps x_pT "
    "x_av_ps x_rs x_o x_oT_ps x_oT x_x1b x_proj_ps x_x2 f_gate_ps f_logit f_top f_topi f_topf "
    "f_gap f_egap f_gden f_gw1 f_gw2 f_wt12 f_wt f_u_ps f_v_ps f_th f_su f_s f_sw f_sT_ps "
    "f_sT f_y_ps f_y "
)
NORM_STEPS = "stats mv ve rstd xn xnT_ps xnT"
Signals = namedtuple("Signals", STEPS + NORM_STEPS)


def build(nc, a):
    ctx = ExitStack()
    with ctx:
        def sb(name, shape, dt=F32):
            return ctx.enter_context(nc.sbuf_tensor(name, shape, dt))

        def sem(name):
            return ctx.enter_context(nc.semaphore(name))

        ident = sb("ident", [P, P])
        ident_bf = sb("ident_bf", [P, P], BF16)
        tri = sb("tri", [P, P])
        ones = sb("ones", [P, P])
        cosT = sb("cosT", [P, T])
        sinT = sb("sinT", [P, T])
        headmask = sb("headmask", [P, HB])
        iota8 = sb("iota8", [P, NE])
        mhalf = sb("mhalf", [P, 2 * H])
        dve_scrap = sb("dve_scrap", [P, 1])
        pool_scrap = sb("pool_scrap", [P, 1])
        wqk = sb("wqk", [P, KC, 2, H * KD])
        wv = sb("wv", [P, KC, D])
        ws = sb("ws", [P, KC, D])
        wg = sb("wg", [P, KC, D])
        wo_raw = sb("wo_raw", [P, KC, D])
        wo = sb("wo", [P, KC, D])
        gnorm = sb("gnorm", [P, 1])
        cw = sb("cw", [P, 4, TAPS])
        xwq = sb("xwq", [P, KC, D])
        xwk = sb("xwk", [P, KC, D])
        xwv = sb("xwv", [P, KC, D])
        xwp = sb("xwp", [P, KC, D])
        xbias = sb("xbias", [P, D])
        fgate = sb("fgate", [P, KC, NE])
        fwu = sb("fwu", [P, KC, NE * R])
        fwv = sb("fwv", [P, KC, NE * R])
        fwo = sb("fwo", [P, RC, D])

        x0 = [sb(f"x0_{i}", [P, TC, D]) for i in range(2)]
        x1 = [sb(f"x1_{i}", [P, TC, D]) for i in range(2)]
        x2 = [sb(f"x2_{i}", [P, TC, D]) for i in range(2)]
        y = [sb(f"y_{i}", [P, TC, D]) for i in range(2)]
        ctxT = [sb(f"ctxT_{i}", [P, KC, S2]) for i in range(2)]
        keep = [sb(f"keep_{i}", [P, TC, S2], U8) for i in range(2)]

        ln_stats = {s: sb(f"{s}_stats", [P, TC, 6]) for s in "axf"}
        ln_mv = {s: sb(f"{s}_mv", [P, TC, 2]) for s in "axf"}
        ln_ve = {s: sb(f"{s}_ve", [P, TC]) for s in "axf"}
        ln_rstd = {s: sb(f"{s}_rstd", [P, TC]) for s in "axf"}
        xn = {s: sb(f"{s}_xn", [P, TC, D]) for s in "axf"}
        xnT = {s: sb(f"{s}_xnT", [P, KC, T]) for s in "axf"}

        raw = sb("a_raw", [P, 4, TAPS - 1 + T])
        conv = sb("a_conv", [P, 4, T])
        convt = sb("a_convt", [P, 4, T])
        qkv = sb("a_qkv", [P, 4, T])
        rot = sb("a_rot", [P, 2, T])
        qkcos = sb("a_qkcos", [P, 2, T])
        qksin = sb("a_qksin", [P, 2, T])
        kr = sb("a_kr", [P, T])
        q_bd = sb("a_q_bd", [P, H, T])
        ktok = sb("a_ktok", [P, P])
        vtok = sb("a_vtok", [P, TC, D])
        gt = sb("a_gt", [P, TC, D])
        gate = sb("a_gate", [P, TC, D])
        sc = sb("a_sc", [P, TC, D])
        E = sb("a_E", [P, TC, D])
        ET = sb("a_ET", [P, KC, T])
        rC = sb("a_rC", [P, TC, D])
        AT = sb("a_AT", [P, TC, H, P])
        PT = sb("a_PT", [P, TC, H, P])
        state = sb("a_state", [P, 2 * D])
        okn = sb("a_okn", [P, TC, D])
        oks = sb("a_oks", [P, TC, D])
        oke = sb("a_oke", [P, TC, D])
        qn = sb("a_qn", [P, TC, D])
        okmax = sb("a_okmax", [P, TC * H])
        ssum = sb("a_ssum", [P, TC * H])
        ssq = sb("a_ssq", [P, TC * H])
        qn_bd = sb("a_qn_bd", [P, 2, 2, T])
        osq = sb("a_osq", [P, TC, D])
        oss = sb("a_oss", [P, TC * H])
        ove = sb("a_ove", [P, TC * H])
        orinv = sb("a_orinv", [P, TC * H])
        o1 = sb("a_o1", [P, TC, D])
        o2 = sb("a_o2", [P, TC, D])
        oT = sb("a_oT", [P, KC, T])

        negmask = sb("x_negmask", [P, TC, S2], BF16)
        QT = sb("x_QT", [P, KC, T])
        KT = sb("x_KT", [P, KC, S2])
        KT_bd = sb("x_KT_bd", [P, KC, HB, S2])
        Vx = sb("x_Vx", [S2, NH, HD + 1])
        smax = sb("x_smax", [P, 2, UH])
        ssub = sb("x_ssub", [P, 2, UH, S2])
        prob = sb("x_prob", [P, 2, UH, S2])
        probT = sb("x_probT", [S2, 2, UH, P])
        xrs = sb("x_rs", [P, TC, NH])
        xo = sb("x_o", [P, TC, D])
        xoT = sb("x_oT", [P, KC, T])
        x1b = sb("x_x1b", [P, TC, D])

        logit = sb("f_logit", [P, TC, NE])
        top = sb("f_top", [P, TC, 8])
        topi = sb("f_topi", [P, TC, 8], U32)
        topf = sb("f_topf", [P, TC, 8])
        gap = sb("f_gap", [P, TC])
        egap = sb("f_egap", [P, TC])
        gden = sb("f_gden", [P, TC])
        gw = sb("f_gw", [P, 2, TC])
        wt1 = sb("f_wt1", [P, TC, NE])
        wt2 = sb("f_wt2", [P, TC, NE])
        wt = sb("f_wt", [P, TC, NE])
        fth = sb("f_th", [P, NE * R])
        fsu = sb("f_su", [P, NE * R])
        fs = sb("f_s", [P, 2, NE * R])
        fsw = sb("f_sw", [P, 2, NE * R])
        fsT = sb("f_sT", [P, 2, RC, P])

        bank = [ctx.enter_context(nc.psum_tensor(f"bank{i}", [P, 512], F32)) for i in range(8)]
        A0, A1, A2, X0, X1, X2, F0, F1 = bank

        ld_w = sem("ld_w")
        ld_x = [sem(f"ld_x{i}") for i in range(2)]
        ld_c = [sem(f"ld_c{i}") for i in range(2)]
        st_y = [sem(f"st_y{i}") for i in range(2)]
        w_ready = sem("w_ready")
        z_ready = sem("z_ready")
        on = Signals(*[sem(n) for n in STEPS.split()],
                     *[{s: sem(f"{s}_{n}") for s in "axf"} for n in NORM_STEPS.split()])

        def upto(row, n=1, k=None):
            return row.half * (2 * n) + (n * row.parity + (n if k is None else k))

        def later(row):
            return row.parity == 1 or not (isinstance(row.half, int) and row.half == 0)

        def before(row):
            return Row(row.half, 0) if row.parity == 1 else Row(row.half - 1, 1)

        def loaded(row, n=1):
            return row.half * (16 * n) + 16 * n

        def hold(eng, scrap):
            eng.tensor_tensor(scrap[:], mhalf[:, 0:1], mhalf[:, 0:1], ALU.mult)

        def iterations(eng, body):
            body(Row(0, 0), None, None)
            body(Row(0, 1), Row(0, 0), None)
            body(Row(1, 0), Row(0, 1), Row(0, 0))
            body(Row(1, 1), Row(1, 0), Row(0, 1))
            with eng.Fori(2, B // 2) as half:
                body(Row(half, 0), Row(half - 1, 1), Row(half - 1, 0))
                body(Row(half, 1), Row(half, 0), Row(half - 1, 1))
            last = B // 2
            body(None, Row(last - 1, 1), Row(last - 1, 0))
            body(None, None, Row(last - 1, 1))

        block = ctx.enter_context(nc.Block())

        weights = [
            (ident[:], a["ident"]), (tri[:], a["tri"]), (cosT[:], a["cosT"]), (sinT[:], a["sinT"]),
            (headmask[:], a["headmask"]), (iota8[:], a["iota8"]),
            (wqk[:, :, 0, :], a["Wq"].rearrange("(k p) n -> p k n", p=P)),
            (wqk[:, :, 1, :], a["Wk"].rearrange("(k p) n -> p k n", p=P)),
            (wv[:], a["Wv"].rearrange("(k p) n -> p k n", p=P)),
            (cw[:, 0, :], a["qconv"].rearrange("c o k -> c (o k)")),
            (cw[:, 1, :], a["kconv"].rearrange("c o k -> c (o k)")),
            (cw[:, 2:4, :], a["vconv"].rearrange("(j p) o k -> p j (o k)", p=P)),
            (ws[:], a["Ws"].rearrange("(k p) n -> p k n", p=P)),
            (wg[:], a["Wg"].rearrange("(k p) n -> p k n", p=P)),
            (wo_raw[:], a["Wo"].rearrange("(k p) n -> p k n", p=P)),
            (gnorm[0:VD, :], a["gnorm"].rearrange("(v o) -> v o", o=1)),
            (gnorm[VD:2 * VD, :], a["gnorm"].rearrange("(v o) -> v o", o=1)),
            (xwq[:], a["xWqT"].rearrange("(k p) n -> p k n", p=P)),
            (xwk[:], a["xWkT"].rearrange("(k p) n -> p k n", p=P)),
            (xwv[:], a["xWvT"].rearrange("(k p) n -> p k n", p=P)),
            (xwp[:], a["xWpT"].rearrange("(k p) n -> p k n", p=P)),
            (xbias[:], a["xbias"]),
            (fgate[:], a["gate_w"].rearrange("(k p) n -> p k n", p=P)),
            (fwo[:], a["fWo"].rearrange("e r n -> (e r) n").rearrange("(c p) n -> p c n", p=P)),
        ] + [
            (w[:, k, :].rearrange("p (e r) -> p e r", e=NE), a[n][:, k * P:(k + 1) * P, :].rearrange("e p r -> p e r"))
            for w, n in ((fwu, "fWu"), (fwv, "fWv")) for k in range(KC)
        ]
        W_LANDED = 16 * len(weights)

        def row_of(ap, row):
            return ap[bass.ds(row.half * 2 + row.parity, 1)]

        @block.sync
        def _(sp):
            def load_x(row):
                sp.dma_start(x0[row.parity][:], row_of(a["x"], row).rearrange("o (c p) d -> p (o c) d", p=P)
                             ).then_inc(ld_x[row.parity], 16)

            def load_context(row):
                c, m = ctxT[row.parity], keep[row.parity]
                sp.dma_start(c[:], row_of(a["ctxT"], row).rearrange("o (k p) s -> p (o k) s", p=P)
                             ).then_inc(ld_c[row.parity], 16)
                sp.dma_start(m[:], row_of(a["mask"], row).rearrange("o u (c p) s -> p (o u c) s", p=P)
                             ).then_inc(ld_c[row.parity], 16)

            def body(ra, rx, rf):
                if ra is not None:
                    if not (isinstance(ra.half, int) and ra.half == 0 and ra.parity == 0):
                        if later(ra):
                            sp.wait_ge(on.a_x1, upto(before(ra)))
                        load_x(Row(ra.half, 1) if ra.parity == 0 else Row(ra.half + 1, 0))
                    if rf is not None:
                        sp.wait_ge(on.x_neg, upto(rf))
                        sp.wait_ge(on.x_v_ps, upto(rf))
                    load_context(ra)
                if rf is not None:
                    sp.wait_ge(on.f_y, upto(rf))
                    sp.dma_start(row_of(a["out"], rf).rearrange("o (c p) d -> p (o c) d", p=P),
                                 y[rf.parity][:]).then_inc(st_y[rf.parity], 16)

            load_x(Row(0, 0))
            for dst, src in weights:
                sp.dma_start(dst, src).then_inc(ld_w, 16)
            load_x(Row(0, 1))
            body(Row(0, 0), None, None)
            body(Row(0, 1), Row(0, 0), None)
            body(Row(1, 0), Row(0, 1), Row(0, 0))
            body(Row(1, 1), Row(1, 0), Row(0, 1))
            with sp.Fori(2, B // 2 - 1) as half:
                body(Row(half, 0), Row(half - 1, 1), Row(half - 1, 0))
                body(Row(half, 1), Row(half, 0), Row(half - 1, 1))
            last = B // 2
            body(Row(last - 1, 0), Row(last - 2, 1), Row(last - 2, 0))
            sp.wait_ge(on.x_neg, upto(Row(last - 2, 1)))
            sp.wait_ge(on.x_v_ps, upto(Row(last - 2, 1)))
            load_context(Row(last - 1, 1))
            for rf in (Row(last - 2, 1), Row(last - 1, 0), Row(last - 1, 1)):
                sp.wait_ge(on.f_y, upto(rf))
                sp.dma_start(row_of(a["out"], rf).rearrange("o (c p) d -> p (o c) d", p=P),
                             y[rf.parity][:]).then_inc(st_y[rf.parity], 16)
            for i in range(2):
                sp.wait_ge(st_y[i], 16 * (B // 2))

        @block.tensor
        def _(pe):
            def mm(out, lhsT, rhs, start=True, stop=True):
                return pe.matmul(out, lhsT, rhs, start=start, stop=stop, skip_group_check=True)

            def turn(dst, src):
                for k in range(KC):
                    for c in range(TC):
                        ins = pe.transpose(dst[:, k * T + c * P:k * T + (c + 1) * P],
                                           src[:, c, k * P:(k + 1) * P], ident[:])
                return ins

            def features(dst, w, act, n=1):
                for k in range(KC):
                    ins = mm(dst, w(k), act(k), start=(k == 0), stop=(k == KC - 1))
                return ins

            def a_turn(r):
                if later(r):
                    pe.wait_ge(on.a_osq, upto(before(r)))
                if later(r):
                    pe.wait_ge(on.a_o1, upto(before(r)))
                pe.wait_ge(on.xn["a"], upto(r))
                turn(A0, xn["a"]).then_inc(on.xnT_ps["a"], 1)

            def a_qk(r):
                pe.wait_ge(on.xnT["a"], upto(r))
                if later(r):
                    pe.wait_ge(on.a_oT, upto(before(r)))
                for j in range(2):
                    ins = features(A1[:, j * T:(j + 1) * T], lambda k: wqk[:, k, j, :], lambda k: xnT["a"][:, k, :])
                ins.then_inc(on.a_qk_ps, 1)

            def a_v(r):
                if later(r):
                    pe.wait_ge(on.a_x1, upto(before(r)))
                for j in range(2):
                    ins = features(A2[:, j * T:(j + 1) * T], lambda k: wv[:, k, j * P:(j + 1) * P],
                                   lambda k: xnT["a"][:, k, :])
                ins.then_inc(on.a_v_ps, 1)

            def tokens(dst, act, w):
                for c in range(TC):
                    for k in range(KC):
                        ins = mm(dst[:, c * D:(c + 1) * D], act[:, k, c * P:(c + 1) * P], w[:, k, :],
                                 start=(k == 0), stop=(k == KC - 1))
                return ins

            def a_s(r):
                tokens(A0, xnT["a"], ws).then_inc(on.a_s_ps, 1)

            def a_g(r):
                pe.wait_ge(on.a_qk_raw, upto(r))
                tokens(A1, xnT["a"], wg).then_inc(on.a_g_ps, 1)

            def a_et(r):
                pe.wait_ge(on.a_v_raw, upto(r))
                pe.wait_ge(on.a_E, upto(r))
                turn(A2, E).then_inc(on.a_ET_ps, 1)

            def a_c(r):
                pe.wait_ge(on.a_sc, upto(r))
                mm(A0[:, 0:D], tri[:], E[:, 0, :])
                mm(A0[:, D:2 * D], ones[:], E[:, 0, :], stop=False)
                mm(A0[:, D:2 * D], tri[:], E[:, 1, :], start=False).then_inc(on.a_C_ps, 1)

            def a_tok(r):
                pe.wait_ge(on.a_kr, upto(r))
                pe.wait_ge(on.a_rC, upto(r))
                pe.transpose(A0[:, 0:P], kr[:, 0:P], ident[:]).then_inc(on.a_tok_ps, 1)
                pe.wait_ge(on.a_v, upto(r))
                pe.wait_ge(on.a_gate, upto(r))
                for c in range(TC):
                    for j in range(2):
                        ins = pe.transpose(A1[:, c * D + j * P:c * D + (j + 1) * P],
                                           qkv[:, 2 + j, c * P:(c + 1) * P], ident[:])
                ins.then_inc(on.a_tok_ps, 1)

            def a_A(r, c):
                if c == 0:
                    pe.wait_ge(on.a_qbd, upto(r))
                    pe.wait_ge(on.a_ET, upto(r))
                else:
                    pe.wait_ge(on.a_ktok, upto(r))
                mm((A2 if c == 0 else A0)[:, :], kr[:, c * P:(c + 1) * P], q_bd[:, :, c * P:(c + 1) * P]
                   ).then_inc(on.a_A_ps, 1)

            def a_state(r):
                pe.wait_ge(on.a_ktok, upto(r))
                pe.wait_ge(on.a_vtok, upto(r))
                mm(A1[:, 0:D], ktok[:], E[:, 0, :])
                for f in range(2):
                    ins = mm(A1[:, D + f * P:D + (f + 1) * P], E[:, 0, f * P:(f + 1) * P],
                             vtok[:, 0, f * P:(f + 1) * P])
                ins.then_inc(on.a_state_ps, 1)

            def a_ok(r):
                pe.wait_ge(on.a_A, upto(r, TC))
                pe.wait_ge(on.a_state, upto(r))
                for h in range(H):
                    mm(A2[:, h * M:(h + 1) * M], AT[:, 0, h, :], E[:, 0, h * M:(h + 1) * M])
                for h in range(H):
                    out = A2[:, D + h * M:D + (h + 1) * M]
                    mm(out, q_bd[:, h, P:2 * P], state[:, h * M:(h + 1) * M], stop=False)
                    ins = mm(out, AT[:, 1, h, :], E[:, 1, h * M:(h + 1) * M], start=False)
                ins.then_inc(on.a_ok_ps, 1)

            def a_qt(r):
                pe.wait_ge(on.a_qn, upto(r))
                turn(A0, qn).then_inc(on.a_qnT_ps, 1)

            def a_P(r, c):
                if c == 0:
                    pe.wait_ge(on.a_qnT, upto(r, 2))
                else:
                    pe.wait_ge(on.a_okn, upto(r))
                dst = A1 if c == 0 else A2
                for f in range(2):
                    ins = mm(dst[:, f * 2 * P:(f + 1) * 2 * P], ET[:, f, c * P:(c + 1) * P],
                             qn_bd[:, f, :, c * P:(c + 1) * P])
                ins.then_inc(on.a_P_ps, 1)

            def a_o(r):
                pe.wait_ge(on.a_P, upto(r, TC))
                for h in range(H):
                    mm(A0[:, h * VD:(h + 1) * VD], PT[:, 0, h, :], vtok[:, 0, h * VD:(h + 1) * VD])
                for h in range(H):
                    f, hh = h // 2, h % 2
                    out = A0[:, D + h * VD:D + (h + 1) * VD]
                    mm(out, qn_bd[:, f, hh, P:2 * P], state[:, D + f * P + hh * VD:D + f * P + (hh + 1) * VD],
                       stop=False)
                    ins = mm(out, PT[:, 1, h, :], vtok[:, 1, h * VD:(h + 1) * VD], start=False)
                ins.then_inc(on.a_o_ps, 1)

            def a_ot(r):
                pe.wait_ge(on.a_o2, upto(r))
                turn(A1, o2).then_inc(on.a_oT_ps, 1)

            def a_wo(r):
                pe.wait_ge(on.a_oT, upto(r))
                tokens(A2, oT, wo).then_inc(on.a_wo_ps, 1)

            def x_turn(r):
                if later(r):
                    pe.wait_ge(on.x_x2, upto(before(r)))
                pe.wait_ge(on.xn["x"], upto(r))
                turn(X0, xn["x"]).then_inc(on.xnT_ps["x"], 1)

            def x_kv(r):
                pe.wait_ge(ld_c[r.parity], loaded(r, 2))
                if later(r):
                    pe.wait_ge(on.x_oT, upto(before(r)))
                c = ctxT[r.parity]
                for j in range(2):
                    ins = features(X1[:, j * S2:(j + 1) * S2], lambda k: xwk[:, k, j * P:(j + 1) * P],
                                   lambda k: c[:, k, :])
                ins.then_inc(on.x_k_ps, 1)
                if later(r):
                    pe.wait_ge(on.x_o, upto(before(r), TC))
                for k in range(KC):
                    ins = mm(X2[0:S2, 0:D], c[:, k, :], xwv[:, k, :], start=(k == 0), stop=(k == KC - 1))
                ins.then_inc(on.x_v_ps, 1)

            def x_q(r):
                pe.wait_ge(on.xnT["x"], upto(r))
                for j in range(2):
                    ins = features(X0[:, j * T:(j + 1) * T], lambda k: xwq[:, k, j * P:(j + 1) * P],
                                   lambda k: xnT["x"][:, k, :])
                ins.then_inc(on.x_q_ps, 1)

            def x_s(r, u):
                c, q = divmod(u, QU)
                f, hh = divmod(q * UH, HB)
                if u == 0:
                    pe.wait_ge(on.x_q, upto(r))
                    pe.wait_ge(on.x_kbd, upto(r))
                    pe.wait_ge(on.x_neg, upto(r))
                else:
                    pe.wait_ge(on.x_sub, upto(r, NU, u))
                out = X0[:, 0:UH * S2]
                mm(out, QT[:, f, c * P:(c + 1) * P], KT_bd[:, f, hh:hh + UH, :], stop=False)
                mm(out, ident_bf[:], negmask[:, c:c + 1, :].broadcast_to([P, UH, S2]), start=False
                   ).then_inc(on.x_s_ps, 1)

            def x_pt(r, u):
                pe.wait_ge(on.x_prob, upto(r, NU, u + 1))
                if u == 0:
                    pe.wait_ge(on.x_k, upto(r))
                else:
                    pe.wait_ge(on.x_pT, upto(r, NU, u))
                for i in range(UH):
                    ins = pe.transpose(X1[0:S2, i * P:(i + 1) * P], prob[:, u % 2, i, :], ident[:])
                ins.then_inc(on.x_pT_ps, 1)

            def x_av(r, u):
                c, q = divmod(u, QU)
                if u == 0:
                    pe.wait_ge(on.x_v, upto(r))
                elif q == 0:
                    pe.wait_ge(on.x_o, upto(r, TC, c))
                pe.wait_ge(on.x_pT, upto(r, NU, u + 1))
                for i in range(UH):
                    h = q * UH + i
                    ins = mm(X2[:, h * (HD + 1):(h + 1) * (HD + 1)], probT[:, u % 2, i, :], Vx[:, h, :])
                ins.then_inc(on.x_av_ps, 1)

            def x_ot(r):
                pe.wait_ge(on.x_o, upto(r, TC))
                turn(X1, xo).then_inc(on.x_oT_ps, 1)

            def x_proj(r):
                pe.wait_ge(on.x_oT, upto(r))
                tokens(X0, xoT, xwp).then_inc(on.x_proj_ps, 1)

            def f_turn(r):
                if later(r):
                    pe.wait_ge(on.f_y, upto(before(r)))
                pe.wait_ge(on.xn["f"], upto(r))
                turn(F0, xn["f"]).then_inc(on.xnT_ps["f"], 1)

            def f_gate(r):
                pe.wait_ge(on.xnT["f"], upto(r))
                if later(r):
                    pe.wait_ge(on.f_sT, upto(before(r), TC))
                for c in range(TC):
                    for k in range(KC):
                        ins = mm(F1[:, c * NE:(c + 1) * NE], xnT["f"][:, k, c * P:(c + 1) * P], fgate[:, k, :],
                                 start=(k == 0), stop=(k == KC - 1))
                ins.then_inc(on.f_gate_ps, 1)

            def f_up(c, dst, w):
                for k in range(KC):
                    ins = mm(dst[:, :], xnT["f"][:, k, c * P:(c + 1) * P], w[:, k, :],
                             start=(k == 0), stop=(k == KC - 1))
                return ins

            def f_u0(r):
                f_up(0, F0, fwu).then_inc(on.f_u_ps, 1)

            def f_v0(r):
                pe.wait_ge(on.f_logit, upto(r))
                f_up(0, F1, fwv).then_inc(on.f_v_ps, 1)

            def f_u1(r):
                pe.wait_ge(on.f_s, upto(r, TC, 1))
                f_up(1, F1, fwu).then_inc(on.f_u_ps, 1)

            def f_v1(r):
                pe.wait_ge(on.f_sT, upto(r, TC, 1))
                f_up(1, F0, fwv).then_inc(on.f_v_ps, 1)

            def f_st(r, c):
                pe.wait_ge(on.f_sw, upto(r, TC, c + 1))
                pe.wait_ge(on.f_su, upto(r, TC, c + 1))
                dst = F0 if c == 0 else F1
                for i in range(RC):
                    ins = pe.transpose(dst[:, i * P:(i + 1) * P], fsw[:, c, i * P:(i + 1) * P], ident[:])
                ins.then_inc(on.f_sT_ps, 1)

            def f_yy(r):
                pe.wait_ge(on.f_sT, upto(r, TC))
                pe.wait_ge(on.f_s, upto(r, TC))
                for c in range(TC):
                    for i in range(RC):
                        ins = mm(F0[:, c * D:(c + 1) * D], fsT[:, c, i, :], fwo[:, i, :],
                                 start=(i == 0), stop=(i == RC - 1))
                ins.then_inc(on.f_y_ps, 1)

            def body(ra, rx, rf):
                def A(f, *k):
                    if ra is not None:
                        f(ra, *k)

                def X(f, *k):
                    if rx is not None:
                        f(rx, *k)

                def F(f, *k):
                    if rf is not None:
                        f(rf, *k)

                A(a_turn); A(a_qk); A(a_v); A(a_s)
                X(x_kv); X(x_turn); A(a_g); X(x_q)
                F(f_turn); F(f_gate); A(a_et); A(a_c); X(x_s, 0); F(f_u0); F(f_v0)
                X(x_pt, 0); X(x_s, 1); A(a_tok)
                X(x_av, 0); X(x_pt, 1); X(x_s, 2); A(a_A, 0); A(a_A, 1)
                F(f_st, 0); A(a_state); X(x_av, 1); X(x_pt, 2); X(x_s, 3)
                F(f_u1); A(a_ok); X(x_av, 2); X(x_pt, 3); X(x_s, 4)
                F(f_v1); X(x_av, 3); X(x_pt, 4); X(x_s, 5)
                A(a_qt); X(x_pt, 5); X(x_s, 6); X(x_av, 4)
                F(f_st, 1); A(a_P, 0); X(x_pt, 6); X(x_s, 7); A(a_P, 1); X(x_av, 5)
                F(f_yy); X(x_pt, 7); A(a_o); X(x_av, 6); X(x_av, 7)
                A(a_ot); X(x_ot); A(a_wo); X(x_proj)

            pe.wait_ge(ld_w, W_LANDED)
            pe.wait_ge(w_ready, 4)
            pe.wait_ge(z_ready, 3)
            iterations(pe, body)

        @block.vector
        def _(dve):
            tt, ts, stt = dve.tensor_tensor, dve.tensor_scalar, dve.scalar_tensor_tensor

            def norm_stats(s, src, r):
                for c in range(TC):
                    dve.bn_stats(ln_stats[s][:, c, :], src[:, c, :]).then_inc(on.stats[s], 1)
                dve.wait_ge(on.stats[s], upto(r, TC))
                hold(dve, dve_scrap)
                for c in range(TC):
                    dve.bn_aggr(ln_mv[s][:, c, :], ln_stats[s][:, c, :]).then_inc(on.mv[s], 1)
                dve.wait_ge(on.mv[s], upto(r, TC))
                ts(ln_ve[s][:], ln_mv[s][:, :, 1], EPS, None, ALU.add).then_inc(on.ve[s], 1)

            def norm_apply(s, src, r):
                dve.wait_ge(on.rstd[s], upto(r))
                if later(r):
                    dve.wait_ge(on.xnT_ps[s], upto(before(r)))
                for c in range(TC):
                    ins = ts(xn[s][:, c, :], src[:, c, :], ln_mv[s][:, c, 0:1], ln_rstd[s][:, c:c + 1],
                             ALU.subtract, ALU.mult)
                ins.then_inc(on.xn[s], 1)

            def heads(ap):
                return ap.rearrange("p (g m) -> p g m", m=M)

            def flat(t):
                return t[:].rearrange("p c d -> p (c d)")

            def spread(small, n):
                return small.rearrange("p (g o) -> p g o", o=1).broadcast_to([P, small.shape[1], n])

            def a_norm1(r):
                dve.wait_ge(ld_x[r.parity], loaded(r))
                norm_stats("a", x0[r.parity], r)

            def a_norm2(r):
                norm_apply("a", x0[r.parity], r)

            def a_clip(r):
                dve.wait_ge(on.a_s_ps, upto(r))
                ts(flat(sc), A0[:, :], -CLIP, CLIP, ALU.max, ALU.min).then_inc(on.a_sc, 1)

            def a_gate(r):
                dve.wait_ge(on.a_gt, upto(r))
                if later(r):
                    dve.wait_ge(on.a_o2, upto(before(r)))
                stt(flat(gate), flat(gt), 1.0, A1[:, :], ALU.add, ALU.mult).then_inc(on.a_gate, 1)

            def a_conv(r):
                dve.wait_ge(on.a_tap0, upto(r))
                n = 0
                for i in range(1, TAPS):
                    for j in range(4):
                        n += 1
                        if i > 1:
                            dve.wait_ge(on.a_conv, upto(r, 3 * 4, n - 4))
                        stt(conv[:, j, :], raw[:, j, i:i + T], cw[:, j, i:i + 1], conv[:, j, :],
                                 ALU.mult, ALU.add).then_inc(on.a_conv, 1)

            def a_silu(r):
                dve.wait_ge(on.a_convt, upto(r, 2, 1))
                stt(qkv[:, 0:2, :], convt[:, 0:2, :], 1.0, conv[:, 0:2, :], ALU.add, ALU.mult).then_inc(on.a_qk, 1)
                dve.wait_ge(on.a_qk, upto(r))
                hold(dve, dve_scrap)
                dve.stream_shuffle(rot[:, :, :], qkv[:, 0:2, :],
                                        [(i + KD // 2) % KD for i in range(KD)]).then_inc(on.a_rot, 1)
                dve.wait_ge(on.a_convt, upto(r, 2, 2))
                stt(qkv[:, 2:4, :], convt[:, 2:4, :], 1.0, conv[:, 2:4, :], ALU.add, ALU.mult).then_inc(on.a_v, 1)

            def a_rope(r):
                dve.wait_ge(on.a_rot, upto(r))
                tt(qksin[:], rot[:], sinT[:].rearrange("p (o t) -> p o t", o=1).broadcast_to([P, 2, T]),
                        ALU.mult).then_inc(on.a_sin, 1)
                dve.wait_ge(on.a_sin, upto(r))
                dve.wait_ge(on.a_cos, upto(r))
                tt(kr[:], qkcos[:, 1, :], qksin[:, 1, :], ALU.add).then_inc(on.a_kr, 1)
                for h in range(H):
                    s = slice(h * KD, (h + 1) * KD)
                    ins = tt(q_bd[s, h, :], qkcos[s, 0, :], qksin[s, 0, :], ALU.add)
                ins.then_inc(on.a_qbd, 1)

            def a_rc(r):
                dve.wait_ge(on.a_C_ps, upto(r))
                dve.reciprocal(flat(rC), A0[:, :]).then_inc(on.a_rC, 1)

            def causal(dst, src):
                return tt(dst, src.rearrange("p (h t) -> p h t", h=H),
                          tri[:].rearrange("p (o t) -> p o t", o=1).broadcast_to([P, H, P]), ALU.mult)

            def a_maskA(r, c):
                dve.wait_ge(on.a_A_ps, upto(r, TC, c + 1))
                causal(AT[:, c], (A2 if c == 0 else A0)[:, :]).then_inc(on.a_A, 1)

            def a_okn(r):
                dve.wait_ge(on.a_ok_ps, upto(r))
                tt(flat(okn), A2[:, :], flat(rC), ALU.mult).then_inc(on.a_okn, 1)
                dve.wait_ge(on.a_okn, upto(r))
                dve.tensor_reduce(okmax[:], heads(flat(okn)), AX.X, ALU.max).then_inc(on.a_max, 1)

            def a_sum(r):
                dve.wait_ge(on.a_oke, upto(r))
                dve.tensor_reduce(ssum[:], heads(flat(oke)), AX.X, ALU.add).then_inc(on.a_sum, 1)
                dve.wait_ge(on.a_sum, upto(r))
                tt(ssq[:], ssum[:], ssum[:], ALU.mult).then_inc(on.a_ssq, 1)

            def a_maskP(r, c):
                dve.wait_ge(on.a_P_ps, upto(r, TC, c + 1))
                causal(PT[:, c], (A1 if c == 0 else A2)[:, :]).then_inc(on.a_P, 1)

            def a_oss(r):
                dve.wait_ge(on.a_osq, upto(r))
                dve.tensor_reduce(oss[:], heads(flat(osq)), AX.X, ALU.add).then_inc(on.a_oss, 1)
                dve.wait_ge(on.a_oss, upto(r))
                dve.wait_ge(on.a_ssq, upto(r))
                stt(ove[:], ssq[:], 4 * EPS * VD, oss[:], ALU.mult, ALU.add).then_inc(on.a_ove, 1)

            def a_o1(r):
                dve.wait_ge(on.a_orinv, upto(r))
                dve.wait_ge(on.a_o_ps, upto(r))
                tt(heads(flat(o1)), heads(A0[:, :]), spread(orinv[:], VD), ALU.mult).then_inc(on.a_o1, 1)

            def a_out(r):
                dve.wait_ge(on.a_wo_ps, upto(r))
                if not (isinstance(r.half, int) and r.half == 0):
                    dve.wait_ge(on.x_x1b, upto(Row(r.half - 1, r.parity)))
                    dve.wait_ge(on.xn["x"], upto(Row(r.half - 1, r.parity)))
                tt(flat(x1[r.parity]), A2[:, :], flat(x0[r.parity]), ALU.add).then_inc(on.a_x1, 1)

            def x_norm1(r):
                dve.wait_ge(on.a_x1, upto(r))
                norm_stats("x", x1[r.parity], r)

            def x_norm2(r):
                norm_apply("x", x1[r.parity], r)

            def x_neg(r):
                dve.wait_ge(ld_c[r.parity], loaded(r, 2))
                if later(r):
                    dve.wait_ge(on.x_s_ps, upto(before(r), NU))
                ts(flat(negmask), keep[r.parity][:].rearrange("p c s -> p (c s)"), 0.0, MASKED,
                        ALU.is_equal, ALU.mult).then_inc(on.x_neg, 1)

            def x_soft(r, u):
                dve.wait_ge(on.x_s_ps, upto(r, NU, u + 1))
                src = X0[:, 0:UH * S2].rearrange("p (h s) -> p h s", h=UH)
                dve.tensor_reduce(smax[:, u % 2, :], src, AX.X, ALU.max).then_inc(on.x_max, 1)
                dve.wait_ge(on.x_max, upto(r, NU, u + 1))
                if u >= 2:
                    dve.wait_ge(on.x_prob, upto(r, NU, u - 1))
                else:
                    if later(r):
                        dve.wait_ge(on.x_prob, upto(before(r), NU, NU - 1 + u))
                tt(ssub[:, u % 2], src, spread(smax[:, u % 2, :], S2), ALU.subtract).then_inc(on.x_sub, 1)

            def x_pt(r, u):
                dve.wait_ge(on.x_pT_ps, upto(r, NU, u + 1))
                if u >= 2:
                    dve.wait_ge(on.x_av_ps, upto(r, NU, u - 1))
                else:
                    if later(r):
                        dve.wait_ge(on.x_av_ps, upto(before(r), NU, NU - 1 + u))
                dve.tensor_copy(probT[:, u % 2].rearrange("p h t -> p (h t)"), X1[0:S2, :]).then_inc(on.x_pT, 1)

            def x_o(r, c):
                dve.wait_ge(on.x_av_ps, upto(r, NU, (c + 1) * QU))
                src = X2[:, 0:NH * (HD + 1)].rearrange("p (h e) -> p h e", h=NH)
                dve.reciprocal(xrs[:, c, :], src[:, :, HD]).then_inc(on.x_rs, 1)
                dve.wait_ge(on.x_rs, upto(r, TC, c + 1))
                if c == 0:
                    if later(r):
                        dve.wait_ge(on.x_oT_ps, upto(before(r)))
                tt(xo[:, c, :].rearrange("p (h e) -> p h e", h=NH), src[:, :, 0:HD],
                        spread(xrs[:, c, :], HD), ALU.mult).then_inc(on.x_o, 1)

            def x_out(r):
                dve.wait_ge(on.x_proj_ps, upto(r))
                dve.wait_ge(on.x_x1b, upto(r))
                if not (isinstance(r.half, int) and r.half == 0):
                    dve.wait_ge(on.f_y, upto(Row(r.half - 1, r.parity)))
                tt(flat(x2[r.parity]), X0[:, :], flat(x1b), ALU.add).then_inc(on.x_x2, 1)

            def f_norm1(r):
                dve.wait_ge(on.x_x2, upto(r))
                norm_stats("f", x2[r.parity], r)

            def f_norm2(r):
                norm_apply("f", x2[r.parity], r)

            def f_top(r):
                dve.wait_ge(on.f_gate_ps, upto(r))
                dve.tensor_copy(flat(logit), F1[:, 0:TC * NE]).then_inc(on.f_logit, 1)
                dve.wait_ge(on.f_logit, upto(r))
                hold(dve, dve_scrap)
                for c in range(TC):
                    dve.max(top[:, c, :], logit[:, c, :]).then_inc(on.f_top, 1)
                dve.wait_ge(on.f_top, upto(r, TC))
                hold(dve, dve_scrap)
                for c in range(TC):
                    dve.max_index(topi[:, c, :], top[:, c, :], logit[:, c, :]).then_inc(on.f_topi, 1)
                tt(gap[:], top[:, :, 1], top[:, :, 0], ALU.subtract).then_inc(on.f_gap, 1)
                dve.wait_ge(on.f_topi, upto(r, TC))
                dve.tensor_copy(flat(topf), topi[:].rearrange("p c n -> p (c n)")).then_inc(on.f_topf, 1)

            def f_weights(r):
                dve.wait_ge(on.f_egap, upto(r))
                ts(gden[:], egap[:], 1.0, 2.0, ALU.add, ALU.mult).then_inc(on.f_gden, 1)
                dve.wait_ge(on.f_gden, upto(r))
                dve.reciprocal(gw[:, 0, :], gden[:]).then_inc(on.f_gw1, 1)
                dve.wait_ge(on.f_gw1, upto(r))
                tt(gw[:, 1, :], gw[:, 0, :], egap[:], ALU.mult).then_inc(on.f_gw2, 1)
                dve.wait_ge(on.f_topf, upto(r))
                dve.wait_ge(on.f_gw2, upto(r))
                for c in range(TC):
                    ts(wt1[:, c, :], iota8[:], topf[:, c, 0:1], gw[:, 0, c:c + 1], ALU.is_equal, ALU.mult)
                    ins = ts(wt2[:, c, :], iota8[:], topf[:, c, 1:2], gw[:, 1, c:c + 1], ALU.is_equal, ALU.mult)
                ins.then_inc(on.f_wt12, 1)
                dve.wait_ge(on.f_wt12, upto(r))
                if later(r):
                    dve.wait_ge(on.f_sw, upto(before(r), TC))
                tt(flat(wt), flat(wt1), flat(wt2), ALU.add).then_inc(on.f_wt, 1)

            def f_s(r, c):
                dve.wait_ge(on.f_th, upto(r, TC, c + 1))
                stt(fsu[:], fth[:], 1.0, (F0 if c == 0 else F1)[:, :], ALU.add, ALU.mult).then_inc(on.f_su, 1)
                dve.wait_ge(on.f_su, upto(r, TC, c + 1))
                dve.wait_ge(on.f_v_ps, upto(r, TC, c + 1))
                if later(r):
                    dve.wait_ge(on.f_sw, upto(before(r), TC, c + 1))
                tt(fs[:, c, :], (F1 if c == 0 else F0)[:, :], fsu[:], ALU.mult).then_inc(on.f_s, 1)

            def f_out(r):
                dve.wait_ge(on.f_y_ps, upto(r))
                if not (isinstance(r.half, int) and r.half == 0):
                    dve.wait_ge(st_y[r.parity], r.half * 16)
                tt(flat(y[r.parity]), F0[:, :], flat(x2[r.parity]), ALU.add).then_inc(on.f_y, 1)

            def body(ra, rx, rf):
                def A(f, *k):
                    if ra is not None:
                        f(ra, *k)

                def X(f, *k):
                    if rx is not None:
                        f(rx, *k)

                def F(f, *k):
                    if rf is not None:
                        f(rf, *k)

                A(a_norm1); X(x_norm1); F(f_norm1); A(a_norm2); X(x_neg); X(x_norm2); F(f_norm2)
                A(a_clip); A(a_gate); A(a_conv); F(f_top); X(x_soft, 0)
                A(a_silu); A(a_rc); A(a_rope); F(f_weights); F(f_s, 0)
                X(x_soft, 1); A(a_maskA, 0); A(a_maskA, 1)
                X(x_pt, 1); X(x_soft, 2)
                X(x_soft, 3)
                A(a_okn); X(x_pt, 3); X(x_o, 0); X(x_soft, 4); F(f_s, 1); X(x_soft, 5)
                A(a_sum); X(x_pt, 5); X(x_soft, 6); A(a_maskP, 0); A(a_maskP, 1)
                X(x_soft, 7); X(x_pt, 7); A(a_oss); A(a_o1); X(x_o, 1); F(f_out)
                A(a_out); X(x_out)

            dve.memset(mhalf[:], -0.5).then_inc(w_ready, 1)
            dve.memset(ones[:], 1.0).then_inc(w_ready, 1)
            dve.wait_ge(ld_w, W_LANDED)
            dve.tensor_copy(ident_bf[:], ident[:]).then_inc(w_ready, 1)
            ts(flat(wo), flat(wo_raw), gnorm[:, 0:1], 0.5 * VD ** 0.5, ALU.mult, ALU.mult).then_inc(w_ready, 1)
            dve.wait_ge(z_ready, 3)
            dve.wait_ge(w_ready, 4)
            iterations(dve, body)

        @block.scalar
        def _(act):
            def flat(t):
                return t[:].rearrange("p c d -> p (c d)")

            def a_xnt(r):
                if later(r):
                    act.wait_ge(on.a_g_ps, upto(before(r)))
                act.wait_ge(on.xnT_ps["a"], upto(r))
                act.activation(flat(xnT["a"]), A0[:, :], ACT.Copy).then_inc(on.xnT["a"], 1)

            def a_raw(r):
                if later(r):
                    act.wait_ge(on.a_conv, upto(before(r), 3 * 4))
                act.wait_ge(on.a_qk_ps, upto(r))
                act.activation(raw[:, 0:2, TAPS - 1:], A1[:, :].rearrange("p (j t) -> p j t", j=2), ACT.Copy).then_inc(on.a_qk_raw, 1)
                act.wait_ge(on.a_v_ps, upto(r))
                act.activation(raw[:, 2:4, TAPS - 1:], A2[:, :].rearrange("p (j t) -> p j t", j=2), ACT.Copy).then_inc(on.a_v_raw, 1)

            def a_e(r):
                act.wait_ge(on.a_sc, upto(r))
                if later(r):
                    act.wait_ge(on.a_ok_ps, upto(before(r)))
                act.activation(flat(E), flat(sc), ACT.Exp).then_inc(on.a_E, 1)

            def a_gt(r):
                act.wait_ge(on.a_g_ps, upto(r))
                act.activation(flat(gt), A1[:, :], ACT.Tanh, scale=0.5).then_inc(on.a_gt, 1)

            def a_convt(r):
                for j in range(2):
                    act.wait_ge(on.a_conv, upto(r, 3 * 4, 3 * 4 - 2 + 2 * j))
                    act.activation(convt[:, 2 * j:2 * j + 2, :], conv[:, 2 * j:2 * j + 2, :], ACT.Tanh,
                                        scale=0.5).then_inc(on.a_convt, 1)

            def a_et(r):
                if later(r):
                    act.wait_ge(on.a_P_ps, upto(before(r), TC))
                act.wait_ge(on.a_ET_ps, upto(r))
                act.activation(flat(ET), A2[:, :], ACT.Copy).then_inc(on.a_ET, 1)

            def a_tok(r):
                if later(r):
                    act.wait_ge(on.a_o_ps, upto(before(r)))
                act.wait_ge(on.a_tok_ps, upto(r, 2, 1))
                act.activation(ktok[:], A0[:, 0:P], ACT.Copy).then_inc(on.a_ktok, 1)
                act.wait_ge(on.a_tok_ps, upto(r, 2, 2))
                act.activation(flat(vtok), A1[:, :], ACT.Copy).then_inc(on.a_vtok, 1)

            def a_state(r):
                act.wait_ge(on.a_state_ps, upto(r))
                act.activation(state[:], A1[:, :], ACT.Copy).then_inc(on.a_state, 1)

            def a_oke(r):
                act.wait_ge(on.a_oks, upto(r))
                act.activation(flat(oke), flat(oks), ACT.Exp, scale=KD ** -0.5 / 4).then_inc(on.a_oke, 1)

            def a_qnt(r):
                act.wait_ge(on.a_qnT_ps, upto(r))
                src = A0[:, :].rearrange("p (f t) -> p f t", f=2)
                for hh in range(2):
                    s = slice(hh * M, (hh + 1) * M)
                    act.activation(qn_bd[s, :, hh, :], src[s], ACT.Copy).then_inc(on.a_qnT, 1)

            def a_osq(r):
                act.wait_ge(on.a_o_ps, upto(r))
                act.activation(flat(osq), A0[:, :], ACT.Square).then_inc(on.a_osq, 1)

            def a_ot(r):
                act.wait_ge(on.a_oT_ps, upto(r))
                act.activation(flat(oT), A1[:, :], ACT.Copy).then_inc(on.a_oT, 1)

            def x_kv(r):
                if later(r):
                    act.wait_ge(on.x_kbd, upto(before(r)))
                act.wait_ge(on.x_k_ps, upto(r))
                act.activation(flat(KT), X1[:, 0:KC * S2], ACT.Copy).then_inc(on.x_k, 1)
                if later(r):
                    act.wait_ge(on.x_av_ps, upto(before(r), NU))
                act.wait_ge(on.x_v_ps, upto(r))
                act.activation(Vx[:, :, 0:HD], X2[0:S2, 0:D].rearrange("p (h e) -> p h e", h=NH), ACT.Copy).then_inc(on.x_v, 1)

            def x_xnt(r):
                act.wait_ge(on.xnT_ps["x"], upto(r))
                act.activation(flat(xnT["x"]), X0[:, :], ACT.Copy).then_inc(on.xnT["x"], 1)

            def x_q(r):
                if later(r):
                    act.wait_ge(on.x_s_ps, upto(before(r), NU))
                act.wait_ge(on.x_q_ps, upto(r))
                act.activation(flat(QT), X0[:, :], ACT.Copy, scale=HD ** -0.5).then_inc(on.x_q, 1)

            def x_prob(r, u):
                act.wait_ge(on.x_sub, upto(r, NU, u + 1))
                if u >= 2:
                    act.wait_ge(on.x_pT_ps, upto(r, NU, u - 1))
                else:
                    if later(r):
                        act.wait_ge(on.x_pT_ps, upto(before(r), NU, NU - 1 + u))
                act.activation(prob[:, u % 2], ssub[:, u % 2], ACT.Exp).then_inc(on.x_prob, 1)

            def x_pt(r, u):
                act.wait_ge(on.x_pT_ps, upto(r, NU, u + 1))
                if u >= 2:
                    act.wait_ge(on.x_av_ps, upto(r, NU, u - 1))
                else:
                    if later(r):
                        act.wait_ge(on.x_av_ps, upto(before(r), NU, NU - 1 + u))
                act.activation(probT[:, u % 2].rearrange("p h t -> p (h t)"), X1[0:S2, :], ACT.Copy).then_inc(on.x_pT, 1)

            def x_ot(r):
                act.wait_ge(on.x_oT_ps, upto(r))
                act.activation(flat(xoT), X1[:, :], ACT.Copy).then_inc(on.x_oT, 1)

            def f_xnt(r):
                act.wait_ge(on.xnT_ps["f"], upto(r))
                act.activation(flat(xnT["f"]), F0[:, :], ACT.Copy).then_inc(on.xnT["f"], 1)

            def f_gap(r):
                act.wait_ge(on.f_gap, upto(r))
                act.activation(egap[:], gap[:], ACT.Exp).then_inc(on.f_egap, 1)

            def f_th(r, c):
                act.wait_ge(on.f_u_ps, upto(r, TC, c + 1))
                if c == 1:
                    act.wait_ge(on.f_su, upto(r, TC, 1))
                act.activation(fth[:], (F0 if c == 0 else F1)[:, :], ACT.Tanh, scale=0.5).then_inc(on.f_th, 1)

            def f_st(r, c):
                act.wait_ge(on.f_sT_ps, upto(r, TC, c + 1))
                act.activation(fsT[:, c].rearrange("p i t -> p (i t)"), (F0 if c == 0 else F1)[:, :],
                                    ACT.Copy).then_inc(on.f_sT, 1)

            def body(ra, rx, rf):
                def A(f, *k):
                    if ra is not None:
                        f(ra, *k)

                def X(f, *k):
                    if rx is not None:
                        f(rx, *k)

                def F(f, *k):
                    if rf is not None:
                        f(rf, *k)

                A(a_xnt); A(a_raw); X(x_kv); X(x_xnt); A(a_gt); A(a_e); X(x_q); F(f_xnt); F(f_gap)
                A(a_et); A(a_convt); X(x_prob, 0); F(f_th, 0); X(x_pt, 0); X(x_prob, 1)
                A(a_tok); X(x_prob, 2); A(a_state); F(f_st, 0)
                X(x_pt, 2); X(x_prob, 3); F(f_th, 1)
                X(x_prob, 4); A(a_oke); X(x_pt, 4); X(x_prob, 5)
                A(a_qnt); X(x_prob, 6); F(f_st, 1); X(x_pt, 6); X(x_prob, 7)
                A(a_osq); A(a_ot); X(x_ot)

            iterations(act, body)

        @block.gpsimd
        def _(pool):
            def heads(t):
                return t[:].rearrange("p c (h m) -> p (c h) m", m=M)

            def spread(small, n):
                return small.rearrange("p (g o) -> p g o", o=1).broadcast_to([P, small.shape[1], n])

            def rstd(s, r):
                pool.wait_ge(on.ve[s], upto(r))
                if later(r):
                    pool.wait_ge(on.xn[s], upto(before(r)))
                pool.tensor_tensor(ln_rstd[s][:], ln_ve[s][:], mhalf[:, 0:TC], ALU.pow).then_inc(on.rstd[s], 1)

            def a_tap0(r):
                pool.wait_ge(on.a_v_raw, upto(r))
                pool.wait_ge(on.a_qk_raw, upto(r))
                if later(r):
                    pool.wait_ge(on.a_v, upto(before(r)))
                hold(pool, pool_scrap)
                for j in range(4):
                    ins = pool.tensor_scalar(conv[:, j, :], raw[:, j, 0:T], cw[:, j, 0:1], 1.0, ALU.mult, ALU.mult)
                ins.then_inc(on.a_tap0, 1)

            def a_cos(r):
                pool.wait_ge(on.a_qk, upto(r))
                pool.tensor_tensor(qkcos[:], qkv[:, 0:2, :],
                                        cosT[:].rearrange("p (o t) -> p o t", o=1).broadcast_to([P, 2, T]),
                                        ALU.mult).then_inc(on.a_cos, 1)

            def a_oks(r):
                pool.wait_ge(on.a_max, upto(r))
                pool.tensor_tensor(heads(oks), heads(okn), spread(okmax[:], M), ALU.subtract).then_inc(on.a_oks, 1)

            def a_qn(r):
                pool.wait_ge(on.a_oke, upto(r))
                pool.tensor_tensor(qn[:], oke[:], rC[:], ALU.mult).then_inc(on.a_qn, 1)

            def a_orinv(r):
                pool.wait_ge(on.a_ove, upto(r))
                pool.tensor_tensor(orinv[:], ove[:], mhalf[:], ALU.pow).then_inc(on.a_orinv, 1)

            def a_o2(r):
                pool.wait_ge(on.a_o1, upto(r))
                pool.wait_ge(on.a_gate, upto(r))
                pool.tensor_tensor(o2[:], o1[:], gate[:], ALU.mult).then_inc(on.a_o2, 1)

            def x_kbd(r):
                pool.wait_ge(on.x_k, upto(r))
                if later(r):
                    pool.wait_ge(on.x_s_ps, upto(before(r), NU))
                for f in range(KC):
                    ins = pool.tensor_tensor(KT_bd[:, f], KT[:, f:f + 1, :].broadcast_to([P, HB, S2]),
                                             spread(headmask[:], S2), ALU.mult)
                ins.then_inc(on.x_kbd, 1)

            def x_x1b(r):
                pool.wait_ge(on.a_x1, upto(r))
                if later(r):
                    pool.wait_ge(on.x_x2, upto(before(r)))
                pool.tensor_tensor(x1b[:], x1[r.parity][:],
                                        xbias[:].rearrange("p (o d) -> p o d", o=1).broadcast_to([P, TC, D]),
                                        ALU.add).then_inc(on.x_x1b, 1)

            def f_sw(r, c):
                pool.wait_ge(on.f_s, upto(r, TC, c + 1))
                pool.wait_ge(on.f_wt, upto(r))
                pool.tensor_tensor(fsw[:, c, :].rearrange("p (e q) -> p e q", e=NE),
                                        fs[:, c, :].rearrange("p (e q) -> p e q", e=NE),
                                        spread(wt[:, c, :], R), ALU.mult).then_inc(on.f_sw, 1)

            def body(ra, rx, rf):
                if ra is not None:
                    rstd("a", ra)
                if rx is not None:
                    rstd("x", rx)
                if rf is not None:
                    rstd("f", rf)
                if ra is not None:
                    a_tap0(ra)
                if rx is not None:
                    x_kbd(rx)
                if ra is not None:
                    a_cos(ra)
                if rf is not None:
                    f_sw(rf, 0)
                if rx is not None:
                    x_x1b(rx)
                if ra is not None:
                    a_oks(ra)
                if rf is not None:
                    f_sw(rf, 1)
                if ra is not None:
                    a_qn(ra)
                    a_orinv(ra)
                    a_o2(ra)

            pool.memset(raw[:], 0.0)
            pool.memset(Vx[:], 1.0).then_inc(z_ready, 1)
            pool.memset(q_bd[:], 0.0).then_inc(z_ready, 1)
            pool.memset(qn_bd[:], 0.0).then_inc(z_ready, 1)
            pool.wait_ge(ld_w, W_LANDED)
            pool.wait_ge(w_ready, 4)
            pool.wait_ge(z_ready, 3)
            iterations(pool, body)


def constants():
    f32 = np.float32
    freq = (1.0 / 10000.0 ** (np.arange(0, KD, 2, dtype=f32) / f32(KD))).astype(f32)
    angle = (np.arange(T, dtype=f32)[:, None] * freq[None, :]).astype(f32)
    lane = np.arange(P) % KD
    cos = np.cos(angle)[:, lane % (KD // 2)].T
    sin = np.sin(angle)[:, lane % (KD // 2)].T * np.where(lane < KD // 2, -1.0, 1.0)[:, None]
    return {
        "ident": np.eye(P, dtype=f32),
        "tri": np.triu(np.ones((P, P), f32)),
        "cosT": np.ascontiguousarray(cos, f32),
        "sinT": np.ascontiguousarray(sin, f32),
        "headmask": (np.arange(P)[:, None] // HD == np.arange(HB)[None, :]).astype(f32),
        "iota8": np.tile(np.arange(NE, dtype=f32), (P, 1)),
    }


def kernel(**inputs):
    import concourse.bacc as bacc
    from concourse.bass_utils import run_bass_kernel_spmd

    def t(name):
        return np.ascontiguousarray(np.transpose(np.asarray(inputs[name])))

    arrays = {
        "x": inputs["x"],
        "ctxT": np.transpose(np.asarray(inputs["ctx_1024"]), (0, 2, 1)),
        "mask": inputs["mask_Bx1xSxS2_bk0"],
        "Wq": inputs["L0_attn_Wq"], "Wk": inputs["L0_attn_Wk"], "Wv": inputs["L0_attn_Wv"],
        "Ws": inputs["L0_attn_Ws"], "Wg": inputs["L0_attn_Wg"], "Wo": inputs["L0_attn_Wo"],
        "qconv": inputs["L0_attn_qconv_w"], "kconv": inputs["L0_attn_kconv_w"],
        "vconv": inputs["L0_attn_vconv_w"], "gnorm": inputs["L0_attn_gnorm_w"],
        "xWqT": t("L0_xattn_W_q"), "xWkT": t("L0_xattn_W_k"), "xWvT": t("L0_xattn_W_v"),
        "xWpT": t("L0_xattn_W_proj"),
        "xbias": np.broadcast_to(np.asarray(inputs["L0_xattn_b_proj"])[None, :], (P, D)),
        "gate_w": inputs["L0_ffn_gate_w"], "fWu": inputs["L0_ffn_Wu"], "fWv": inputs["L0_ffn_Wv"],
        "fWo": inputs["L0_ffn_Wo"],
    } | constants()
    arrays = {f"in_{n}": np.ascontiguousarray(v) for n, v in arrays.items()}

    nc = bacc.Bacc("TRN2", target_bir_lowering=False, num_devices=1)
    aps = {n[3:]: nc.dram_tensor(n, v.shape, mybir.dt.from_np(v.dtype), kind="ExternalInput").ap()
           for n, v in arrays.items()}
    aps["out"] = nc.dram_tensor("out_0", (B, T, D), F32, kind="ExternalOutput").ap()
    build(nc, aps)
    return run_bass_kernel_spmd(nc, [arrays], core_ids=[0]).results[0]["out_0"]
```

```python
from collections import namedtuple
from contextlib import ExitStack

import numpy as np

import concourse.bass as bass
from concourse import mybir

F32 = mybir.dt.float32
F32R = mybir.dt.float32r
BF16 = mybir.dt.bfloat16
U8 = mybir.dt.uint8
U32 = mybir.dt.uint32
ALU = mybir.AluOpType
ACT = mybir.ActivationFunctionType
AX = mybir.AxisListType

P = 128
B, T, D = 32, 256, 256
TC = T // P
KC = D // P
H, M, KD, VD = 4, 64, 32, 64
TAPS = 4
S2, NH, HD = 77, 16, 16
UH = 4
QU = NH // UH
NU = TC * QU
HB = P // HD
NE, R, TOPK = 8, 64, 2
RC = NE * R // P
EPS = 1e-5
CLIP = 32.0
MASKED = -(2.0 ** 100)

Row = namedtuple("Row", "half parity")


STEPS = (
    "a_qk_ps a_v_ps a_s_ps a_g_ps a_qk_raw a_v_raw a_tap0 a_conv a_convt a_qk a_v a_rot a_cos "
    "a_sin a_kr a_qbd a_sc a_E a_C_ps a_rC a_ET_ps a_ET a_ktok_ps a_vtok_ps a_ktok a_vtok a_gt a_gate "
    "a_A_ps a_A a_state_ps a_state a_ok_ps a_okn a_max a_oks a_oke a_sum a_ssq a_qn a_qnT_ps "
    "a_qnT a_P_ps a_P a_o_ps a_osq a_oss a_ove a_orinv a_o1 a_o2 a_oT_ps a_oT a_wo_ps a_x1 "
    "x_k_ps x_v_ps x_q_ps x_k x_kl x_kbd x_v x_q x_ql a_xnTl f_xnTl x_neg x_s_ps x_max x_sub x_prob x_pT_ps x_pT "
    "x_av_ps x_rs x_o x_oT_ps x_oT x_x1b x_proj_ps x_x2 f_gate_ps f_logit f_top f_topi f_topf "
    "f_gap f_egap f_gden f_gw1 f_gw2 f_wt12 f_wt f_u_ps f_v_ps f_th f_su f_s f_sw f_sT_ps "
    "f_sT f_y_ps f_y "
)
NORM_STEPS = "stats mv ve rstd xn xnT_ps xnT"
Signals = namedtuple("Signals", STEPS + NORM_STEPS)


def build(nc, a):
    ctx = ExitStack()
    with ctx:
        def sb(name, shape, dt=F32):
            return ctx.enter_context(nc.sbuf_tensor(name, shape, dt))

        def halves(name, shape):
            return sb(f"{name}_hi", shape, F32R), sb(f"{name}_lo", shape, F32R)

        def sem(name):
            return ctx.enter_context(nc.semaphore(name))

        ident = sb("ident", [P, P])
        ident_bf = sb("ident_bf", [P, P], BF16)
        tri = sb("tri", [P, P])
        ones = sb("ones", [P, P])
        cosT = sb("cosT", [P, T])
        sinT = sb("sinT", [P, T])
        headmask = sb("headmask", [P, HB])
        iota8 = sb("iota8", [P, NE])
        mhalf = sb("mhalf", [P, 2 * H])
        dve_scrap = sb("dve_scrap", [P, 1])
        pool_scrap = sb("pool_scrap", [P, 1])
        wqk = halves("wqk", [P, KC, 2, H * KD])
        wv = halves("wv", [P, KC, D])
        ws = halves("ws", [P, KC, D])
        wg = halves("wg", [P, KC, D])
        wo = sb("wo", [P, KC, D])
        gnorm = sb("gnorm", [P, 1])
        cw = sb("cw", [P, 4, TAPS])
        xwq = sb("xwq", [P, KC, D])
        xwk = sb("xwk", [P, KC, D])
        xwv = sb("xwv", [P, KC, D])
        xwp = sb("xwp", [P, KC, D])
        xbias = sb("xbias", [P, D])
        fgate_raw = sb("fgate_raw", [P, KC, NE])
        fgate = halves("fgate", [P, KC, NE])
        fwu = halves("fwu", [P, KC, NE * R])
        fwv = halves("fwv", [P, KC, NE * R])
        fwo = sb("fwo", [P, RC, D])

        x0 = [sb(f"x0_{i}", [P, TC, D]) for i in range(2)]
        x1 = [sb(f"x1_{i}", [P, TC, D]) for i in range(2)]
        x2 = [sb(f"x2_{i}", [P, TC, D]) for i in range(2)]
        y = [sb(f"y_{i}", [P, TC, D]) for i in range(2)]
        ctxT = [sb(f"ctxT_{i}", [P, KC, S2]) for i in range(2)]
        keep = [sb(f"keep_{i}", [P, TC, S2], U8) for i in range(2)]

        ln_stats = {s: sb(f"{s}_stats", [P, TC, 6]) for s in "axf"}
        ln_mv = {s: sb(f"{s}_mv", [P, TC, 2]) for s in "axf"}
        ln_ve = {s: sb(f"{s}_ve", [P, TC]) for s in "axf"}
        ln_rstd = {s: sb(f"{s}_rstd", [P, TC]) for s in "axf"}
        xn = {s: sb(f"{s}_xn", [P, TC, D]) for s in "axf"}
        xnT = {"a": halves("a_xnT", [P, KC, T]), "x": sb("x_xnT", [P, KC, T]), "f": halves("f_xnT", [P, KC, T])}

        raw = sb("a_raw", [P, 4, TAPS - 1 + T])
        conv = sb("a_conv", [P, 4, T])
        convt = sb("a_convt", [P, 4, T])
        qkv = sb("a_qkv", [P, 4, T])
        rot = sb("a_rot", [P, 2, T])
        qkcos = sb("a_qkcos", [P, 2, T])
        qksin = sb("a_qksin", [P, 2, T])
        qkr = sb("a_qkr", [P, 2, T])
        kr = qkr[:, 1, :]
        q_bd = sb("a_q_bd", [P, H, T])
        ktok = sb("a_ktok", [P, P])
        vtok = sb("a_vtok", [P, TC, D])
        gt = sb("a_gt", [P, TC, D])
        gate = sb("a_gate", [P, TC, D])
        sc = sb("a_sc", [P, TC, D])
        E = sb("a_E", [P, TC, D])
        ET = sb("a_ET", [P, KC, T])
        rC = sb("a_rC", [P, TC, D])
        AT = sb("a_AT", [P, TC, H, P])
        PT = sb("a_PT", [P, TC, H, P])
        state = sb("a_state", [P, 2 * D])
        okn = sb("a_okn", [P, TC, D])
        oks = sb("a_oks", [P, TC, D])
        oke = sb("a_oke", [P, TC, D])
        qn = sb("a_qn", [P, TC, D])
        okmax = sb("a_okmax", [P, TC * H])
        ssum = sb("a_ssum", [P, TC * H])
        ssq = sb("a_ssq", [P, TC * H])
        qn_bd = sb("a_qn_bd", [P, 2, 2, T])
        osq = sb("a_osq", [P, TC, D])
        oss = sb("a_oss", [P, TC * H])
        ove = sb("a_ove", [P, TC * H])
        orinv = sb("a_orinv", [P, TC * H])
        o1 = sb("a_o1", [P, TC, D])
        o2 = sb("a_o2", [P, TC, D])
        oT = sb("a_oT", [P, KC, T])

        at_flat, pt_flat = [t[:].rearrange("p c h t -> p (c h t)") for t in (AT, PT)]
        wqk_raw = at_flat[:, 0:KC * 2 * P].rearrange("p (k j n) -> p k j n", k=KC, j=2)
        wv_raw = at_flat[:, KC * D:2 * KC * D].rearrange("p (k n) -> p k n", k=KC)
        ws_raw = pt_flat[:, 0:KC * D].rearrange("p (k n) -> p k n", k=KC)
        wg_raw = pt_flat[:, KC * D:2 * KC * D].rearrange("p (k n) -> p k n", k=KC)
        wo_raw = o1

        negmask = sb("x_negmask", [P, TC, S2], BF16)
        QT = halves("x_QT", [P, KC, T])
        KT = halves("x_KT", [P, KC, S2])
        KT_bd = halves("x_KT_bd", [P, KC, HB, S2])
        Vx = sb("x_Vx", [S2, NH, HD + 1])
        smax = sb("x_smax", [P, 2, UH])
        ssub = sb("x_ssub", [P, 2, UH, S2])
        prob = sb("x_prob", [P, 2, UH, S2])
        probT = sb("x_probT", [S2, 2, UH, P])
        xrs = sb("x_rs", [P, TC, NH])
        xo = sb("x_o", [P, TC, D])
        xoT = sb("x_oT", [P, KC, T])
        x1b = sb("x_x1b", [P, TC, D])

        logit = sb("f_logit", [P, TC, NE])
        top = sb("f_top", [P, TC, 8])
        topi = sb("f_topi", [P, TC, 8], U32)
        topf = sb("f_topf", [P, TC, 8])
        gap = sb("f_gap", [P, TC])
        egap = sb("f_egap", [P, TC])
        gden = sb("f_gden", [P, TC])
        gw = sb("f_gw", [P, 2, TC])
        wt1 = sb("f_wt1", [P, TC, NE])
        wt2 = sb("f_wt2", [P, TC, NE])
        wt = sb("f_wt", [P, TC, NE])
        fth = sb("f_th", [P, NE * R])
        fsu = sb("f_su", [P, NE * R])
        fs = sb("f_s", [P, 2, NE * R])
        fsw = sb("f_sw", [P, 2, NE * R])
        fwu_raw, fwv_raw = fs, fsw
        fsT = sb("f_sT", [P, 2, RC, P])

        bank = [ctx.enter_context(nc.psum_tensor(f"bank{i}", [P, 512], F32)) for i in range(8)]
        A0, A1, A2, X0, X1, X2, F0, F1 = bank

        ld_w = sem("ld_w")
        ld_x = [sem(f"ld_x{i}") for i in range(2)]
        ld_c = [sem(f"ld_c{i}") for i in range(2)]
        st_y = [sem(f"st_y{i}") for i in range(2)]
        w_ready = sem("w_ready")
        w_split = sem("w_split")
        z_ready = sem("z_ready")
        on = Signals(*[sem(n) for n in STEPS.split()],
                     *[{s: sem(f"{s}_{n}") for s in "axf"} for n in NORM_STEPS.split()])

        def upto(row, n=1, k=None):
            return row.half * (2 * n) + (n * row.parity + (n if k is None else k))

        def later(row):
            return row.parity == 1 or not (isinstance(row.half, int) and row.half == 0)

        def before(row):
            return Row(row.half, 0) if row.parity == 1 else Row(row.half - 1, 1)

        def loaded(row, n=1):
            return row.half * (16 * n) + 16 * n

        def hold(eng, scrap):
            eng.tensor_tensor(scrap[:], mhalf[:, 0:1], mhalf[:, 0:1], ALU.mult)

        def iterations(eng, body):
            body(Row(0, 0), None, None, None)
            body(Row(0, 1), Row(0, 0), None, None)
            body(Row(1, 0), Row(0, 1), Row(0, 0), None)
            body(Row(1, 1), Row(1, 0), Row(0, 1), Row(0, 0))
            body(Row(2, 0), Row(1, 1), Row(1, 0), Row(0, 1))
            last = B // 2
            with eng.Fori(2, last - 1) as half:
                body(Row(half, 1), Row(half, 0), Row(half - 1, 1), Row(half - 1, 0))
                body(Row(half + 1, 0), Row(half, 1), Row(half, 0), Row(half - 1, 1))
            body(Row(last - 1, 1), Row(last - 1, 0), Row(last - 2, 1), Row(last - 2, 0))
            body(None, Row(last - 1, 1), Row(last - 1, 0), Row(last - 2, 1))
            body(None, None, Row(last - 1, 1), Row(last - 1, 0))
            body(None, None, None, Row(last - 1, 1))

        block = ctx.enter_context(nc.Block())

        weights = [
            (ident[:], a["ident"]), (tri[:], a["tri"]), (cosT[:], a["cosT"]), (sinT[:], a["sinT"]),
            (headmask[:], a["headmask"]), (iota8[:], a["iota8"]),
            (wqk_raw[:, :, 0, :], a["Wq"].rearrange("(k p) n -> p k n", p=P)),
            (wqk_raw[:, :, 1, :], a["Wk"].rearrange("(k p) n -> p k n", p=P)),
            (wv_raw[:], a["Wv"].rearrange("(k p) n -> p k n", p=P)),
            (cw[:, 0, :], a["qconv"].rearrange("c o k -> c (o k)")),
            (cw[:, 1, :], a["kconv"].rearrange("c o k -> c (o k)")),
            (cw[:, 2:4, :], a["vconv"].rearrange("(j p) o k -> p j (o k)", p=P)),
            (ws_raw[:], a["Ws"].rearrange("(k p) n -> p k n", p=P)),
            (wg_raw[:], a["Wg"].rearrange("(k p) n -> p k n", p=P)),
            (wo_raw[:], a["Wo"].rearrange("(k p) n -> p k n", p=P)),
            (gnorm[0:VD, :], a["gnorm"].rearrange("(v o) -> v o", o=1)),
            (gnorm[VD:2 * VD, :], a["gnorm"].rearrange("(v o) -> v o", o=1)),
            (xwq[:], a["xWqT"].rearrange("(k p) n -> p k n", p=P)),
            (xwk[:], a["xWkT"].rearrange("(k p) n -> p k n", p=P)),
            (xwv[:], a["xWvT"].rearrange("(k p) n -> p k n", p=P)),
            (xwp[:], a["xWpT"].rearrange("(k p) n -> p k n", p=P)),
            (xbias[:], a["xbias"]),
            (fgate_raw[:], a["gate_w"].rearrange("(k p) n -> p k n", p=P)),
            (fwo[:], a["fWo"].rearrange("e r n -> (e r) n").rearrange("(c p) n -> p c n", p=P)),
        ] + [
            (w[:, k, :].rearrange("p (e r) -> p e r", e=NE), a[n][:, k * P:(k + 1) * P, :].rearrange("e p r -> p e r"))
            for w, n in ((fwu_raw, "fWu"), (fwv_raw, "fWv")) for k in range(KC)
        ]
        splits = [(wqk, wqk_raw), (wv, wv_raw), (ws, ws_raw), (wg, wg_raw), (fgate, fgate_raw), (fwu, fwu_raw),
                  (fwv, fwv_raw)]
        W_LANDED = 16 * len(weights)

        def row_of(ap, row):
            return ap[bass.ds(row.half * 2 + row.parity, 1)]

        @block.sync
        def _(sp):
            def load_x(row):
                sp.dma_start(x0[row.parity][:], row_of(a["x"], row).rearrange("o (c p) d -> p (o c) d", p=P)
                             ).then_inc(ld_x[row.parity], 16)

            def load_context(row):
                c, m = ctxT[row.parity], keep[row.parity]
                sp.dma_start(c[:], row_of(a["ctxT"], row).rearrange("o (k p) s -> p (o k) s", p=P)
                             ).then_inc(ld_c[row.parity], 16)
                sp.dma_start(m[:], row_of(a["mask"], row).rearrange("o u (c p) s -> p (o u c) s", p=P)
                             ).then_inc(ld_c[row.parity], 16)

            def body(ra, rx, rf):
                if ra is not None:
                    if not (isinstance(ra.half, int) and ra.half == 0 and ra.parity == 0):
                        if later(ra):
                            sp.wait_ge(on.a_x1, upto(before(ra)))
                        load_x(Row(ra.half, 1) if ra.parity == 0 else Row(ra.half + 1, 0))
                    if rf is not None:
                        sp.wait_ge(on.x_neg, upto(rf))
                        sp.wait_ge(on.x_v_ps, upto(rf))
                    load_context(ra)
                if rf is not None:
                    sp.wait_ge(on.f_y, upto(rf))
                    sp.dma_start(row_of(a["out"], rf).rearrange("o (c p) d -> p (o c) d", p=P),
                                 y[rf.parity][:]).then_inc(st_y[rf.parity], 16)

            load_x(Row(0, 0))
            for dst, src in weights:
                sp.dma_start(dst, src).then_inc(ld_w, 16)
            load_x(Row(0, 1))
            body(Row(0, 0), None, None)
            body(Row(0, 1), Row(0, 0), None)
            body(Row(1, 0), Row(0, 1), Row(0, 0))
            body(Row(1, 1), Row(1, 0), Row(0, 1))
            with sp.Fori(2, B // 2 - 1) as half:
                body(Row(half, 0), Row(half - 1, 1), Row(half - 1, 0))
                body(Row(half, 1), Row(half, 0), Row(half - 1, 1))
            last = B // 2
            body(Row(last - 1, 0), Row(last - 2, 1), Row(last - 2, 0))
            sp.wait_ge(on.x_neg, upto(Row(last - 2, 1)))
            sp.wait_ge(on.x_v_ps, upto(Row(last - 2, 1)))
            load_context(Row(last - 1, 1))
            for rf in (Row(last - 2, 1), Row(last - 1, 0), Row(last - 1, 1)):
                sp.wait_ge(on.f_y, upto(rf))
                sp.dma_start(row_of(a["out"], rf).rearrange("o (c p) d -> p (o c) d", p=P),
                             y[rf.parity][:]).then_inc(st_y[rf.parity], 16)
            for i in range(2):
                sp.wait_ge(st_y[i], 16 * (B // 2))

        @block.tensor
        def _(pe):
            def mm(out, lhsT, rhs, start=True, stop=True):
                return pe.matmul(out, lhsT, rhs, start=start, stop=stop, skip_group_check=True)

            def turn(dst, src):
                for k in range(KC):
                    for c in range(TC):
                        ins = pe.transpose(dst[:, k * T + c * P:k * T + (c + 1) * P],
                                           src[:, c, k * P:(k + 1) * P], ident[:])
                return ins

            def mm_halves(dst, pairs):
                n = len(pairs)
                for i, (lhsT, rhs) in enumerate(pairs):
                    mm(dst, lhsT(0), rhs(0), start=(i == 0), stop=False)
                    mm(dst, lhsT(0), rhs(1), start=False, stop=False)
                    ins = mm(dst, lhsT(1), rhs(0), start=False, stop=(i == n - 1))
                return ins

            def features(dst, w, act):
                for k in range(KC):
                    ins = mm(dst, w(k), act(k), start=(k == 0), stop=(k == KC - 1))
                return ins

            def a_turn(r):
                if later(r):
                    pe.wait_ge(on.a_osq, upto(before(r)))
                if later(r):
                    pe.wait_ge(on.a_o1, upto(before(r)))
                pe.wait_ge(on.xn["a"], upto(r))
                turn(A0, xn["a"]).then_inc(on.xnT_ps["a"], 1)

            def a_qk(r):
                pe.wait_ge(on.xnT["a"], upto(r))
                if later(r):
                    pe.wait_ge(on.a_oT, upto(before(r)))
                pe.wait_ge(on.a_xnTl, upto(r))
                for j in range(2):
                    ins = mm_halves(A1[:, j * T:(j + 1) * T], [
                        (lambda i, k=k: wqk[i][:, k, j, :], lambda i, k=k: xnT["a"][i][:, k, :]) for k in range(KC)])
                ins.then_inc(on.a_qk_ps, 1)

            def a_v(r):
                if later(r):
                    pe.wait_ge(on.a_x1, upto(before(r)))
                pe.wait_ge(on.xnT["a"], upto(r))
                pe.wait_ge(on.a_xnTl, upto(r))
                for j in range(2):
                    ins = mm_halves(A2[:, j * T:(j + 1) * T], [
                        (lambda i, k=k: wv[i][:, k, j * P:(j + 1) * P], lambda i, k=k: xnT["a"][i][:, k, :])
                        for k in range(KC)])
                ins.then_inc(on.a_v_ps, 1)

            def tokens(dst, act, w):
                for c in range(TC):
                    for k in range(KC):
                        ins = mm(dst[:, c * D:(c + 1) * D], act[:, k, c * P:(c + 1) * P], w[:, k, :],
                                 start=(k == 0), stop=(k == KC - 1))
                return ins

            def tokens_halves(dst, act, w):
                for c in range(TC):
                    ins = mm_halves(dst[:, c * D:(c + 1) * D], [
                        (lambda i, k=k: act[i][:, k, c * P:(c + 1) * P], lambda i, k=k: w[i][:, k, :])
                        for k in range(KC)])
                return ins

            def a_s(r):
                pe.wait_ge(on.xnT["a"], upto(r))
                pe.wait_ge(on.a_xnTl, upto(r))
                tokens_halves(A0, xnT["a"], ws).then_inc(on.a_s_ps, 1)

            def a_g(r):
                pe.wait_ge(on.a_qk_raw, upto(r))
                pe.wait_ge(on.xnT["a"], upto(r))
                pe.wait_ge(on.a_xnTl, upto(r))
                tokens_halves(A1, xnT["a"], wg).then_inc(on.a_g_ps, 1)

            def a_et(r):
                pe.wait_ge(on.a_v_raw, upto(r))
                pe.wait_ge(on.a_E, upto(r))
                turn(A2, E).then_inc(on.a_ET_ps, 1)

            def a_c(r):
                pe.wait_ge(on.a_sc, upto(r))
                pe.wait_ge(on.a_E, upto(r))
                mm(A0[:, 0:D], tri[:], E[:, 0, :])
                mm(A0[:, D:2 * D], ones[:], E[:, 0, :], stop=False)
                mm(A0[:, D:2 * D], tri[:], E[:, 1, :], start=False).then_inc(on.a_C_ps, 1)

            def a_ktok(r):
                pe.wait_ge(on.a_kr, upto(r))
                pe.wait_ge(on.a_rC, upto(r))
                pe.transpose(A0[:, 0:P], kr[:, 0:P], ident[:]).then_inc(on.a_ktok_ps, 1)

            def a_vtok(r):
                pe.wait_ge(on.a_v, upto(r))
                pe.wait_ge(on.a_gate, upto(r))
                for c in range(TC):
                    for j in range(2):
                        ins = pe.transpose(A1[:, c * D + j * P:c * D + (j + 1) * P],
                                           qkv[:, 2 + j, c * P:(c + 1) * P], ident[:])
                ins.then_inc(on.a_vtok_ps, 1)

            def a_A(r, c):
                if c == 0:
                    pe.wait_ge(on.a_kr, upto(r))
                    pe.wait_ge(on.a_qbd, upto(r))
                    pe.wait_ge(on.a_ET, upto(r))
                else:
                    pe.wait_ge(on.a_qbd, upto(r))
                    pe.wait_ge(on.a_ktok, upto(r))
                mm((A2 if c == 0 else A0)[:, :], kr[:, c * P:(c + 1) * P], q_bd[:, :, c * P:(c + 1) * P]
                   ).then_inc(on.a_A_ps, 1)

            def a_state(r):
                pe.wait_ge(on.a_ktok, upto(r))
                pe.wait_ge(on.a_vtok, upto(r))
                mm(A1[:, 0:D], ktok[:], E[:, 0, :])
                for f in range(2):
                    ins = mm(A1[:, D + f * P:D + (f + 1) * P], E[:, 0, f * P:(f + 1) * P],
                             vtok[:, 0, f * P:(f + 1) * P])
                ins.then_inc(on.a_state_ps, 1)

            def a_ok(r):
                pe.wait_ge(on.a_A, upto(r, TC))
                pe.wait_ge(on.a_state, upto(r))
                pe.wait_ge(on.a_E, upto(r))
                for h in range(H):
                    mm(A2[:, h * M:(h + 1) * M], AT[:, 0, h, :], E[:, 0, h * M:(h + 1) * M])
                for h in range(H):
                    out = A2[:, D + h * M:D + (h + 1) * M]
                    mm(out, q_bd[:, h, P:2 * P], state[:, h * M:(h + 1) * M], stop=False)
                    ins = mm(out, AT[:, 1, h, :], E[:, 1, h * M:(h + 1) * M], start=False)
                ins.then_inc(on.a_ok_ps, 1)

            def a_qt(r):
                pe.wait_ge(on.a_qn, upto(r))
                turn(A0, qn).then_inc(on.a_qnT_ps, 1)

            def a_P(r, c):
                if c == 0:
                    pe.wait_ge(on.a_qnT, upto(r, 2))
                else:
                    pe.wait_ge(on.a_qnT, upto(r, 2))
                    pe.wait_ge(on.a_okn, upto(r))
                dst = A1 if c == 0 else A2
                for f in range(2):
                    ins = mm(dst[:, f * 2 * P:(f + 1) * 2 * P], ET[:, f, c * P:(c + 1) * P],
                             qn_bd[:, f, :, c * P:(c + 1) * P])
                ins.then_inc(on.a_P_ps, 1)

            def a_o(r):
                pe.wait_ge(on.a_P, upto(r, TC))
                for h in range(H):
                    mm(A0[:, h * VD:(h + 1) * VD], PT[:, 0, h, :], vtok[:, 0, h * VD:(h + 1) * VD])
                for h in range(H):
                    f, hh = h // 2, h % 2
                    out = A0[:, D + h * VD:D + (h + 1) * VD]
                    mm(out, qn_bd[:, f, hh, P:2 * P], state[:, D + f * P + hh * VD:D + f * P + (hh + 1) * VD],
                       stop=False)
                    ins = mm(out, PT[:, 1, h, :], vtok[:, 1, h * VD:(h + 1) * VD], start=False)
                ins.then_inc(on.a_o_ps, 1)

            def a_ot(r):
                pe.wait_ge(on.a_o2, upto(r))
                turn(A1, o2).then_inc(on.a_oT_ps, 1)

            def a_wo(r):
                pe.wait_ge(on.a_oT, upto(r))
                tokens(A2, oT, wo).then_inc(on.a_wo_ps, 1)

            def x_turn(r):
                if later(r):
                    pe.wait_ge(on.x_x2, upto(before(r)))
                pe.wait_ge(on.xn["x"], upto(r))
                turn(X0, xn["x"]).then_inc(on.xnT_ps["x"], 1)

            def x_k(r):
                pe.wait_ge(ld_c[r.parity], loaded(r, 2))
                if later(r):
                    pe.wait_ge(on.x_oT, upto(before(r)))
                c = ctxT[r.parity]
                for j in range(2):
                    ins = features(X1[:, j * S2:(j + 1) * S2], lambda k: xwk[:, k, j * P:(j + 1) * P],
                                   lambda k: c[:, k, :])
                ins.then_inc(on.x_k_ps, 1)

            def x_v(r):
                pe.wait_ge(ld_c[r.parity], loaded(r, 2))
                c = ctxT[r.parity]
                if later(r):
                    pe.wait_ge(on.x_o, upto(before(r), TC))
                for k in range(KC):
                    ins = mm(X2[0:S2, 0:D], c[:, k, :], xwv[:, k, :], start=(k == 0), stop=(k == KC - 1))
                ins.then_inc(on.x_v_ps, 1)

            def x_q(r):
                pe.wait_ge(on.xnT["x"], upto(r))
                for j in range(2):
                    ins = features(X0[:, j * T:(j + 1) * T], lambda k: xwq[:, k, j * P:(j + 1) * P],
                                   lambda k: xnT["x"][:, k, :])
                ins.then_inc(on.x_q_ps, 1)

            def x_s(r, u):
                c, q = divmod(u, QU)
                f, hh = divmod(q * UH, HB)
                if u == 0:
                    pe.wait_ge(on.x_q, upto(r))
                    pe.wait_ge(on.x_ql, upto(r))
                    pe.wait_ge(on.x_kbd, upto(r))
                    pe.wait_ge(on.x_neg, upto(r))
                else:
                    pe.wait_ge(on.x_sub, upto(r, NU, u))
                out = X0[:, 0:UH * S2]
                mm(out, QT[0][:, f, c * P:(c + 1) * P], KT_bd[0][:, f, hh:hh + UH, :], stop=False)
                mm(out, QT[0][:, f, c * P:(c + 1) * P], KT_bd[1][:, f, hh:hh + UH, :], start=False, stop=False)
                mm(out, QT[1][:, f, c * P:(c + 1) * P], KT_bd[0][:, f, hh:hh + UH, :], start=False, stop=False)
                mm(out, ident_bf[:], negmask[:, c:c + 1, :].broadcast_to([P, UH, S2]), start=False
                   ).then_inc(on.x_s_ps, 1)

            def x_pt(r, u):
                pe.wait_ge(on.x_prob, upto(r, NU, u + 1))
                if u == 0:
                    pe.wait_ge(on.x_k, upto(r))
                    pe.wait_ge(on.x_kl, upto(r))
                else:
                    pe.wait_ge(on.x_pT, upto(r, NU, u))
                for i in range(UH):
                    ins = pe.transpose(X1[0:S2, i * P:(i + 1) * P], prob[:, u % 2, i, :], ident[:])
                ins.then_inc(on.x_pT_ps, 1)

            def x_av(r, u):
                c, q = divmod(u, QU)
                if u == 0:
                    pe.wait_ge(on.x_v, upto(r))
                elif q == 0:
                    pe.wait_ge(on.x_o, upto(r, TC, c))
                pe.wait_ge(on.x_pT, upto(r, NU, u + 1))
                for i in range(UH):
                    h = q * UH + i
                    ins = mm(X2[:, h * (HD + 1):(h + 1) * (HD + 1)], probT[:, u % 2, i, :], Vx[:, h, :])
                ins.then_inc(on.x_av_ps, 1)

            def x_ot(r):
                pe.wait_ge(on.x_o, upto(r, TC))
                turn(X1, xo).then_inc(on.x_oT_ps, 1)

            def x_proj(r):
                pe.wait_ge(on.x_oT, upto(r))
                tokens(X0, xoT, xwp).then_inc(on.x_proj_ps, 1)

            def f_turn(r):
                if later(r):
                    pe.wait_ge(on.f_y, upto(before(r)))
                pe.wait_ge(on.xn["f"], upto(r))
                turn(F0, xn["f"]).then_inc(on.xnT_ps["f"], 1)

            def f_gate(r):
                pe.wait_ge(on.xnT["f"], upto(r))
                if later(r):
                    pe.wait_ge(on.f_sT, upto(before(r), TC))
                pe.wait_ge(on.f_xnTl, upto(r))
                for c in range(TC):
                    ins = mm_halves(F1[:, c * NE:(c + 1) * NE], [
                        (lambda i, k=k: xnT["f"][i][:, k, c * P:(c + 1) * P], lambda i, k=k: fgate[i][:, k, :])
                        for k in range(KC)])
                ins.then_inc(on.f_gate_ps, 1)

            def f_up(c, dst, w):
                return mm_halves(dst[:, :], [
                    (lambda i, k=k: xnT["f"][i][:, k, c * P:(c + 1) * P], lambda i, k=k: w[i][:, k, :])
                    for k in range(KC)])

            def f_u0(r):
                pe.wait_ge(on.xnT["f"], upto(r))
                pe.wait_ge(on.f_xnTl, upto(r))
                f_up(0, F0, fwu).then_inc(on.f_u_ps, 1)

            def f_v0(r):
                pe.wait_ge(on.f_logit, upto(r))
                f_up(0, F1, fwv).then_inc(on.f_v_ps, 1)

            def f_u1(r):
                pe.wait_ge(on.f_s, upto(r, TC, 1))
                f_up(1, F1, fwu).then_inc(on.f_u_ps, 1)

            def f_v1(r):
                pe.wait_ge(on.f_sT, upto(r, TC, 1))
                f_up(1, F0, fwv).then_inc(on.f_v_ps, 1)

            def f_st(r, c):
                pe.wait_ge(on.f_sw, upto(r, TC, c + 1))
                pe.wait_ge(on.f_su, upto(r, TC, c + 1))
                dst = F0 if c == 0 else F1
                for i in range(RC):
                    ins = pe.transpose(dst[:, i * P:(i + 1) * P], fsw[:, c, i * P:(i + 1) * P], ident[:])
                ins.then_inc(on.f_sT_ps, 1)

            def f_yy(r):
                pe.wait_ge(on.f_sT, upto(r, TC))
                pe.wait_ge(on.f_s, upto(r, TC))
                for c in range(TC):
                    for i in range(RC):
                        ins = mm(F0[:, c * D:(c + 1) * D], fsT[:, c, i, :], fwo[:, i, :],
                                 start=(i == 0), stop=(i == RC - 1))
                ins.then_inc(on.f_y_ps, 1)

            def body(rn, ra, rx, rf):
                def N(f, *k):
                    if rn is not None:
                        f(rn, *k)

                def A(f, *k):
                    if ra is not None:
                        f(ra, *k)

                def X(f, *k):
                    if rx is not None:
                        f(rx, *k)

                def F(f, *k):
                    if rf is not None:
                        f(rf, *k)

                A(a_turn); X(x_k); X(x_v); A(a_qk); A(a_v); A(a_s); A(a_g); F(f_turn); X(x_turn); A(a_et)
                X(x_q); F(f_gate); F(f_u0); X(x_s, 0); A(a_c); F(f_v0); X(x_pt, 0); X(x_s, 1); X(x_av, 0)
                A(a_ktok); A(a_vtok); A(a_A, 0); A(a_A, 1); X(x_pt, 1); X(x_s, 2); X(x_av, 1); A(a_state)
                X(x_pt, 2); X(x_s, 3); A(a_ok); X(x_av, 2); X(x_pt, 3); X(x_s, 4); X(x_av, 3); F(f_st, 0)
                F(f_u1); X(x_pt, 4); X(x_s, 5); F(f_v1); A(a_qt); X(x_pt, 5); X(x_s, 6); X(x_av, 4); A(a_P, 0)
                A(a_P, 1); X(x_pt, 6); X(x_s, 7); A(a_o); X(x_av, 5); X(x_pt, 7); F(f_st, 1); X(x_av, 6)
                X(x_av, 7); F(f_yy); X(x_ot); A(a_ot); X(x_proj); A(a_wo)

            pe.wait_ge(ld_w, W_LANDED)
            pe.wait_ge(w_ready, 4)
            pe.wait_ge(w_split, 2 * len(splits))
            pe.wait_ge(z_ready, 3)
            iterations(pe, body)

        @block.vector
        def _(dve):
            tt, ts, stt = dve.tensor_tensor, dve.tensor_scalar, dve.scalar_tensor_tensor

            def norm_stats(s, src, r):
                for c in range(TC):
                    dve.bn_stats(ln_stats[s][:, c, :], src[:, c, :]).then_inc(on.stats[s], 1)
                dve.wait_ge(on.stats[s], upto(r, TC))
                hold(dve, dve_scrap)
                for c in range(TC):
                    dve.bn_aggr(ln_mv[s][:, c, :], ln_stats[s][:, c, :]).then_inc(on.mv[s], 1)
                dve.wait_ge(on.mv[s], upto(r, TC))
                ts(ln_ve[s][:], ln_mv[s][:, :, 1], EPS, None, ALU.add).then_inc(on.ve[s], 1)

            def norm_apply(s, src, r):
                dve.wait_ge(on.rstd[s], upto(r))
                if later(r):
                    dve.wait_ge(on.xnT_ps[s], upto(before(r)))
                for c in range(TC):
                    ins = ts(xn[s][:, c, :], src[:, c, :], ln_mv[s][:, c, 0:1], ln_rstd[s][:, c:c + 1],
                             ALU.subtract, ALU.mult)
                ins.then_inc(on.xn[s], 1)

            def heads(ap):
                return ap.rearrange("p (g m) -> p g m", m=M)

            def flat(t):
                return t[:].rearrange("p c d -> p (c d)")

            def spread(small, n):
                return small.rearrange("p (g o) -> p g o", o=1).broadcast_to([P, small.shape[1], n])

            def low(lo, src, hi):
                return tt(flat(lo), src, flat(hi).bitcast(F32), ALU.subtract)

            def a_xntl(r):
                dve.wait_ge(on.xnT["a"], upto(r))
                if later(r):
                    dve.wait_ge(on.a_g_ps, upto(before(r)))
                low(xnT["a"][1], A0[:, :], xnT["a"][0]).then_inc(on.a_xnTl, 1)

            def a_norm1(r):
                dve.wait_ge(ld_x[r.parity], loaded(r))
                norm_stats("a", x0[r.parity], r)

            def a_norm2(r):
                norm_apply("a", x0[r.parity], r)

            def a_clip(r):
                dve.wait_ge(on.a_s_ps, upto(r))
                ts(flat(sc), A0[:, :], -CLIP, CLIP, ALU.max, ALU.min).then_inc(on.a_sc, 1)

            def a_gate(r):
                dve.wait_ge(on.a_gt, upto(r))
                if later(r):
                    dve.wait_ge(on.a_o2, upto(before(r)))
                stt(flat(gate), flat(gt), 1.0, A1[:, :], ALU.add, ALU.mult).then_inc(on.a_gate, 1)

            def a_conv(r):
                dve.wait_ge(on.a_tap0, upto(r))
                n = 0
                for i in range(1, TAPS):
                    for j in range(4):
                        n += 1
                        if i > 1:
                            dve.wait_ge(on.a_conv, upto(r, 3 * 4, n - 4))
                        stt(conv[:, j, :], raw[:, j, i:i + T], cw[:, j, i:i + 1], conv[:, j, :],
                                 ALU.mult, ALU.add).then_inc(on.a_conv, 1)

            def a_silu_qk(r):
                dve.wait_ge(on.a_convt, upto(r, 2, 1))
                stt(qkv[:, 0:2, :], convt[:, 0:2, :], 1.0, conv[:, 0:2, :], ALU.add, ALU.mult).then_inc(on.a_qk, 1)

            def a_rot(r):
                dve.wait_ge(on.a_qk, upto(r))
                if later(r):
                    dve.wait_ge(on.a_sin, upto(before(r)))
                hold(dve, dve_scrap)
                dve.stream_shuffle(rot[:, :, :], qkv[:, 0:2, :],
                                        [(i + KD // 2) % KD for i in range(KD)]).then_inc(on.a_rot, 1)

            def a_silu_v(r):
                dve.wait_ge(on.a_convt, upto(r, 2, 2))
                stt(qkv[:, 2:4, :], convt[:, 2:4, :], 1.0, conv[:, 2:4, :], ALU.add, ALU.mult).then_inc(on.a_v, 1)

            def a_qbd(r):
                dve.wait_ge(on.a_kr, upto(r))
                if later(r):
                    dve.wait_ge(on.a_ok_ps, upto(before(r)))
                for h in range(H):
                    s = slice(h * KD, (h + 1) * KD)
                    ins = dve.tensor_copy(q_bd[s, h, :], qkr[s, 0, :])
                ins.then_inc(on.a_qbd, 1)

            def a_rc(r):
                dve.wait_ge(on.a_C_ps, upto(r))
                dve.reciprocal(flat(rC), A0[:, :]).then_inc(on.a_rC, 1)

            def causal(dst, src):
                return tt(dst, src.rearrange("p (h t) -> p h t", h=H),
                          tri[:].rearrange("p (o t) -> p o t", o=1).broadcast_to([P, H, P]), ALU.mult)

            def a_maskA(r, c):
                dve.wait_ge(on.a_A_ps, upto(r, TC, c + 1))
                causal(AT[:, c], (A2 if c == 0 else A0)[:, :]).then_inc(on.a_A, 1)

            def a_okn(r):
                dve.wait_ge(on.a_ok_ps, upto(r))
                tt(flat(okn), A2[:, :], flat(rC), ALU.mult).then_inc(on.a_okn, 1)
                dve.wait_ge(on.a_okn, upto(r))
                dve.tensor_reduce(okmax[:], heads(flat(okn)), AX.X, ALU.max).then_inc(on.a_max, 1)

            def a_sum(r):
                dve.wait_ge(on.a_oke, upto(r))
                dve.tensor_reduce(ssum[:], heads(flat(oke)), AX.X, ALU.add).then_inc(on.a_sum, 1)
                dve.wait_ge(on.a_sum, upto(r))
                tt(ssq[:], ssum[:], ssum[:], ALU.mult).then_inc(on.a_ssq, 1)

            def a_maskP(r, c):
                dve.wait_ge(on.a_P_ps, upto(r, TC, c + 1))
                causal(PT[:, c], (A1 if c == 0 else A2)[:, :]).then_inc(on.a_P, 1)

            def a_oss(r):
                dve.wait_ge(on.a_osq, upto(r))
                dve.tensor_reduce(oss[:], heads(flat(osq)), AX.X, ALU.add).then_inc(on.a_oss, 1)
                dve.wait_ge(on.a_oss, upto(r))
                dve.wait_ge(on.a_ssq, upto(r))
                stt(ove[:], ssq[:], 4 * EPS * VD, oss[:], ALU.mult, ALU.add).then_inc(on.a_ove, 1)

            def a_o1(r):
                dve.wait_ge(on.a_orinv, upto(r))
                dve.wait_ge(on.a_o_ps, upto(r))
                tt(heads(flat(o1)), heads(A0[:, :]), spread(orinv[:], VD), ALU.mult).then_inc(on.a_o1, 1)

            def a_out(r):
                dve.wait_ge(on.a_wo_ps, upto(r))
                if not (isinstance(r.half, int) and r.half == 0):
                    dve.wait_ge(on.x_x1b, upto(Row(r.half - 1, r.parity)))
                    dve.wait_ge(on.xn["x"], upto(Row(r.half - 1, r.parity)))
                tt(flat(x1[r.parity]), A2[:, :], flat(x0[r.parity]), ALU.add).then_inc(on.a_x1, 1)

            def x_norm1(r):
                dve.wait_ge(on.a_x1, upto(r))
                norm_stats("x", x1[r.parity], r)

            def x_norm2(r):
                norm_apply("x", x1[r.parity], r)

            def x_kl(r):
                dve.wait_ge(on.x_k, upto(r))
                low(KT[1], X1[:, 0:KC * S2], KT[0]).then_inc(on.x_kl, 1)

            def x_ql(r):
                dve.wait_ge(on.x_q, upto(r))
                stt(flat(QT[1]), X0[:, :], HD ** -0.5, flat(QT[0]).bitcast(F32), ALU.mult, ALU.subtract
                    ).then_inc(on.x_ql, 1)

            def x_neg(r):
                dve.wait_ge(ld_c[r.parity], loaded(r, 2))
                if later(r):
                    dve.wait_ge(on.x_s_ps, upto(before(r), NU))
                ts(flat(negmask), keep[r.parity][:].rearrange("p c s -> p (c s)"), 0.0, MASKED,
                        ALU.is_equal, ALU.mult).then_inc(on.x_neg, 1)

            def x_soft(r, u):
                dve.wait_ge(on.x_s_ps, upto(r, NU, u + 1))
                src = X0[:, 0:UH * S2].rearrange("p (h s) -> p h s", h=UH)
                dve.tensor_reduce(smax[:, u % 2, :], src, AX.X, ALU.max).then_inc(on.x_max, 1)
                dve.wait_ge(on.x_max, upto(r, NU, u + 1))
                if u >= 2:
                    dve.wait_ge(on.x_prob, upto(r, NU, u - 1))
                else:
                    if later(r):
                        dve.wait_ge(on.x_prob, upto(before(r), NU, NU - 1 + u))
                tt(ssub[:, u % 2], src, spread(smax[:, u % 2, :], S2), ALU.subtract).then_inc(on.x_sub, 1)

            def x_o(r, c):
                dve.wait_ge(on.x_av_ps, upto(r, NU, (c + 1) * QU))
                src = X2[:, 0:NH * (HD + 1)].rearrange("p (h e) -> p h e", h=NH)
                dve.reciprocal(xrs[:, c, :], src[:, :, HD]).then_inc(on.x_rs, 1)
                dve.wait_ge(on.x_rs, upto(r, TC, c + 1))
                if c == 0:
                    if later(r):
                        dve.wait_ge(on.x_oT_ps, upto(before(r)))
                tt(xo[:, c, :].rearrange("p (h e) -> p h e", h=NH), src[:, :, 0:HD],
                        spread(xrs[:, c, :], HD), ALU.mult).then_inc(on.x_o, 1)

            def x_out(r):
                dve.wait_ge(on.x_proj_ps, upto(r))
                dve.wait_ge(on.x_x1b, upto(r))
                if not (isinstance(r.half, int) and r.half == 0):
                    dve.wait_ge(on.f_y, upto(Row(r.half - 1, r.parity)))
                tt(flat(x2[r.parity]), X0[:, :], flat(x1b), ALU.add).then_inc(on.x_x2, 1)

            def f_norm1(r):
                dve.wait_ge(on.x_x2, upto(r))
                norm_stats("f", x2[r.parity], r)

            def f_norm2(r):
                norm_apply("f", x2[r.parity], r)

            def f_xntl(r):
                dve.wait_ge(on.xnT["f"], upto(r))
                low(xnT["f"][1], F0[:, :], xnT["f"][0]).then_inc(on.f_xnTl, 1)

            def f_top(r):
                dve.wait_ge(on.f_gate_ps, upto(r))
                dve.tensor_copy(flat(logit), F1[:, 0:TC * NE]).then_inc(on.f_logit, 1)
                dve.wait_ge(on.f_logit, upto(r))
                hold(dve, dve_scrap)
                for c in range(TC):
                    dve.max(top[:, c, :], logit[:, c, :]).then_inc(on.f_top, 1)
                dve.wait_ge(on.f_top, upto(r, TC))
                hold(dve, dve_scrap)
                for c in range(TC):
                    dve.max_index(topi[:, c, :], top[:, c, :], logit[:, c, :]).then_inc(on.f_topi, 1)
                tt(gap[:], top[:, :, 1], top[:, :, 0], ALU.subtract).then_inc(on.f_gap, 1)
                dve.wait_ge(on.f_topi, upto(r, TC))
                dve.tensor_copy(flat(topf), topi[:].rearrange("p c n -> p (c n)")).then_inc(on.f_topf, 1)

            def f_weights(r):
                dve.wait_ge(on.f_egap, upto(r))
                ts(gden[:], egap[:], 1.0, 2.0, ALU.add, ALU.mult).then_inc(on.f_gden, 1)
                dve.wait_ge(on.f_gden, upto(r))
                dve.reciprocal(gw[:, 0, :], gden[:]).then_inc(on.f_gw1, 1)
                dve.wait_ge(on.f_gw1, upto(r))
                tt(gw[:, 1, :], gw[:, 0, :], egap[:], ALU.mult).then_inc(on.f_gw2, 1)
                dve.wait_ge(on.f_topf, upto(r))
                dve.wait_ge(on.f_gw2, upto(r))
                for c in range(TC):
                    ts(wt1[:, c, :], iota8[:], topf[:, c, 0:1], gw[:, 0, c:c + 1], ALU.is_equal, ALU.mult)
                    ins = ts(wt2[:, c, :], iota8[:], topf[:, c, 1:2], gw[:, 1, c:c + 1], ALU.is_equal, ALU.mult)
                ins.then_inc(on.f_wt12, 1)
                dve.wait_ge(on.f_wt12, upto(r))
                if later(r):
                    dve.wait_ge(on.f_sw, upto(before(r), TC))
                tt(flat(wt), flat(wt1), flat(wt2), ALU.add).then_inc(on.f_wt, 1)

            def f_s(r, c):
                dve.wait_ge(on.f_th, upto(r, TC, c + 1))
                stt(fsu[:], fth[:], 1.0, (F0 if c == 0 else F1)[:, :], ALU.add, ALU.mult).then_inc(on.f_su, 1)
                dve.wait_ge(on.f_su, upto(r, TC, c + 1))
                dve.wait_ge(on.f_v_ps, upto(r, TC, c + 1))
                if later(r):
                    dve.wait_ge(on.f_sw, upto(before(r), TC, c + 1))
                tt(fs[:, c, :], (F1 if c == 0 else F0)[:, :], fsu[:], ALU.mult).then_inc(on.f_s, 1)

            def f_out(r):
                dve.wait_ge(on.f_y_ps, upto(r))
                if not (isinstance(r.half, int) and r.half == 0):
                    dve.wait_ge(st_y[r.parity], r.half * 16)
                tt(flat(y[r.parity]), F0[:, :], flat(x2[r.parity]), ALU.add).then_inc(on.f_y, 1)

            def body(rn, ra, rx, rf):
                def N(f, *k):
                    if rn is not None:
                        f(rn, *k)

                def A(f, *k):
                    if ra is not None:
                        f(ra, *k)

                def X(f, *k):
                    if rx is not None:
                        f(rx, *k)

                def F(f, *k):
                    if rf is not None:
                        f(rf, *k)

                A(a_xntl); X(x_norm1); F(f_norm1); X(x_neg); X(x_norm2); N(a_norm1); X(x_kl); A(a_clip)
                F(f_norm2); A(a_gate); A(a_conv); F(f_xntl); A(a_silu_qk); X(x_ql); F(f_top); A(a_rot)
                A(a_silu_v); X(x_soft, 0); A(a_rc); A(a_qbd); X(x_soft, 1); A(a_maskA, 0); F(f_weights)
                X(x_soft, 2); A(a_maskA, 1); F(f_s, 0); X(x_soft, 3); A(a_okn); N(a_norm2); X(x_o, 0)
                X(x_soft, 4); X(x_soft, 5); A(a_sum); F(f_s, 1); X(x_soft, 6); A(a_maskP, 0); A(a_maskP, 1)
                X(x_soft, 7); A(a_oss); X(x_o, 1); A(a_o1); F(f_out); X(x_out); A(a_out)

            dve.memset(mhalf[:], -0.5).then_inc(w_ready, 1)
            dve.memset(ones[:], 1.0).then_inc(w_ready, 1)
            dve.wait_ge(ld_w, W_LANDED)
            for i, (w, w_raw) in enumerate(splits):
                dve.tensor_copy(w[0][:], w_raw[:]).then_inc(w_split, 1)
                dve.wait_ge(w_split, 2 * i + 1)
                tt(w[1][:], w_raw[:], w[0][:].bitcast(F32), ALU.subtract).then_inc(w_split, 1)
            dve.tensor_copy(ident_bf[:], ident[:]).then_inc(w_ready, 1)
            ts(flat(wo), flat(wo_raw), gnorm[:, 0:1], 0.5 * VD ** 0.5, ALU.mult, ALU.mult).then_inc(w_ready, 1)
            dve.wait_ge(z_ready, 3)
            dve.wait_ge(w_ready, 4)
            iterations(dve, body)

        @block.scalar
        def _(act):
            def flat(t):
                return t[:].rearrange("p c d -> p (c d)")

            def a_xnt(r):
                if later(r):
                    act.wait_ge(on.a_g_ps, upto(before(r)))
                act.wait_ge(on.xnT_ps["a"], upto(r))
                act.activation(flat(xnT["a"][0]), A0[:, :], ACT.Copy).then_inc(on.xnT["a"], 1)

            def a_raw_qk(r):
                if later(r):
                    act.wait_ge(on.a_conv, upto(before(r), 3 * 4))
                act.wait_ge(on.a_qk_ps, upto(r))
                act.activation(raw[:, 0:2, TAPS - 1:], A1[:, :].rearrange("p (j t) -> p j t", j=2), ACT.Copy).then_inc(on.a_qk_raw, 1)

            def a_raw_v(r):
                if later(r):
                    act.wait_ge(on.a_conv, upto(before(r), 3 * 4))
                act.wait_ge(on.a_v_ps, upto(r))
                act.activation(raw[:, 2:4, TAPS - 1:], A2[:, :].rearrange("p (j t) -> p j t", j=2), ACT.Copy).then_inc(on.a_v_raw, 1)

            def a_e(r):
                act.wait_ge(on.a_sc, upto(r))
                if later(r):
                    act.wait_ge(on.a_ok_ps, upto(before(r)))
                act.activation(flat(E), flat(sc), ACT.Exp).then_inc(on.a_E, 1)

            def a_gt(r):
                act.wait_ge(on.a_g_ps, upto(r))
                act.activation(flat(gt), A1[:, :], ACT.Tanh, scale=0.5).then_inc(on.a_gt, 1)

            def a_convt(r, j):
                act.wait_ge(on.a_conv, upto(r, 3 * 4, 3 * 4 - 2 + 2 * j))
                if later(r):
                    if j == 0:
                        act.wait_ge(on.a_qk, upto(before(r)))
                    else:
                        act.wait_ge(on.a_v, upto(before(r)))
                act.activation(convt[:, 2 * j:2 * j + 2, :], conv[:, 2 * j:2 * j + 2, :], ACT.Tanh,
                               scale=0.5).then_inc(on.a_convt, 1)

            def a_et(r):
                if later(r):
                    act.wait_ge(on.a_P_ps, upto(before(r), TC))
                act.wait_ge(on.a_ET_ps, upto(r))
                act.activation(flat(ET), A2[:, :], ACT.Copy).then_inc(on.a_ET, 1)

            def a_ktok(r):
                if later(r):
                    act.wait_ge(on.a_o_ps, upto(before(r)))
                act.wait_ge(on.a_ktok_ps, upto(r))
                act.activation(ktok[:], A0[:, 0:P], ACT.Copy).then_inc(on.a_ktok, 1)

            def a_vtok(r):
                if later(r):
                    act.wait_ge(on.a_o_ps, upto(before(r)))
                act.wait_ge(on.a_vtok_ps, upto(r))
                act.activation(flat(vtok), A1[:, :], ACT.Copy).then_inc(on.a_vtok, 1)

            def a_state(r):
                act.wait_ge(on.a_state_ps, upto(r))
                act.activation(state[:], A1[:, :], ACT.Copy).then_inc(on.a_state, 1)

            def a_oke(r):
                act.wait_ge(on.a_oks, upto(r))
                act.activation(flat(oke), flat(oks), ACT.Exp, scale=KD ** -0.5 / 4).then_inc(on.a_oke, 1)

            def a_qnt(r):
                act.wait_ge(on.a_qnT_ps, upto(r))
                src = A0[:, :].rearrange("p (f t) -> p f t", f=2)
                for hh in range(2):
                    s = slice(hh * M, (hh + 1) * M)
                    act.activation(qn_bd[s, :, hh, :], src[s], ACT.Copy).then_inc(on.a_qnT, 1)

            def a_osq(r):
                act.wait_ge(on.a_o_ps, upto(r))
                act.activation(flat(osq), A0[:, :], ACT.Square).then_inc(on.a_osq, 1)

            def a_ot(r):
                act.wait_ge(on.a_oT_ps, upto(r))
                act.activation(flat(oT), A1[:, :], ACT.Copy).then_inc(on.a_oT, 1)

            def x_k(r):
                if later(r):
                    act.wait_ge(on.x_kbd, upto(before(r)))
                act.wait_ge(on.x_k_ps, upto(r))
                act.activation(flat(KT[0]), X1[:, 0:KC * S2], ACT.Copy).then_inc(on.x_k, 1)

            def x_v(r):
                if later(r):
                    act.wait_ge(on.x_av_ps, upto(before(r), NU))
                act.wait_ge(on.x_v_ps, upto(r))
                act.activation(Vx[:, :, 0:HD], X2[0:S2, 0:D].rearrange("p (h e) -> p h e", h=NH), ACT.Copy).then_inc(on.x_v, 1)

            def x_xnt(r):
                act.wait_ge(on.xnT_ps["x"], upto(r))
                act.activation(flat(xnT["x"]), X0[:, :], ACT.Copy).then_inc(on.xnT["x"], 1)

            def x_q(r):
                if later(r):
                    act.wait_ge(on.x_s_ps, upto(before(r), NU))
                act.wait_ge(on.x_q_ps, upto(r))
                act.activation(flat(QT[0]), X0[:, :], ACT.Copy, scale=HD ** -0.5).then_inc(on.x_q, 1)

            def x_prob(r, u):
                act.wait_ge(on.x_sub, upto(r, NU, u + 1))
                if u >= 2:
                    act.wait_ge(on.x_pT_ps, upto(r, NU, u - 1))
                else:
                    if later(r):
                        act.wait_ge(on.x_pT_ps, upto(before(r), NU, NU - 1 + u))
                act.activation(prob[:, u % 2], ssub[:, u % 2], ACT.Exp).then_inc(on.x_prob, 1)

            def x_pt(r, u):
                act.wait_ge(on.x_pT_ps, upto(r, NU, u + 1))
                if u >= 2:
                    act.wait_ge(on.x_av_ps, upto(r, NU, u - 1))
                else:
                    if later(r):
                        act.wait_ge(on.x_av_ps, upto(before(r), NU, NU - 1 + u))
                act.activation(probT[:, u % 2].rearrange("p h t -> p (h t)"), X1[0:S2, :], ACT.Copy).then_inc(on.x_pT, 1)

            def x_ot(r):
                act.wait_ge(on.x_oT_ps, upto(r))
                act.activation(flat(xoT), X1[:, :], ACT.Copy).then_inc(on.x_oT, 1)

            def f_xnt(r):
                act.wait_ge(on.xnT_ps["f"], upto(r))
                act.activation(flat(xnT["f"][0]), F0[:, :], ACT.Copy).then_inc(on.xnT["f"], 1)

            def f_gap(r):
                act.wait_ge(on.f_gap, upto(r))
                act.activation(egap[:], gap[:], ACT.Exp).then_inc(on.f_egap, 1)

            def f_th(r, c):
                act.wait_ge(on.f_u_ps, upto(r, TC, c + 1))
                if c == 1:
                    act.wait_ge(on.f_su, upto(r, TC, 1))
                act.activation(fth[:], (F0 if c == 0 else F1)[:, :], ACT.Tanh, scale=0.5).then_inc(on.f_th, 1)

            def f_st(r, c):
                act.wait_ge(on.f_sT_ps, upto(r, TC, c + 1))
                act.activation(fsT[:, c].rearrange("p i t -> p (i t)"), (F0 if c == 0 else F1)[:, :],
                                    ACT.Copy).then_inc(on.f_sT, 1)

            def body(rn, ra, rx, rf):
                def N(f, *k):
                    if rn is not None:
                        f(rn, *k)

                def A(f, *k):
                    if ra is not None:
                        f(ra, *k)

                def X(f, *k):
                    if rx is not None:
                        f(rx, *k)

                def F(f, *k):
                    if rf is not None:
                        f(rf, *k)

                A(a_xnt); A(a_raw_qk); A(a_raw_v); X(x_k); A(a_gt); X(x_v); A(a_e); X(x_xnt); F(f_xnt); X(x_q)
                A(a_et); A(a_convt, 0); A(a_convt, 1); X(x_prob, 0); X(x_pt, 0); A(a_ktok); F(f_gap); A(a_vtok)
                X(x_prob, 1); X(x_pt, 1); F(f_th, 0); X(x_prob, 2); A(a_state); X(x_pt, 2); X(x_prob, 3)
                X(x_pt, 3); A(a_oke); X(x_prob, 4); F(f_st, 0); X(x_pt, 4); F(f_th, 1); X(x_prob, 5); A(a_qnt)
                X(x_pt, 5); X(x_prob, 6); X(x_pt, 6); X(x_prob, 7); A(a_osq); X(x_pt, 7); F(f_st, 1); X(x_ot)
                A(a_ot)

            iterations(act, body)

        @block.gpsimd
        def _(pool):
            def heads(t):
                return t[:].rearrange("p c (h m) -> p (c h) m", m=M)

            def spread(small, n):
                return small.rearrange("p (g o) -> p g o", o=1).broadcast_to([P, small.shape[1], n])

            def rstd(s, r):
                pool.wait_ge(on.ve[s], upto(r))
                if later(r):
                    pool.wait_ge(on.xn[s], upto(before(r)))
                pool.tensor_tensor(ln_rstd[s][:], ln_ve[s][:], mhalf[:, 0:TC], ALU.pow).then_inc(on.rstd[s], 1)

            def a_rstd(r):
                rstd("a", r)

            def x_rstd(r):
                rstd("x", r)

            def f_rstd(r):
                rstd("f", r)

            def a_tap0(r):
                pool.wait_ge(on.a_v_raw, upto(r))
                pool.wait_ge(on.a_qk_raw, upto(r))
                if later(r):
                    pool.wait_ge(on.a_v, upto(before(r)))
                hold(pool, pool_scrap)
                for j in range(4):
                    ins = pool.tensor_scalar(conv[:, j, :], raw[:, j, 0:T], cw[:, j, 0:1], 1.0, ALU.mult, ALU.mult)
                ins.then_inc(on.a_tap0, 1)

            def a_cos(r):
                pool.wait_ge(on.a_qk, upto(r))
                pool.tensor_tensor(qkcos[:], qkv[:, 0:2, :],
                                        cosT[:].rearrange("p (o t) -> p o t", o=1).broadcast_to([P, 2, T]),
                                        ALU.mult).then_inc(on.a_cos, 1)

            def a_sin(r):
                pool.wait_ge(on.a_rot, upto(r))
                pool.tensor_tensor(qksin[:], rot[:],
                                   sinT[:].rearrange("p (o t) -> p o t", o=1).broadcast_to([P, 2, T]),
                                   ALU.mult).then_inc(on.a_sin, 1)

            def a_kr(r):
                pool.wait_ge(on.a_cos, upto(r))
                pool.wait_ge(on.a_sin, upto(r))
                pool.tensor_tensor(qkr[:], qkcos[:], qksin[:], ALU.add).then_inc(on.a_kr, 1)

            def a_oks(r):
                pool.wait_ge(on.a_max, upto(r))
                pool.tensor_tensor(heads(oks), heads(okn), spread(okmax[:], M), ALU.subtract).then_inc(on.a_oks, 1)

            def a_qn(r):
                pool.wait_ge(on.a_oke, upto(r))
                pool.tensor_tensor(qn[:], oke[:], rC[:], ALU.mult).then_inc(on.a_qn, 1)

            def a_orinv(r):
                pool.wait_ge(on.a_ove, upto(r))
                pool.tensor_tensor(orinv[:], ove[:], mhalf[:], ALU.pow).then_inc(on.a_orinv, 1)

            def a_o2(r):
                pool.wait_ge(on.a_o1, upto(r))
                pool.wait_ge(on.a_gate, upto(r))
                pool.tensor_tensor(o2[:], o1[:], gate[:], ALU.mult).then_inc(on.a_o2, 1)

            def x_kbd(r):
                pool.wait_ge(on.x_k, upto(r))
                if later(r):
                    pool.wait_ge(on.x_s_ps, upto(before(r), NU))
                pool.wait_ge(on.x_kl, upto(r))
                for i in range(2):
                    for f in range(KC):
                        ins = pool.tensor_tensor(KT_bd[i][:, f],
                                                 KT[i][:, f:f + 1, :].bitcast(F32).broadcast_to([P, HB, S2]),
                                                 spread(headmask[:], S2), ALU.mult)
                ins.then_inc(on.x_kbd, 1)

            def x_x1b(r):
                pool.wait_ge(on.a_x1, upto(r))
                if later(r):
                    pool.wait_ge(on.x_x2, upto(before(r)))
                pool.tensor_tensor(x1b[:], x1[r.parity][:],
                                        xbias[:].rearrange("p (o d) -> p o d", o=1).broadcast_to([P, TC, D]),
                                        ALU.add).then_inc(on.x_x1b, 1)

            def f_sw(r, c):
                pool.wait_ge(on.f_s, upto(r, TC, c + 1))
                pool.wait_ge(on.f_wt, upto(r))
                pool.tensor_tensor(fsw[:, c, :].rearrange("p (e q) -> p e q", e=NE),
                                        fs[:, c, :].rearrange("p (e q) -> p e q", e=NE),
                                        spread(wt[:, c, :], R), ALU.mult).then_inc(on.f_sw, 1)

            def body(rn, ra, rx, rf):
                def N(f, *k):
                    if rn is not None:
                        f(rn, *k)

                def A(f, *k):
                    if ra is not None:
                        f(ra, *k)

                def X(f, *k):
                    if rx is not None:
                        f(rx, *k)

                def F(f, *k):
                    if rf is not None:
                        f(rf, *k)

                X(x_rstd); F(f_rstd); A(a_tap0); X(x_kbd); N(a_rstd); A(a_cos); A(a_sin); A(a_kr); F(f_sw, 0)
                X(x_x1b); A(a_oks); A(a_qn); F(f_sw, 1); A(a_orinv); A(a_o2)

            pool.memset(raw[:], 0.0)
            pool.memset(Vx[:], 1.0).then_inc(z_ready, 1)
            pool.memset(q_bd[:], 0.0).then_inc(z_ready, 1)
            pool.memset(qn_bd[:], 0.0).then_inc(z_ready, 1)
            pool.wait_ge(ld_w, W_LANDED)
            pool.wait_ge(w_ready, 4)
            pool.wait_ge(z_ready, 3)
            iterations(pool, body)


def constants():
    f32 = np.float32
    freq = (1.0 / 10000.0 ** (np.arange(0, KD, 2, dtype=f32) / f32(KD))).astype(f32)
    angle = (np.arange(T, dtype=f32)[:, None] * freq[None, :]).astype(f32)
    lane = np.arange(P) % KD
    cos = np.cos(angle)[:, lane % (KD // 2)].T
    sin = np.sin(angle)[:, lane % (KD // 2)].T * np.where(lane < KD // 2, -1.0, 1.0)[:, None]
    return {
        "ident": np.eye(P, dtype=f32),
        "tri": np.triu(np.ones((P, P), f32)),
        "cosT": np.ascontiguousarray(cos, f32),
        "sinT": np.ascontiguousarray(sin, f32),
        "headmask": (np.arange(P)[:, None] // HD == np.arange(HB)[None, :]).astype(f32),
        "iota8": np.tile(np.arange(NE, dtype=f32), (P, 1)),
    }


def kernel(**inputs):
    import concourse.bacc as bacc
    from concourse.bass_utils import run_bass_kernel_spmd

    def t(name):
        return np.ascontiguousarray(np.transpose(np.asarray(inputs[name])))

    arrays = {
        "x": inputs["x"],
        "ctxT": np.transpose(np.asarray(inputs["ctx_1024"]), (0, 2, 1)),
        "mask": inputs["mask_Bx1xSxS2_bk0"],
        "Wq": inputs["L0_attn_Wq"], "Wk": inputs["L0_attn_Wk"], "Wv": inputs["L0_attn_Wv"],
        "Ws": inputs["L0_attn_Ws"], "Wg": inputs["L0_attn_Wg"], "Wo": inputs["L0_attn_Wo"],
        "qconv": inputs["L0_attn_qconv_w"], "kconv": inputs["L0_attn_kconv_w"],
        "vconv": inputs["L0_attn_vconv_w"], "gnorm": inputs["L0_attn_gnorm_w"],
        "xWqT": t("L0_xattn_W_q"), "xWkT": t("L0_xattn_W_k"), "xWvT": t("L0_xattn_W_v"),
        "xWpT": t("L0_xattn_W_proj"),
        "xbias": np.broadcast_to(np.asarray(inputs["L0_xattn_b_proj"])[None, :], (P, D)),
        "gate_w": inputs["L0_ffn_gate_w"], "fWu": inputs["L0_ffn_Wu"], "fWv": inputs["L0_ffn_Wv"],
        "fWo": inputs["L0_ffn_Wo"],
    } | constants()
    arrays = {f"in_{n}": np.ascontiguousarray(v) for n, v in arrays.items()}

    nc = bacc.Bacc("TRN2", target_bir_lowering=False, num_devices=1)
    aps = {n[3:]: nc.dram_tensor(n, v.shape, mybir.dt.from_np(v.dtype), kind="ExternalInput").ap()
           for n, v in arrays.items()}
    aps["out"] = nc.dram_tensor("out_0", (B, T, D), F32, kind="ExternalOutput").ap()
    build(nc, aps)
    return run_bass_kernel_spmd(nc, [arrays], core_ids=[0]).results[0]["out_0"]
```

```python
from collections import namedtuple
from contextlib import ExitStack

import numpy as np

import concourse.bass as bass
from concourse import mybir

F32 = mybir.dt.float32
F32R = mybir.dt.float32r
BF16 = mybir.dt.bfloat16
U8 = mybir.dt.uint8
U32 = mybir.dt.uint32
ALU = mybir.AluOpType
ACT = mybir.ActivationFunctionType
AX = mybir.AxisListType

P = 128
B, T, D = 32, 256, 256
TC = T // P
KC = D // P
H, M, KD, VD = 4, 64, 32, 64
TAPS = 4
S2, NH, HD = 77, 16, 16
UH = 4
QU = NH // UH
NU = TC * QU
HB = P // HD
NE, R, TOPK = 8, 64, 2
RC = NE * R // P
EPS = 1e-5
CLIP = 32.0
MASKED = 2.0 ** 100

Row = namedtuple("Row", "half parity")


STEPS = (
    "a_qk_ps a_v_ps a_s_ps a_g_ps a_qk_raw a_v_raw a_tap0 a_conv a_convt a_qk a_v a_rot a_cos "
    "a_sin a_kr a_qbd a_sc a_E a_C_ps a_rC a_ET_ps a_ET a_ktok_ps a_vtok_ps a_ktok a_vtok a_gt "
    "a_gate a_A_ps a_A a_state_ps a_state a_ok_ps a_okn a_max a_oks a_oke a_sum a_ssq a_qn "
    "a_qnT_ps a_qnT a_P_ps a_P a_o_ps a_osq a_oss a_ove a_orinv a_o1 a_o2 a_oT_ps a_oT a_wo_ps "
    "a_x1 x_k_ps x_v_ps x_q_ps x_k x_kl x_kbd x_v x_q x_ql a_xnTl x_xnTl f_xnTl a_Ehi a_Elo a_oTl "
    "x_oTl f_sTl x_neg x_s_ps x_max x_prob x_pT_ps x_pT x_av_ps x_rs x_o x_oT_ps x_oT x_x1b "
    "x_proj_ps x_x2 f_gate_ps f_lgT f_lg_ps f_logit f_top f_topi f_topf f_gap f_egap f_gden f_gw1 "
    "f_gw2 f_wt12 f_wt f_u_ps f_v_ps f_th f_su f_s f_sw f_sT_ps f_sT f_y_ps f_y"
)
NORM_STEPS = "stats mv ve rstd xn xnT_ps xnT"
Signals = namedtuple("Signals", STEPS + " " + NORM_STEPS)


def build(nc, a):
    ctx = ExitStack()
    with ctx:
        def sb(name, shape, dt=F32):
            return ctx.enter_context(nc.sbuf_tensor(name, shape, dt))

        def halves(name, shape):
            return sb(f"{name}_hi", shape, F32R), sb(f"{name}_lo", shape, F32R)

        def sem(name):
            return ctx.enter_context(nc.semaphore(name))

        ident = sb("ident", [P, P])
        ident_bf = sb("ident_bf", [P, P], BF16)
        tri_r = sb("tri", [P, P], F32R)
        tri = tri_r[:].bitcast(F32)
        ones = sb("ones", [P, P])
        ones_r = sb("ones_r", [P, P], F32R)
        cosT = sb("cosT", [P, T])
        sinT = sb("sinT", [P, T])
        headmask = sb("headmask", [P, HB])
        groupmask = sb("groupmask", [P, UH])
        blockmask = sb("blockmask", [P, 2 * H])
        iota8 = sb("iota8", [P, NE])
        mhalf = sb("mhalf", [P, 2 * H])
        dve_scrap = sb("dve_scrap", [P, 1])
        pool_scrap = sb("pool_scrap", [P, 1])
        wqk = halves("wqk", [P, KC, 2, H * KD])
        wv = halves("wv", [P, KC, D])
        ws = halves("ws", [P, KC, D])
        wg = halves("wg", [P, KC, D])
        wo = halves("wo", [P, KC, D])
        gnorm = sb("gnorm", [P, 1])
        cw = sb("cw", [P, 4, TAPS])
        xwq = halves("xwq", [P, KC, D])
        xwk = sb("xwk", [P, KC, D])
        xwv = sb("xwv", [P, KC, D])
        xwp = halves("xwp", [P, KC, D])
        xbias = sb("xbias", [P, D])
        fgate = halves("fgate", [P, KC, NE])
        fwu = halves("fwu", [P, KC, NE * R])
        fwv = halves("fwv", [P, KC, NE * R])
        fwo = halves("fwo", [P, RC, D])

        x0 = [sb(f"x0_{i}", [P, TC, D]) for i in range(2)]
        x1 = [sb(f"x1_{i}", [P, TC, D]) for i in range(2)]
        x2 = [sb(f"x2_{i}", [P, TC, D]) for i in range(2)]
        ctxT = [sb(f"ctxT_{i}", [P, KC, S2]) for i in range(2)]
        keep = [sb(f"keep_{i}", [P, TC, S2], U8) for i in range(2)]

        ln_stats = {s: sb(f"{s}_stats", [P, TC, 6]) for s in "axf"}
        ln_mv = {s: sb(f"{s}_mv", [P, TC, 2]) for s in "axf"}
        ln_ve = {s: sb(f"{s}_ve", [P, TC]) for s in "axf"}
        ln_rstd = {s: sb(f"{s}_rstd", [P, TC]) for s in "axf"}
        xn = {s: sb(f"{s}_xn", [P, TC, D]) for s in "axf"}
        xnT = {s: halves(f"{s}_xnT", [P, KC, T]) for s in "axf"}

        raw = sb("a_raw", [P, 4, TAPS - 1 + T])
        conv = sb("a_conv", [P, 4, T])
        qkv = sb("a_qkv", [P, 4, T])
        rot = conv[:, 0:2, :]
        qkr = [sb(f"a_qkr_{i}", [P, 2, T]) for i in range(2)]
        q_bd = [sb(f"a_q_bd_{i}", [P, H, T]) for i in range(2)]
        ktok = sb("a_ktok", [P, P])
        vtok = [sb(f"a_vtok_{i}", [P, TC, D]) for i in range(2)]
        gate = [sb(f"a_gate_{i}", [P, TC, D]) for i in range(2)]
        E = [sb(f"a_E_{i}", [P, TC, D]) for i in range(2)]
        E_halves = halves("a_Er", [P, TC, D])
        ET = [sb(f"a_ET_{i}", [P, KC, T]) for i in range(2)]
        rC = [sb(f"a_rC_{i}", [P, TC, D]) for i in range(2)]
        AT = sb("a_AT", [P, TC, H, P])
        PT = AT
        state = sb("a_state", [P, 2 * D])
        okn = sb("a_okn", [P, TC, D])
        qn = sb("a_qn", [P, TC, D])
        okmax = sb("a_okmax", [P, TC * H])
        ssum = sb("a_ssum", [P, TC * H])
        ssq = sb("a_ssq", [P, TC * H])
        qn_bd = sb("a_qn_bd", [P, 2, 2, T])
        qn_last = sb("a_qn_last", [P, 2, P])
        osq = okn
        oss = sb("a_oss", [P, TC * H])
        ove = sb("a_ove", [P, TC * H])
        orinv = sb("a_orinv", [P, TC * H])
        o1 = sb("a_o1", [P, TC, D])
        oT = halves("a_oT", [P, KC, T])

        at_flat = AT[:].rearrange("p c h t -> p (c h t)")
        wqk_raw = at_flat[:, 0:KC * 2 * P].rearrange("p (k j n) -> p k j n", k=KC, j=2)
        wv_raw = at_flat[:, KC * D:2 * KC * D].rearrange("p (k n) -> p k n", k=KC)
        ws_raw, wg_raw = okn[:], qn[:]
        tri_raw = state[:, 0:P]

        negmask = sb("x_negmask", [P, TC, S2], BF16)
        Q_stack = sb("x_Q_stack", [P, QU, T], F32R)
        K_stack = sb("x_K_stack", [P, QU, S2], F32R)
        KT_lo = sb("x_KT_lo", [P, KC, S2], F32R)
        K_bd = sb("x_K_bd", [P, QU, UH, S2], F32R)
        KT_lo_bd = sb("x_KT_lo_bd", [P, KC, HB, S2], F32R)
        Vx = sb("x_Vx", [S2, NH, HD + 1])
        nmax = sb("x_nmax", [P, 2, UH])
        prob = sb("x_prob", [P, 2, UH, S2])
        probT = sb("x_probT", [S2, 2, UH, P])
        xrs = sb("x_rs", [P, TC, NH])
        xo = sb("x_o", [P, TC, D])
        xoT = halves("x_oT", [P, KC, T])

        logit = sb("f_logit", [P, TC, NE])
        top = sb("f_top", [P, TC, 8])
        topi = sb("f_topi", [P, TC, 8], U32)
        topf = sb("f_topf", [P, TC, 8])
        gap = sb("f_gap", [P, TC])
        egap = sb("f_egap", [P, TC])
        gden = sb("f_gden", [P, TC])
        gw = sb("f_gw", [P, 2, TC])
        wt1 = sb("f_wt1", [P, TC, NE])
        wt2 = sb("f_wt2", [P, TC, NE])
        wt = sb("f_wt", [P, TC, NE])
        fth = sb("f_th", [P, NE * R])
        fs = sb("f_s", [P, 2, NE * R])
        lgT = fth[0:NE, 0:T]
        fsT = halves("f_sT", [P, 2, RC, P])

        wo_raw, wo_normed = o1[:], xo[:]
        xwq_raw, xwp_raw = x2[0][:], x2[1][:]
        fgate_raw = topf
        fwu_raw = [fs[:, 0, :], fs[:, 1, :]]
        fwv_raw = [t[1][:].rearrange("p c d -> p (c d)") for t in (E, ET)]
        fwo_raw = [t[1][:] for t in (rC, vtok)]

        bank = [ctx.enter_context(nc.psum_tensor(f"bank{i}", [P, 512], F32)) for i in range(8)]
        E0, A0, A1, X0, X1, X2, F0, F1 = bank

        ld_w = sem("ld_w")
        ld_v = sem("ld_v")
        ld_x = [sem(f"ld_x{i}") for i in range(2)]
        ld_c = [sem(f"ld_c{i}") for i in range(2)]
        st_y = [sem(f"st_y{i}") for i in range(2)]
        w_ready = sem("w_ready")
        w_hi = sem("w_hi")
        w_lo = sem("w_lo")
        z_ready = sem("z_ready")
        on = Signals(*[sem(n) for n in STEPS.split()],
                     *[{s: sem(f"{s}_{n}") for s in "axf"} for n in NORM_STEPS.split()])

        def upto(row, n=1, k=None):
            return row.half * (2 * n) + (n * row.parity + (n if k is None else k))

        def later(row):
            return row.parity == 1 or not (isinstance(row.half, int) and row.half == 0)

        def before(row):
            return Row(row.half, 0) if row.parity == 1 else Row(row.half - 1, 1)

        def two_before(row):
            return Row(row.half - 1, row.parity)

        def second(row):
            return not (isinstance(row.half, int) and row.half == 0)

        def loaded(row, n=1):
            return row.half * (16 * n) + 16 * n

        def hold(eng, scrap):
            eng.tensor_tensor(scrap[:], mhalf[:, 0:1], mhalf[:, 0:1], ALU.mult)

        def iterations(body, others, eng):
            body(Row(0, 0), None, None, None)
            others()
            body(Row(0, 1), Row(0, 0), None, None)
            body(Row(1, 0), Row(0, 1), Row(0, 0), None)
            body(Row(1, 1), Row(1, 0), Row(0, 1), Row(0, 0))
            body(Row(2, 0), Row(1, 1), Row(1, 0), Row(0, 1))
            last = B // 2
            with eng.Fori(2, last - 1) as half:
                body(Row(half, 1), Row(half, 0), Row(half - 1, 1), Row(half - 1, 0))
                body(Row(half + 1, 0), Row(half, 1), Row(half, 0), Row(half - 1, 1))
            body(Row(last - 1, 1), Row(last - 1, 0), Row(last - 2, 1), Row(last - 2, 0))
            body(None, Row(last - 1, 1), Row(last - 1, 0), Row(last - 2, 1))
            body(None, None, Row(last - 1, 1), Row(last - 1, 0))
            body(None, None, None, Row(last - 1, 1))

        block = ctx.enter_context(nc.Block())

        def k_major(ap):
            return ap.rearrange("(k p) n -> p k n", p=P)

        weights = [
            (ident[:], a["ident"]),
            (wqk_raw[:, :, 0, :], k_major(a["Wq"])), (wqk_raw[:, :, 1, :], k_major(a["Wk"])),
            (wv_raw, k_major(a["Wv"])), (ws_raw, k_major(a["Ws"])), (wg_raw, k_major(a["Wg"])),
            (cw[:, 0, :], a["qconv"].rearrange("c o k -> c (o k)")),
            (cw[:, 1, :], a["kconv"].rearrange("c o k -> c (o k)")),
            (cw[:, 2:4, :], a["vconv"].rearrange("(j p) o k -> p j (o k)", p=P)),
            (tri_raw, a["tri"]), (cosT[:], a["cosT"]), (sinT[:], a["sinT"]),
        ]
        other_weights = [
            (headmask[:], a["headmask"]), (groupmask[:], a["groupmask"]),
            (blockmask[:], a["blockmask"]), (iota8[:], a["iota8"]), (wo_raw, k_major(a["Wo"])),
            (gnorm[0:VD, :], a["gnorm"].rearrange("(v o) -> v o", o=1)),
            (gnorm[VD:2 * VD, :], a["gnorm"].rearrange("(v o) -> v o", o=1)),
            (xwq_raw, k_major(a["xWqT"])), (xwk[:], k_major(a["xWkT"])), (xwv[:], k_major(a["xWvT"])),
            (xwp_raw, k_major(a["xWpT"])), (xbias[:], a["xbias"]), (fgate_raw[:], k_major(a["gate_w"])),
        ] + [
            (fwo_raw[i], a["fWo"].rearrange("e r n -> (e r) n").rearrange("(c p) n -> p c n", p=P)[:, 2 * i:2 * i + 2])
            for i in range(2)
        ] + [
            (w[k].rearrange("p (e r) -> p e r", e=NE), a[n][:, k * P:(k + 1) * P, :].rearrange("e p r -> p e r"))
            for w, n in ((fwu_raw, "fWu"), (fwv_raw, "fWv")) for k in range(KC)
        ]
        def full(t):
            return t[:]

        def part(w, sl):
            return w[0][:, sl], w[1][:, sl]

        splits = [(wqk, wqk_raw), (wv, wv_raw), (ws, ws_raw), (wg, wg_raw)]
        other_splits = [(wo, wo_normed), (xwq, xwq_raw), (xwp, xwp_raw), (fgate, fgate_raw[:])] + [
            (part(w, k), w_raw[k]) for w, w_raw in ((fwu, fwu_raw), (fwv, fwv_raw)) for k in range(KC)
        ] + [(part(fwo, slice(2 * i, 2 * i + 2)), fwo_raw[i]) for i in range(2)]
        ALL_SPLIT = len(splits) + len(other_splits)
        W_LANDED = 16 * len(weights)
        V_LANDED = 16 * len(other_weights)

        def row_of(ap, row):
            return ap[bass.ds(row.half * 2 + row.parity, 1)]

        @block.sync
        def _(sp):
            def load_x(row):
                sp.dma_start(x0[row.parity][:], row_of(a["x"], row).rearrange("o (c p) d -> p (o c) d", p=P)
                             ).then_inc(ld_x[row.parity], 16)

            def load_context(row):
                c, m = ctxT[row.parity], keep[row.parity]
                sp.dma_start(c[:], row_of(a["ctxT"], row).rearrange("o (k p) s -> p (o k) s", p=P)
                             ).then_inc(ld_c[row.parity], 16)
                sp.dma_start(m[:], row_of(a["mask"], row).rearrange("o u (c p) s -> p (o u c) s", p=P)
                             ).then_inc(ld_c[row.parity], 16)

            def body(ra, rx, rf):
                if ra is not None:
                    if not (isinstance(ra.half, int) and ra.half == 0 and ra.parity == 0):
                        if later(ra):
                            sp.wait_ge(on.a_x1, upto(before(ra)))
                        load_x(Row(ra.half, 1) if ra.parity == 0 else Row(ra.half + 1, 0))
                    if rf is not None:
                        sp.wait_ge(on.x_neg, upto(rf))
                        sp.wait_ge(on.x_v_ps, upto(rf))
                    load_context(ra)
                if rf is not None:
                    sp.wait_ge(on.f_y, upto(rf))
                    sp.dma_start(row_of(a["out"], rf).rearrange("o (c p) d -> p (o c) d", p=P),
                                 x2[rf.parity][:]).then_inc(st_y[rf.parity], 16)

            load_x(Row(0, 0))
            for dst, src in weights:
                sp.dma_start(dst, src).then_inc(ld_w, 16)
            for dst, src in other_weights:
                sp.dma_start(dst, src).then_inc(ld_v, 16)
            load_x(Row(0, 1))
            body(Row(0, 0), None, None)
            body(Row(0, 1), Row(0, 0), None)
            body(Row(1, 0), Row(0, 1), Row(0, 0))
            body(Row(1, 1), Row(1, 0), Row(0, 1))
            with sp.Fori(2, B // 2 - 1) as half:
                body(Row(half, 0), Row(half - 1, 1), Row(half - 1, 0))
                body(Row(half, 1), Row(half, 0), Row(half - 1, 1))
            last = B // 2
            body(Row(last - 1, 0), Row(last - 2, 1), Row(last - 2, 0))
            sp.wait_ge(on.x_neg, upto(Row(last - 2, 1)))
            sp.wait_ge(on.x_v_ps, upto(Row(last - 2, 1)))
            load_context(Row(last - 1, 1))
            for rf in (Row(last - 2, 1), Row(last - 1, 0), Row(last - 1, 1)):
                sp.wait_ge(on.f_y, upto(rf))
                sp.dma_start(row_of(a["out"], rf).rearrange("o (c p) d -> p (o c) d", p=P),
                             x2[rf.parity][:]).then_inc(st_y[rf.parity], 16)
            for i in range(2):
                sp.wait_ge(st_y[i], 16 * (B // 2))

        @block.tensor
        def _(pe):
            def mm(out, lhsT, rhs, start=True, stop=True):
                return pe.matmul(out, lhsT, rhs, start=start, stop=stop, skip_group_check=True)

            def turn(dst, src):
                for k in range(KC):
                    for c in range(TC):
                        ins = pe.transpose(dst[:, k * T + c * P:k * T + (c + 1) * P],
                                           src[:, c, k * P:(k + 1) * P], ident[:])
                return ins

            def mm_halves(dst, pairs):
                n = len(pairs)
                for i, (lhsT, rhs) in enumerate(pairs):
                    mm(dst, lhsT(0), rhs(0), start=(i == 0), stop=False)
                    mm(dst, lhsT(0), rhs(1), start=False, stop=False)
                    ins = mm(dst, lhsT(1), rhs(0), start=False, stop=(i == n - 1))
                return ins

            def features(dst, w, act):
                for k in range(KC):
                    ins = mm(dst, w(k), act(k), start=(k == 0), stop=(k == KC - 1))
                return ins

            def a_turn(r):
                if later(r):
                    pe.wait_ge(on.a_vtok, upto(before(r)))
                pe.wait_ge(on.xn["a"], upto(r))
                turn(E0, xn["a"]).then_inc(on.xnT_ps["a"], 1)

            def a_qk(r):
                pe.wait_ge(on.xnT["a"], upto(r))
                pe.wait_ge(on.a_xnTl, upto(r))
                for j in range(2):
                    ins = mm_halves(E0[:, j * T:(j + 1) * T], [
                        (lambda i, k=k: wqk[i][:, k, j, :], lambda i, k=k: xnT["a"][i][:, k, :]) for k in range(KC)])
                ins.then_inc(on.a_qk_ps, 1)

            def a_v(r):
                pe.wait_ge(on.a_qk_raw, upto(r))
                for j in range(2):
                    ins = mm_halves(E0[:, j * T:(j + 1) * T], [
                        (lambda i, k=k: wv[i][:, k, j * P:(j + 1) * P], lambda i, k=k: xnT["a"][i][:, k, :])
                        for k in range(KC)])
                ins.then_inc(on.a_v_ps, 1)

            def tokens_halves(dst, act, w):
                for c in range(TC):
                    ins = mm_halves(dst[:, c * D:(c + 1) * D], [
                        (lambda i, k=k: act[i][:, k, c * P:(c + 1) * P], lambda i, k=k: w[i][:, k, :])
                        for k in range(KC)])
                return ins

            def a_s(r):
                pe.wait_ge(on.a_v_raw, upto(r))
                tokens_halves(E0, xnT["a"], ws).then_inc(on.a_s_ps, 1)

            def a_g(r):
                pe.wait_ge(on.a_sc, upto(r))
                tokens_halves(E0, xnT["a"], wg).then_inc(on.a_g_ps, 1)

            def a_c(r):
                pe.wait_ge(on.a_gate, upto(r))
                pe.wait_ge(on.a_Ehi, upto(r))
                pe.wait_ge(on.a_Elo, upto(r))
                for i in range(2):
                    mm(E0[:, 0:D], tri_r[:], E_halves[i][:, 0, :], start=(i == 0), stop=(i == 1))
                for i in range(2):
                    mm(E0[:, D:2 * D], ones_r[:], E_halves[i][:, 0, :], start=(i == 0), stop=False)
                    ins = mm(E0[:, D:2 * D], tri_r[:], E_halves[i][:, 1, :], start=False, stop=(i == 1))
                ins.then_inc(on.a_C_ps, 1)

            def a_et(r):
                pe.wait_ge(on.a_rC, upto(r))
                pe.wait_ge(on.a_E, upto(r))
                turn(E0, E[r.parity]).then_inc(on.a_ET_ps, 1)

            def a_vtok(r):
                pe.wait_ge(on.a_v, upto(r))
                pe.wait_ge(on.a_ET, upto(r))
                for c in range(TC):
                    for j in range(2):
                        ins = pe.transpose(E0[:, c * D + j * P:c * D + (j + 1) * P],
                                           qkv[:, 2 + j, c * P:(c + 1) * P], ident[:])
                ins.then_inc(on.a_vtok_ps, 1)

            def a_ktok(r):
                pe.wait_ge(on.a_kr, upto(r))
                if later(r):
                    pe.wait_ge(on.a_x1, upto(before(r)))
                pe.transpose(A1[:, 0:P], qkr[r.parity][:, 1, 0:P], ident[:]).then_inc(on.a_ktok_ps, 1)

            def a_A(r, c):
                if c == 0:
                    pe.wait_ge(on.a_qbd, upto(r))
                    if later(r):
                        pe.wait_ge(on.a_oT, upto(before(r)))
                        pe.wait_ge(on.a_oTl, upto(before(r)))
                else:
                    pe.wait_ge(on.a_ktok, upto(r))
                mm((A0 if c == 0 else A1)[:, :], qkr[r.parity][:, 1, c * P:(c + 1) * P],
                   q_bd[r.parity][:, :, c * P:(c + 1) * P]).then_inc(on.a_A_ps, 1)

            def a_state(r):
                e, v = E[r.parity], vtok[r.parity]
                pe.wait_ge(on.a_ktok, upto(r))
                pe.wait_ge(on.a_vtok, upto(r))
                pe.wait_ge(on.a_A, upto(r, TC, 1))
                mm(A0[:, 0:D], ktok[:], e[:, 0, :])
                for f in range(2):
                    ins = mm(A0[:, D + f * P:D + (f + 1) * P], e[:, 0, f * P:(f + 1) * P],
                             v[:, 0, f * P:(f + 1) * P])
                ins.then_inc(on.a_state_ps, 1)

            def a_ok(r):
                e = E[r.parity]
                pe.wait_ge(on.a_A, upto(r, TC))
                pe.wait_ge(on.a_state, upto(r))
                for h in range(H):
                    mm(A1[:, h * M:(h + 1) * M], AT[:, 0, h, :], e[:, 0, h * M:(h + 1) * M])
                mm(A1[:, D:2 * D], qkr[r.parity][:, 0, P:2 * P], state[:, 0:D], stop=False)
                for h in range(H):
                    out = A1[:, D + h * M:D + (h + 1) * M]
                    ins = mm(out, AT[:, 1, h, :], e[:, 1, h * M:(h + 1) * M], start=False)
                ins.then_inc(on.a_ok_ps, 1)

            def a_qt(r):
                pe.wait_ge(on.a_qn, upto(r))
                turn(A0, qn).then_inc(on.a_qnT_ps, 1)

            def a_P(r, c):
                pe.wait_ge(on.a_qnT, upto(r, 3))
                dst = A1 if c == 0 else A0
                for f in range(2):
                    ins = mm(dst[:, f * 2 * P:(f + 1) * 2 * P], ET[r.parity][:, f, c * P:(c + 1) * P],
                             qn_bd[:, f, :, c * P:(c + 1) * P])
                ins.then_inc(on.a_P_ps, 1)

            def a_o(r):
                v = vtok[r.parity]
                pe.wait_ge(on.a_P, upto(r, TC))
                for h in range(H):
                    mm(A1[:, h * VD:(h + 1) * VD], PT[:, 0, h, :], v[:, 0, h * VD:(h + 1) * VD])
                for h in range(H):
                    f = h // 2
                    if h % 2 == 0:
                        mm(A1[:, D + f * P:D + (f + 1) * P], qn_last[:, f, :], state[:, D + f * P:D + (f + 1) * P],
                           stop=False)
                    out = A1[:, D + h * VD:D + (h + 1) * VD]
                    ins = mm(out, PT[:, 1, h, :], v[:, 1, h * VD:(h + 1) * VD], start=False)
                ins.then_inc(on.a_o_ps, 1)

            def a_ot(r):
                pe.wait_ge(on.a_o2, upto(r))
                turn(A0, o1).then_inc(on.a_oT_ps, 1)

            def a_wo(r):
                pe.wait_ge(on.a_oT, upto(r))
                pe.wait_ge(on.a_osq, upto(r))
                pe.wait_ge(on.a_oTl, upto(r))
                tokens_halves(A1, oT, wo).then_inc(on.a_wo_ps, 1)

            def x_turn(r):
                if later(r):
                    pe.wait_ge(on.x_x2, upto(before(r)))
                pe.wait_ge(on.xn["x"], upto(r))
                turn(X0, xn["x"]).then_inc(on.xnT_ps["x"], 1)

            def x_k(r):
                pe.wait_ge(ld_c[r.parity], loaded(r, 2))
                if later(r):
                    pe.wait_ge(on.x_oT, upto(before(r)))
                    pe.wait_ge(on.x_oTl, upto(before(r)))
                c = ctxT[r.parity]
                for j in range(2):
                    ins = features(X1[:, j * S2:(j + 1) * S2], lambda k: xwk[:, k, j * P:(j + 1) * P],
                                   lambda k: c[:, k, :])
                ins.then_inc(on.x_k_ps, 1)

            def x_v(r):
                pe.wait_ge(ld_c[r.parity], loaded(r, 2))
                c = ctxT[r.parity]
                if later(r):
                    pe.wait_ge(on.x_o, upto(before(r), TC))
                for k in range(KC):
                    ins = mm(X2[0:S2, 0:D], c[:, k, :], xwv[:, k, :], start=(k == 0), stop=(k == KC - 1))
                ins.then_inc(on.x_v_ps, 1)

            def x_q(r):
                pe.wait_ge(on.xnT["x"], upto(r))
                pe.wait_ge(on.x_xnTl, upto(r))
                for j in range(2):
                    ins = mm_halves(X0[:, j * T:(j + 1) * T], [
                        (lambda i, k=k: xwq[i][:, k, j * P:(j + 1) * P], lambda i, k=k: xnT["x"][i][:, k, :])
                        for k in range(KC)])
                ins.then_inc(on.x_q_ps, 1)

            def x_s(r, u):
                c, q = divmod(u, QU)
                f, hh = divmod(q * UH, HB)
                if u == 0:
                    pe.wait_ge(on.x_q, upto(r))
                    pe.wait_ge(on.x_ql, upto(r))
                    pe.wait_ge(on.x_kbd, upto(r))
                    pe.wait_ge(on.x_neg, upto(r))
                else:
                    pe.wait_ge(on.x_prob, upto(r, NU, u))
                out = X0[:, 0:UH * S2]
                mm(out, Q_stack[:, q, c * P:(c + 1) * P], K_bd[:, q], stop=False)
                mm(out, Q_stack[:, q, c * P:(c + 1) * P], KT_lo_bd[:, f, hh:hh + UH, :], start=False, stop=False)
                mm(out, ident_bf[:], negmask[:, c:c + 1, :].broadcast_to([P, UH, S2]), start=False
                   ).then_inc(on.x_s_ps, 1)

            def x_pt(r, u):
                pe.wait_ge(on.x_prob, upto(r, NU, u + 1))
                if u == 0:
                    pe.wait_ge(on.x_k, upto(r))
                    pe.wait_ge(on.x_kl, upto(r))
                else:
                    pe.wait_ge(on.x_pT, upto(r, NU, u))
                for i in range(UH):
                    ins = pe.transpose(X1[0:S2, i * P:(i + 1) * P], prob[:, u % 2, i, :], ident[:])
                ins.then_inc(on.x_pT_ps, 1)

            def x_av(r, u):
                c, q = divmod(u, QU)
                if u == 0:
                    pe.wait_ge(on.x_v, upto(r))
                elif q == 0:
                    pe.wait_ge(on.x_o, upto(r, TC, c))
                pe.wait_ge(on.x_pT, upto(r, NU, u + 1))
                for i in range(UH):
                    h = q * UH + i
                    ins = mm(X2[:, h * (HD + 1):(h + 1) * (HD + 1)], probT[:, u % 2, i, :], Vx[:, h, :])
                ins.then_inc(on.x_av_ps, 1)

            def x_ot(r):
                pe.wait_ge(on.x_o, upto(r, TC))
                turn(X1, xo).then_inc(on.x_oT_ps, 1)

            def x_proj(r):
                pe.wait_ge(on.x_oT, upto(r))
                pe.wait_ge(on.x_oTl, upto(r))
                tokens_halves(X0, xoT, xwp).then_inc(on.x_proj_ps, 1)

            def f_turn(r):
                if later(r):
                    pe.wait_ge(on.f_y, upto(before(r)))
                pe.wait_ge(on.xn["f"], upto(r))
                turn(F0, xn["f"]).then_inc(on.xnT_ps["f"], 1)

            def f_gate(r):
                pe.wait_ge(on.xnT["f"], upto(r))
                pe.wait_ge(on.f_xnTl, upto(r))
                if later(r):
                    pe.wait_ge(on.f_sT, upto(before(r), TC))
                    pe.wait_ge(on.f_sTl, upto(before(r), TC))
                mm_halves(F1[0:NE, 0:T], [
                    (lambda i, k=k: fgate[i][:, k, :], lambda i, k=k: xnT["f"][i][:, k, :]) for k in range(KC)
                ]).then_inc(on.f_gate_ps, 1)

            def f_lg(r):
                pe.wait_ge(on.f_lgT, upto(r))
                for c in range(TC):
                    ins = mm(F1[:, T + c * NE:T + (c + 1) * NE], lgT[:, c * P:(c + 1) * P], ident[0:NE, 0:NE])
                ins.then_inc(on.f_lg_ps, 1)

            def f_up(c, dst, w):
                return mm_halves(dst[:, :], [
                    (lambda i, k=k: xnT["f"][i][:, k, c * P:(c + 1) * P], lambda i, k=k: w[i][:, k, :])
                    for k in range(KC)])

            def f_u0(r):
                pe.wait_ge(on.xnT["f"], upto(r))
                pe.wait_ge(on.f_xnTl, upto(r))
                f_up(0, F0, fwu).then_inc(on.f_u_ps, 1)

            def f_v0(r):
                pe.wait_ge(on.f_logit, upto(r))
                f_up(0, F1, fwv).then_inc(on.f_v_ps, 1)

            def f_u1(r):
                pe.wait_ge(on.f_s, upto(r, TC, 1))
                f_up(1, F1, fwu).then_inc(on.f_u_ps, 1)

            def f_v1(r):
                pe.wait_ge(on.f_sT, upto(r, TC, 1))
                pe.wait_ge(on.f_sTl, upto(r, TC, 1))
                f_up(1, F0, fwv).then_inc(on.f_v_ps, 1)

            def f_st(r, c):
                pe.wait_ge(on.f_sw, upto(r, TC, c + 1))
                pe.wait_ge(on.f_su, upto(r, TC, c + 1))
                dst = F0 if c == 0 else F1
                for i in range(RC):
                    ins = pe.transpose(dst[:, i * P:(i + 1) * P], fs[:, c, i * P:(i + 1) * P], ident[:])
                ins.then_inc(on.f_sT_ps, 1)

            def f_yy(r):
                pe.wait_ge(on.f_sT, upto(r, TC))
                pe.wait_ge(on.f_sTl, upto(r, TC))
                pe.wait_ge(on.f_s, upto(r, TC))
                for c in range(TC):
                    ins = mm_halves(F0[:, c * D:(c + 1) * D], [
                        (lambda h, i=i: fsT[h][:, c, i, :], lambda h, i=i: fwo[h][:, i, :]) for i in range(RC)])
                ins.then_inc(on.f_y_ps, 1)

            def body(rn, ra, rx, rf):
                def N(f, *k):
                    if rn is not None:
                        f(rn, *k)

                def A(f, *k):
                    if ra is not None:
                        f(ra, *k)

                def X(f, *k):
                    if rx is not None:
                        f(rx, *k)

                def F(f, *k):
                    if rf is not None:
                        f(rf, *k)

                X(x_k); A(a_ktok); A(a_A, 0); X(x_v); X(x_turn); A(a_A, 1); A(a_state); F(f_turn); N(a_turn)
                X(x_q); F(f_gate); A(a_ok); X(x_s, 0); F(f_lg); N(a_qk); F(f_u0); X(x_s, 1); N(a_v); X(x_pt, 0)
                F(f_v0); X(x_s, 2); N(a_s); X(x_pt, 1); X(x_av, 0); X(x_s, 3); A(a_qt); X(x_pt, 2); X(x_av, 1)
                N(a_g); F(f_st, 0); A(a_P, 0); X(x_s, 4); A(a_P, 1); X(x_pt, 3); X(x_av, 2); X(x_s, 5); A(a_o)
                F(f_u1); X(x_pt, 4); X(x_s, 6); F(f_v1); X(x_av, 3); N(a_c); X(x_pt, 5); X(x_s, 7); X(x_av, 4)
                X(x_pt, 6); X(x_av, 5); A(a_ot); X(x_pt, 7); F(f_st, 1); X(x_av, 6); X(x_av, 7); A(a_wo)
                X(x_ot); F(f_yy); X(x_proj); N(a_et); N(a_vtok)

            def others():
                pe.wait_ge(ld_v, V_LANDED)
                pe.wait_ge(w_hi, ALL_SPLIT)
                pe.wait_ge(w_lo, ALL_SPLIT)
                pe.wait_ge(z_ready, 4)

            pe.wait_ge(ld_w, W_LANDED)
            pe.wait_ge(w_ready, 4)
            pe.wait_ge(w_hi, len(splits))
            pe.wait_ge(w_lo, len(splits))
            iterations(body, others, pe)

        @block.vector
        def _(dve):
            tt, ts, stt = dve.tensor_tensor, dve.tensor_scalar, dve.scalar_tensor_tensor

            def norm_stats(s, src, r):
                for c in range(TC):
                    dve.bn_stats(ln_stats[s][:, c, :], src[:, c, :]).then_inc(on.stats[s], 1)
                dve.wait_ge(on.stats[s], upto(r, TC))
                hold(dve, dve_scrap)
                for c in range(TC):
                    dve.bn_aggr(ln_mv[s][:, c, :], ln_stats[s][:, c, :]).then_inc(on.mv[s], 1)
                dve.wait_ge(on.mv[s], upto(r, TC))
                ts(ln_ve[s][:], ln_mv[s][:, :, 1], EPS, None, ALU.add).then_inc(on.ve[s], 1)

            def norm_apply(s, src, r):
                dve.wait_ge(on.rstd[s], upto(r))
                if later(r):
                    dve.wait_ge(on.xnT_ps[s], upto(before(r)))
                for c in range(TC):
                    ins = ts(xn[s][:, c, :], src[:, c, :], ln_mv[s][:, c, 0:1], ln_rstd[s][:, c:c + 1],
                             ALU.subtract, ALU.mult)
                ins.then_inc(on.xn[s], 1)

            def heads(ap):
                return ap.rearrange("p (g m) -> p g m", m=M)

            def flat(t):
                return t[:].rearrange("p c d -> p (c d)")

            def spread(small, n):
                return small.rearrange("p (g o) -> p g o", o=1).broadcast_to([P, small.shape[1], n])

            def low(lo, src, hi):
                return tt(flat(lo), src, flat(hi).bitcast(F32), ALU.subtract)

            def a_xntl(r):
                dve.wait_ge(on.xnT["a"], upto(r))
                low(xnT["a"][1], E0[:, :], xnT["a"][0]).then_inc(on.a_xnTl, 1)

            def a_norm1(r):
                dve.wait_ge(ld_x[r.parity], loaded(r))
                norm_stats("a", x0[r.parity], r)

            def a_norm2(r):
                norm_apply("a", x0[r.parity], r)

            def a_clip(r):
                dve.wait_ge(on.a_s_ps, upto(r))
                if second(r):
                    dve.wait_ge(on.a_ok_ps, upto(two_before(r)))
                ts(flat(E[r.parity]), E0[:, :], -CLIP, CLIP, ALU.max, ALU.min).then_inc(on.a_sc, 1)

            def a_gate(r):
                dve.wait_ge(on.a_gt, upto(r))
                g = flat(gate[r.parity])
                stt(g, g, 1.0, E0[:, :], ALU.add, ALU.mult).then_inc(on.a_gate, 1)

            def a_conv(r):
                dve.wait_ge(on.a_tap0, upto(r))
                n = 0
                for i in range(1, TAPS):
                    for j in range(4):
                        n += 1
                        if i > 1:
                            dve.wait_ge(on.a_conv, upto(r, 3 * 4, n - 4))
                        stt(conv[:, j, :], raw[:, j, i:i + T], cw[:, j, i:i + 1], conv[:, j, :],
                                 ALU.mult, ALU.add).then_inc(on.a_conv, 1)

            def a_silu_qk(r):
                dve.wait_ge(on.a_convt, upto(r, 2, 1))
                stt(qkv[:, 0:2, :], qkv[:, 0:2, :], 1.0, conv[:, 0:2, :], ALU.add, ALU.mult).then_inc(on.a_qk, 1)

            def a_rot(r):
                dve.wait_ge(on.a_qk, upto(r))
                hold(dve, dve_scrap)
                dve.stream_shuffle(rot, qkv[:, 0:2, :],
                                        [(i + KD // 2) % KD for i in range(KD)]).then_inc(on.a_rot, 1)

            def a_silu_v(r):
                dve.wait_ge(on.a_convt, upto(r, 2, 2))
                stt(qkv[:, 2:4, :], qkv[:, 2:4, :], 1.0, conv[:, 2:4, :], ALU.add, ALU.mult).then_inc(on.a_v, 1)

            def a_qbd(r):
                dve.wait_ge(on.a_kr, upto(r))
                if second(r):
                    dve.wait_ge(on.a_ok_ps, upto(two_before(r)))
                for h in range(H):
                    s = slice(h * KD, (h + 1) * KD)
                    ins = dve.tensor_copy(q_bd[r.parity][s, h, :], qkr[r.parity][s, 0, :])
                ins.then_inc(on.a_qbd, 1)

            def a_rc(r):
                dve.wait_ge(on.a_C_ps, upto(r))
                if second(r):
                    dve.wait_ge(on.a_qn, upto(two_before(r)))
                dve.reciprocal(flat(rC[r.parity]), E0[:, :]).then_inc(on.a_rC, 1)

            def causal(dst, src):
                return tt(dst, src.rearrange("p (h t) -> p h t", h=H),
                          tri.rearrange("p (o t) -> p o t", o=1).broadcast_to([P, H, P]), ALU.mult)

            def a_maskA(r, c):
                dve.wait_ge(on.a_A_ps, upto(r, TC, c + 1))
                causal(AT[:, c], (A0 if c == 0 else A1)[:, :]).then_inc(on.a_A, 1)

            def a_state(r):
                dve.wait_ge(on.a_state_ps, upto(r))
                tt(heads(state[:]), heads(A0[:, :]), spread(blockmask[:], M), ALU.mult).then_inc(on.a_state, 1)

            def a_okn(r):
                dve.wait_ge(on.a_ok_ps, upto(r))
                tt(flat(okn), A1[:, :], flat(rC[r.parity]), ALU.mult).then_inc(on.a_okn, 1)
                dve.wait_ge(on.a_okn, upto(r))
                dve.tensor_reduce(okmax[:], heads(flat(okn)), AX.X, ALU.max).then_inc(on.a_max, 1)

            def a_sum(r):
                dve.wait_ge(on.a_oke, upto(r))
                dve.tensor_reduce(ssum[:], heads(flat(okn)), AX.X, ALU.add).then_inc(on.a_sum, 1)
                dve.wait_ge(on.a_sum, upto(r))
                tt(ssq[:], ssum[:], ssum[:], ALU.mult).then_inc(on.a_ssq, 1)

            def a_maskP(r, c):
                dve.wait_ge(on.a_P_ps, upto(r, TC, c + 1))
                causal(PT[:, c], (A1 if c == 0 else A0)[:, :]).then_inc(on.a_P, 1)

            def a_oss(r):
                dve.wait_ge(on.a_osq, upto(r))
                dve.tensor_reduce(oss[:], heads(flat(osq)), AX.X, ALU.add).then_inc(on.a_oss, 1)
                dve.wait_ge(on.a_oss, upto(r))
                dve.wait_ge(on.a_ssq, upto(r))
                stt(ove[:], ssq[:], 4 * EPS * VD, oss[:], ALU.mult, ALU.add).then_inc(on.a_ove, 1)

            def a_o1(r):
                dve.wait_ge(on.a_orinv, upto(r))
                dve.wait_ge(on.a_o_ps, upto(r))
                tt(heads(flat(o1)), heads(A1[:, :]), spread(orinv[:], VD), ALU.mult).then_inc(on.a_o1, 1)

            def a_otl(r):
                dve.wait_ge(on.a_oT, upto(r))
                low(oT[1], A0[:, :], oT[0]).then_inc(on.a_oTl, 1)

            def a_out(r):
                dve.wait_ge(on.a_wo_ps, upto(r))
                if second(r):
                    dve.wait_ge(on.x_x2, upto(two_before(r)))
                tt(flat(x1[r.parity]), A1[:, :], flat(x0[r.parity]), ALU.add).then_inc(on.a_x1, 1)

            def x_norm1(r):
                dve.wait_ge(on.a_x1, upto(r))
                norm_stats("x", x1[r.parity], r)

            def x_norm2(r):
                norm_apply("x", x1[r.parity], r)

            def x_xntl(r):
                dve.wait_ge(on.xnT["x"], upto(r))
                low(xnT["x"][1], X0[:, :], xnT["x"][0]).then_inc(on.x_xnTl, 1)

            def x_otl(r):
                dve.wait_ge(on.x_oT, upto(r))
                low(xoT[1], X1[:, :], xoT[0]).then_inc(on.x_oTl, 1)

            def x_kl(r):
                dve.wait_ge(on.x_k, upto(r))
                src = X1[:, 0:KC * S2].rearrange("p (f s) -> p f s", f=KC)
                for i in range(2):
                    rows = slice(i * P // 2, (i + 1) * P // 2)
                    ins = tt(KT_lo[rows], src[rows], K_stack[rows, i::2, :].bitcast(F32), ALU.subtract)
                ins.then_inc(on.x_kl, 1)

            def x_ql(r):
                dve.wait_ge(on.x_q, upto(r))
                src = X0[:, :].rearrange("p (f t) -> p f t", f=KC)
                for i in range(2):
                    rows, other = [slice(j * P // 2, (j + 1) * P // 2) for j in (i, 1 - i)]
                    ins = stt(Q_stack[other, i::2, :], src[rows], -HD ** -0.5, Q_stack[rows, i::2, :].bitcast(F32),
                              ALU.mult, ALU.subtract)
                ins.then_inc(on.x_ql, 1)

            def x_neg(r):
                dve.wait_ge(ld_c[r.parity], loaded(r, 2))
                if later(r):
                    dve.wait_ge(on.x_s_ps, upto(before(r), NU))
                ts(flat(negmask), keep[r.parity][:].rearrange("p c s -> p (c s)"), 0.0, MASKED,
                        ALU.is_equal, ALU.mult).then_inc(on.x_neg, 1)

            def x_soft(r, u):
                dve.wait_ge(on.x_s_ps, upto(r, NU, u + 1))
                if u >= 2:
                    dve.wait_ge(on.x_prob, upto(r, NU, u - 1))
                elif later(r):
                    dve.wait_ge(on.x_prob, upto(before(r), NU, NU - 1 + u))
                dve.tensor_reduce(nmax[:, u % 2, :], X0[:, 0:UH * S2].rearrange("p (h s) -> p h s", h=UH), AX.X,
                                  ALU.min).then_inc(on.x_max, 1)

            def x_o(r, c):
                dve.wait_ge(on.x_av_ps, upto(r, NU, (c + 1) * QU))
                src = X2[:, 0:NH * (HD + 1)].rearrange("p (h e) -> p h e", h=NH)
                dve.reciprocal(xrs[:, c, :], src[:, :, HD]).then_inc(on.x_rs, 1)
                dve.wait_ge(on.x_rs, upto(r, TC, c + 1))
                if c == 0:
                    if later(r):
                        dve.wait_ge(on.x_oT_ps, upto(before(r)))
                tt(xo[:, c, :].rearrange("p (h e) -> p h e", h=NH), src[:, :, 0:HD],
                        spread(xrs[:, c, :], HD), ALU.mult).then_inc(on.x_o, 1)

            def x_out(r):
                dve.wait_ge(on.x_proj_ps, upto(r))
                dve.wait_ge(on.x_x1b, upto(r))
                if second(r):
                    dve.wait_ge(st_y[r.parity], r.half * 16)
                tt(flat(x2[r.parity]), X0[:, :], flat(x1[r.parity]), ALU.add).then_inc(on.x_x2, 1)

            def f_norm1(r):
                dve.wait_ge(on.x_x2, upto(r))
                norm_stats("f", x2[r.parity], r)

            def f_norm2(r):
                norm_apply("f", x2[r.parity], r)

            def f_xntl(r):
                dve.wait_ge(on.xnT["f"], upto(r))
                low(xnT["f"][1], F0[:, :], xnT["f"][0]).then_inc(on.f_xnTl, 1)

            def f_top(r):
                dve.wait_ge(on.f_lg_ps, upto(r))
                dve.tensor_copy(flat(logit), F1[:, T:T + TC * NE]).then_inc(on.f_logit, 1)
                dve.wait_ge(on.f_logit, upto(r))
                hold(dve, dve_scrap)
                for c in range(TC):
                    dve.max(top[:, c, :], logit[:, c, :]).then_inc(on.f_top, 1)
                dve.wait_ge(on.f_top, upto(r, TC))
                hold(dve, dve_scrap)
                for c in range(TC):
                    dve.max_index(topi[:, c, :], top[:, c, :], logit[:, c, :]).then_inc(on.f_topi, 1)
                tt(gap[:], top[:, :, 1], top[:, :, 0], ALU.subtract).then_inc(on.f_gap, 1)
                dve.wait_ge(on.f_topi, upto(r, TC))
                dve.tensor_copy(flat(topf), topi[:].rearrange("p c n -> p (c n)")).then_inc(on.f_topf, 1)

            def f_weights(r):
                dve.wait_ge(on.f_egap, upto(r))
                ts(gden[:], egap[:], 1.0, 2.0, ALU.add, ALU.mult).then_inc(on.f_gden, 1)
                dve.wait_ge(on.f_gden, upto(r))
                dve.reciprocal(gw[:, 0, :], gden[:]).then_inc(on.f_gw1, 1)
                dve.wait_ge(on.f_gw1, upto(r))
                tt(gw[:, 1, :], gw[:, 0, :], egap[:], ALU.mult).then_inc(on.f_gw2, 1)
                dve.wait_ge(on.f_topf, upto(r))
                dve.wait_ge(on.f_gw2, upto(r))
                for c in range(TC):
                    ts(wt1[:, c, :], iota8[:], topf[:, c, 0:1], gw[:, 0, c:c + 1], ALU.is_equal, ALU.mult)
                    ins = ts(wt2[:, c, :], iota8[:], topf[:, c, 1:2], gw[:, 1, c:c + 1], ALU.is_equal, ALU.mult)
                ins.then_inc(on.f_wt12, 1)
                dve.wait_ge(on.f_wt12, upto(r))
                if later(r):
                    dve.wait_ge(on.f_sw, upto(before(r), TC))
                tt(flat(wt), flat(wt1), flat(wt2), ALU.add).then_inc(on.f_wt, 1)

            def f_s(r, c):
                dve.wait_ge(on.f_th, upto(r, TC, c + 1))
                stt(fth[:], fth[:], 1.0, (F0 if c == 0 else F1)[:, :], ALU.add, ALU.mult).then_inc(on.f_su, 1)
                dve.wait_ge(on.f_su, upto(r, TC, c + 1))
                dve.wait_ge(on.f_v_ps, upto(r, TC, c + 1))
                if later(r):
                    dve.wait_ge(on.f_sT_ps, upto(before(r), TC, c + 1))
                tt(fs[:, c, :], (F1 if c == 0 else F0)[:, :], fth[:], ALU.mult).then_inc(on.f_s, 1)

            def f_stl(r, c):
                dve.wait_ge(on.f_sT, upto(r, TC, c + 1))
                hi, lo = [fsT[i][:, c].rearrange("p i t -> p (i t)") for i in range(2)]
                tt(lo, (F0 if c == 0 else F1)[:, :], hi.bitcast(F32), ALU.subtract).then_inc(on.f_sTl, 1)

            def f_out(r):
                dve.wait_ge(on.f_y_ps, upto(r))
                tt(flat(x2[r.parity]), F0[:, :], flat(x2[r.parity]), ALU.add).then_inc(on.f_y, 1)

            def body(rn, ra, rx, rf):
                def N(f, *k):
                    if rn is not None:
                        f(rn, *k)

                def A(f, *k):
                    if ra is not None:
                        f(ra, *k)

                def X(f, *k):
                    if rx is not None:
                        f(rx, *k)

                def F(f, *k):
                    if rf is not None:
                        f(rf, *k)

                X(x_norm1); F(f_norm1); X(x_norm2); N(a_norm1); A(a_maskA, 0); X(x_kl); F(f_norm2); N(a_norm2)
                X(x_xntl); A(a_maskA, 1); F(f_xntl); A(a_state); X(x_neg); X(x_ql); N(a_xntl); X(x_soft, 0)
                A(a_okn); F(f_top); X(x_soft, 1); F(f_weights); X(x_soft, 2); F(f_s, 0); A(a_sum); N(a_clip)
                X(x_soft, 3); N(a_conv); X(x_soft, 4); A(a_maskP, 0); A(a_maskP, 1); N(a_gate); N(a_silu_qk)
                F(f_stl, 0); X(x_soft, 5); A(a_oss); X(x_soft, 6); N(a_rot); F(f_s, 1); X(x_o, 0); A(a_o1)
                X(x_soft, 7); N(a_rc); A(a_otl); F(f_stl, 1); X(x_o, 1); N(a_silu_v); N(a_qbd); X(x_otl)
                A(a_out); F(f_out); X(x_out)

            def split(pairs, before):
                for i, (w, w_raw) in enumerate(pairs):
                    dve.wait_ge(w_hi, before + i + 1)
                    tt(full(w[1]), w_raw, full(w[0]).bitcast(F32), ALU.subtract).then_inc(w_lo, 1)

            def others():
                dve.wait_ge(ld_v, V_LANDED)
                ts(wo_normed, wo_raw, gnorm[:, 0:1], 0.5 * VD ** 0.5, ALU.mult, ALU.mult
                   ).then_inc(w_ready, 1)
                split(other_splits, len(splits))
                dve.wait_ge(z_ready, 4)

            dve.memset(mhalf[:], -0.5).then_inc(w_ready, 1)
            dve.memset(ones[:], 1.0).then_inc(w_ready, 1)
            dve.wait_ge(w_ready, 2)
            dve.tensor_copy(ones_r[:], ones[:])
            dve.wait_ge(ld_w, W_LANDED)
            dve.tensor_copy(tri_r[:], tri_raw).then_inc(w_ready, 1)
            dve.tensor_copy(ident_bf[:], ident[:]).then_inc(w_ready, 1)
            split(splits, 0)
            dve.wait_ge(z_ready, 4)
            dve.wait_ge(w_ready, 4)
            iterations(body, others, dve)

        @block.scalar
        def _(act):
            def flat(t):
                return t[:].rearrange("p c d -> p (c d)")

            def a_xnt(r):
                if later(r):
                    act.wait_ge(on.a_g_ps, upto(before(r)))
                act.wait_ge(on.xnT_ps["a"], upto(r))
                act.activation(flat(xnT["a"][0]), E0[:, :], ACT.Copy).then_inc(on.xnT["a"], 1)

            def a_raw_qk(r):
                if later(r):
                    act.wait_ge(on.a_conv, upto(before(r), 3 * 4))
                act.wait_ge(on.a_qk_ps, upto(r))
                act.activation(raw[:, 0:2, TAPS - 1:], E0[:, :].rearrange("p (j t) -> p j t", j=2), ACT.Copy
                               ).then_inc(on.a_qk_raw, 1)

            def a_raw_v(r):
                if later(r):
                    act.wait_ge(on.a_conv, upto(before(r), 3 * 4))
                act.wait_ge(on.a_v_ps, upto(r))
                act.activation(raw[:, 2:4, TAPS - 1:], E0[:, :].rearrange("p (j t) -> p j t", j=2), ACT.Copy
                               ).then_inc(on.a_v_raw, 1)

            def a_e(r):
                act.wait_ge(on.a_sc, upto(r))
                act.activation(flat(E[r.parity]), flat(E[r.parity]), ACT.Exp).then_inc(on.a_E, 1)

            def a_ehi(r):
                act.wait_ge(on.a_E, upto(r))
                if later(r):
                    act.wait_ge(on.a_C_ps, upto(before(r)))
                act.activation(flat(E_halves[0]), flat(E[r.parity]), ACT.Copy).then_inc(on.a_Ehi, 1)

            def a_gt(r):
                act.wait_ge(on.a_g_ps, upto(r))
                if second(r):
                    act.wait_ge(on.a_o2, upto(two_before(r)))
                act.activation(flat(gate[r.parity]), E0[:, :], ACT.Tanh, scale=0.5).then_inc(on.a_gt, 1)

            def a_convt(r, j):
                act.wait_ge(on.a_conv, upto(r, 3 * 4, 3 * 4 - 2 + 2 * j))
                if later(r):
                    act.wait_ge(on.a_kr if j == 0 else on.a_vtok_ps, upto(before(r)))
                act.activation(qkv[:, 2 * j:2 * j + 2, :], conv[:, 2 * j:2 * j + 2, :], ACT.Tanh,
                               scale=0.5).then_inc(on.a_convt, 1)

            def a_et(r):
                if second(r):
                    act.wait_ge(on.a_P_ps, upto(two_before(r), TC))
                act.wait_ge(on.a_ET_ps, upto(r))
                act.activation(flat(ET[r.parity]), E0[:, :], ACT.Copy).then_inc(on.a_ET, 1)

            def a_ktok(r):
                if later(r):
                    act.wait_ge(on.a_o_ps, upto(before(r)))
                act.wait_ge(on.a_ktok_ps, upto(r))
                act.activation(ktok[:], A1[:, 0:P], ACT.Copy).then_inc(on.a_ktok, 1)

            def a_vtok(r):
                if second(r):
                    act.wait_ge(on.a_o_ps, upto(two_before(r)))
                act.wait_ge(on.a_vtok_ps, upto(r))
                act.activation(flat(vtok[r.parity]), E0[:, :], ACT.Copy).then_inc(on.a_vtok, 1)

            def a_oke(r):
                act.wait_ge(on.a_oks, upto(r))
                act.activation(flat(okn), flat(okn), ACT.Exp, scale=KD ** -0.5 / 4).then_inc(on.a_oke, 1)

            def a_qnt(r):
                act.wait_ge(on.a_qnT_ps, upto(r))
                src = A0[:, :].rearrange("p (f t) -> p f t", f=2)
                for hh in range(2):
                    s = slice(hh * M, (hh + 1) * M)
                    act.activation(qn_bd[s, :, hh, :], src[s], ACT.Copy).then_inc(on.a_qnT, 1)
                act.activation(qn_last[:], src[:, :, P:2 * P], ACT.Copy).then_inc(on.a_qnT, 1)

            def a_osq(r):
                act.wait_ge(on.a_o_ps, upto(r))
                act.activation(flat(osq), A1[:, :], ACT.Square).then_inc(on.a_osq, 1)

            def a_ot(r):
                act.wait_ge(on.a_oT_ps, upto(r))
                act.activation(flat(oT[0]), A0[:, :], ACT.Copy).then_inc(on.a_oT, 1)

            def x_k(r):
                if later(r):
                    act.wait_ge(on.x_kbd, upto(before(r)))
                act.wait_ge(on.x_k_ps, upto(r))
                src = X1[:, 0:KC * S2].rearrange("p (f s) -> p f s", f=KC)
                for i in range(2):
                    rows, other = [slice(j * P // 2, (j + 1) * P // 2) for j in (i, 1 - i)]
                    act.activation(K_stack[rows, i::2, :], src[rows], ACT.Copy)
                    ins = act.activation(K_stack[other, i::2, :], src[rows], ACT.Copy)
                ins.then_inc(on.x_k, 1)

            def x_v(r):
                if later(r):
                    act.wait_ge(on.x_av_ps, upto(before(r), NU))
                act.wait_ge(on.x_v_ps, upto(r))
                act.activation(Vx[:, :, 0:HD], X2[0:S2, 0:D].rearrange("p (h e) -> p h e", h=NH), ACT.Copy
                               ).then_inc(on.x_v, 1)

            def x_xnt(r):
                act.wait_ge(on.xnT_ps["x"], upto(r))
                act.activation(flat(xnT["x"][0]), X0[:, :], ACT.Copy).then_inc(on.xnT["x"], 1)

            def x_q(r):
                if later(r):
                    act.wait_ge(on.x_s_ps, upto(before(r), NU))
                act.wait_ge(on.x_q_ps, upto(r))
                src = X0[:, :].rearrange("p (f t) -> p f t", f=KC)
                for i in range(2):
                    rows = slice(i * P // 2, (i + 1) * P // 2)
                    ins = act.activation(Q_stack[rows, i::2, :], src[rows], ACT.Copy, scale=-HD ** -0.5)
                ins.then_inc(on.x_q, 1)

            def x_prob(r, u):
                act.wait_ge(on.x_max, upto(r, NU, u + 1))
                if u >= 2:
                    act.wait_ge(on.x_pT_ps, upto(r, NU, u - 1))
                else:
                    if later(r):
                        act.wait_ge(on.x_pT_ps, upto(before(r), NU, NU - 1 + u))
                for i in range(UH):
                    ins = act.activation(prob[:, u % 2, i, :], X0[:, i * S2:(i + 1) * S2], ACT.Exp, scale=-1.0,
                                         bias=nmax[:, u % 2, i:i + 1])
                ins.then_inc(on.x_prob, 1)

            def x_pt(r, u):
                act.wait_ge(on.x_pT_ps, upto(r, NU, u + 1))
                if u >= 2:
                    act.wait_ge(on.x_av_ps, upto(r, NU, u - 1))
                else:
                    if later(r):
                        act.wait_ge(on.x_av_ps, upto(before(r), NU, NU - 1 + u))
                act.activation(probT[:, u % 2].rearrange("p h t -> p (h t)"), X1[0:S2, :], ACT.Copy
                               ).then_inc(on.x_pT, 1)

            def x_ot(r):
                act.wait_ge(on.x_oT_ps, upto(r))
                act.activation(flat(xoT[0]), X1[:, :], ACT.Copy).then_inc(on.x_oT, 1)

            def f_xnt(r):
                act.wait_ge(on.xnT_ps["f"], upto(r))
                act.activation(flat(xnT["f"][0]), F0[:, :], ACT.Copy).then_inc(on.xnT["f"], 1)

            def f_lgt(r):
                act.wait_ge(on.f_gate_ps, upto(r))
                if later(r):
                    act.wait_ge(on.f_s, upto(before(r), TC))
                act.activation(lgT, F1[0:NE, 0:T], ACT.Copy).then_inc(on.f_lgT, 1)

            def f_gap(r):
                act.wait_ge(on.f_gap, upto(r))
                act.activation(egap[:], gap[:], ACT.Exp).then_inc(on.f_egap, 1)

            def f_th(r, c):
                act.wait_ge(on.f_u_ps, upto(r, TC, c + 1))
                if c == 1:
                    act.wait_ge(on.f_s, upto(r, TC, 1))
                act.activation(fth[:], (F0 if c == 0 else F1)[:, :], ACT.Tanh, scale=0.5).then_inc(on.f_th, 1)

            def f_st(r, c):
                act.wait_ge(on.f_sT_ps, upto(r, TC, c + 1))
                act.activation(fsT[0][:, c].rearrange("p i t -> p (i t)"), (F0 if c == 0 else F1)[:, :],
                                    ACT.Copy).then_inc(on.f_sT, 1)

            def body(rn, ra, rx, rf):
                def N(f, *k):
                    if rn is not None:
                        f(rn, *k)

                def A(f, *k):
                    if ra is not None:
                        f(ra, *k)

                def X(f, *k):
                    if rx is not None:
                        f(rx, *k)

                def F(f, *k):
                    if rf is not None:
                        f(rf, *k)

                X(x_k); A(a_ktok); X(x_xnt); F(f_xnt); X(x_q); N(a_xnt); F(f_lgt); X(x_prob, 0); N(a_raw_qk)
                F(f_gap); X(x_v); X(x_prob, 1); N(a_raw_v); A(a_oke); X(x_pt, 0); F(f_th, 0); X(x_prob, 2)
                X(x_pt, 1); A(a_qnt); X(x_prob, 3); X(x_pt, 2); N(a_e); N(a_ehi); N(a_gt); F(f_st, 0)
                X(x_prob, 4); X(x_pt, 3); N(a_convt, 0); X(x_prob, 5); A(a_osq); X(x_pt, 4); F(f_th, 1)
                X(x_prob, 6); X(x_pt, 5); X(x_prob, 7); X(x_pt, 6); A(a_ot); X(x_pt, 7); N(a_convt, 1)
                F(f_st, 1); X(x_ot); N(a_et); N(a_vtok)

            def split(pairs):
                for w, w_raw in pairs:
                    act.activation(full(w[0]), w_raw, ACT.Copy).then_inc(w_hi, 1)

            def others():
                act.wait_ge(ld_v, V_LANDED)
                act.wait_ge(w_ready, 5)
                split(other_splits)
                act.wait_ge(z_ready, 4)

            act.wait_ge(ld_w, W_LANDED)
            split(splits)
            iterations(body, others, act)

        @block.gpsimd
        def _(pool):
            def heads(t):
                return t[:].rearrange("p c (h m) -> p (c h) m", m=M)

            def spread(small, n):
                return small.rearrange("p (g o) -> p g o", o=1).broadcast_to([P, small.shape[1], n])

            def rstd(s, r):
                pool.wait_ge(on.ve[s], upto(r))
                if later(r):
                    pool.wait_ge(on.xn[s], upto(before(r)))
                pool.tensor_tensor(ln_rstd[s][:], ln_ve[s][:], mhalf[:, 0:TC], ALU.pow).then_inc(on.rstd[s], 1)

            def a_rstd(r):
                rstd("a", r)

            def x_rstd(r):
                rstd("x", r)

            def f_rstd(r):
                rstd("f", r)

            def a_tap0(r):
                pool.wait_ge(on.a_v_raw, upto(r))
                pool.wait_ge(on.a_qk_raw, upto(r))
                if later(r):
                    pool.wait_ge(on.a_v, upto(before(r)))
                    pool.wait_ge(on.a_kr, upto(before(r)))
                hold(pool, pool_scrap)
                for j in range(4):
                    ins = pool.tensor_scalar(conv[:, j, :], raw[:, j, 0:T], cw[:, j, 0:1], 1.0, ALU.mult, ALU.mult)
                ins.then_inc(on.a_tap0, 1)

            def a_elo(r):
                pool.wait_ge(on.a_Ehi, upto(r))
                pool.tensor_tensor(E_halves[1][:], E[r.parity][:], E_halves[0][:].bitcast(F32), ALU.subtract
                                   ).then_inc(on.a_Elo, 1)

            def a_cos(r):
                pool.wait_ge(on.a_qk, upto(r))
                if second(r):
                    pool.wait_ge(on.a_ok_ps, upto(two_before(r)))
                pool.tensor_tensor(qkr[r.parity][:], qkv[:, 0:2, :],
                                   cosT[:].rearrange("p (o t) -> p o t", o=1).broadcast_to([P, 2, T]),
                                   ALU.mult).then_inc(on.a_cos, 1)

            def a_sin(r):
                pool.wait_ge(on.a_rot, upto(r))
                pool.tensor_tensor(rot, rot,
                                   sinT[:].rearrange("p (o t) -> p o t", o=1).broadcast_to([P, 2, T]),
                                   ALU.mult).then_inc(on.a_sin, 1)

            def a_kr(r):
                pool.wait_ge(on.a_cos, upto(r))
                pool.wait_ge(on.a_sin, upto(r))
                pool.tensor_tensor(qkr[r.parity][:], qkr[r.parity][:], rot, ALU.add).then_inc(on.a_kr, 1)

            def a_oks(r):
                pool.wait_ge(on.a_max, upto(r))
                pool.tensor_tensor(heads(okn), heads(okn), spread(okmax[:], M), ALU.subtract).then_inc(on.a_oks, 1)

            def a_qn(r):
                pool.wait_ge(on.a_oke, upto(r))
                pool.tensor_tensor(qn[:], okn[:], rC[r.parity][:], ALU.mult).then_inc(on.a_qn, 1)

            def a_orinv(r):
                pool.wait_ge(on.a_ove, upto(r))
                pool.tensor_tensor(orinv[:], ove[:], mhalf[:], ALU.pow).then_inc(on.a_orinv, 1)

            def a_o2(r):
                pool.wait_ge(on.a_o1, upto(r))
                pool.wait_ge(on.a_gate, upto(r))
                pool.tensor_tensor(o1[:], o1[:], gate[r.parity][:], ALU.mult).then_inc(on.a_o2, 1)

            def x_kbd(r):
                pool.wait_ge(on.x_k, upto(r))
                if later(r):
                    pool.wait_ge(on.x_s_ps, upto(before(r), NU))
                pool.wait_ge(on.x_kl, upto(r))
                for q in range(QU):
                    pool.tensor_tensor(K_bd[:, q], K_stack[:, q:q + 1, :].bitcast(F32).broadcast_to([P, UH, S2]),
                                       spread(groupmask[:], S2), ALU.mult)
                for f in range(KC):
                    ins = pool.tensor_tensor(KT_lo_bd[:, f],
                                             KT_lo[:, f:f + 1, :].bitcast(F32).broadcast_to([P, HB, S2]),
                                             spread(headmask[:], S2), ALU.mult)
                ins.then_inc(on.x_kbd, 1)

            def x_x1b(r):
                pool.wait_ge(on.xn["x"], upto(r))
                pool.tensor_tensor(x1[r.parity][:], x1[r.parity][:],
                                   xbias[:].rearrange("p (o d) -> p o d", o=1).broadcast_to([P, TC, D]),
                                   ALU.add).then_inc(on.x_x1b, 1)

            def f_sw(r, c):
                pool.wait_ge(on.f_s, upto(r, TC, c + 1))
                pool.wait_ge(on.f_wt, upto(r))
                pool.tensor_tensor(fs[:, c, :].rearrange("p (e q) -> p e q", e=NE),
                                        fs[:, c, :].rearrange("p (e q) -> p e q", e=NE),
                                        spread(wt[:, c, :], R), ALU.mult).then_inc(on.f_sw, 1)

            def body(rn, ra, rx, rf):
                def N(f, *k):
                    if rn is not None:
                        f(rn, *k)

                def A(f, *k):
                    if ra is not None:
                        f(ra, *k)

                def X(f, *k):
                    if rx is not None:
                        f(rx, *k)

                def F(f, *k):
                    if rf is not None:
                        f(rf, *k)

                X(x_rstd); F(f_rstd); N(a_rstd); X(x_kbd); A(a_oks); X(x_x1b); N(a_tap0); A(a_qn); F(f_sw, 0)
                N(a_elo); N(a_cos); A(a_orinv); F(f_sw, 1); A(a_o2); N(a_sin); N(a_kr)

            pool.memset(raw[:], 0.0)
            pool.memset(Vx[:], 1.0).then_inc(z_ready, 1)
            for i in range(2):
                pool.memset(q_bd[i][:], 0.0).then_inc(z_ready, 1)
            pool.memset(qn_bd[:], 0.0).then_inc(z_ready, 1)
            def others():
                pool.wait_ge(ld_v, V_LANDED)
                pool.wait_ge(z_ready, 4)

            pool.wait_ge(ld_w, W_LANDED)
            pool.wait_ge(w_ready, 4)
            iterations(body, others, pool)


def constants():
    f32 = np.float32
    freq = (1.0 / 10000.0 ** (np.arange(0, KD, 2, dtype=f32) / f32(KD))).astype(f32)
    angle = (np.arange(T, dtype=f32)[:, None] * freq[None, :]).astype(f32)
    lane = np.arange(P) % KD
    cos = np.cos(angle)[:, lane % (KD // 2)].T
    sin = np.sin(angle)[:, lane % (KD // 2)].T * np.where(lane < KD // 2, -1.0, 1.0)[:, None]
    return {
        "ident": np.eye(P, dtype=f32),
        "tri": np.triu(np.ones((P, P), f32)),
        "cosT": np.ascontiguousarray(cos, f32),
        "sinT": np.ascontiguousarray(sin, f32),
        "headmask": (np.arange(P)[:, None] // HD == np.arange(HB)[None, :]).astype(f32),
        "groupmask": (np.arange(P)[:, None] % (P // 2) // HD == np.arange(UH)[None, :]).astype(f32),
        "blockmask": np.concatenate([np.arange(P)[:, None] // KD == np.arange(H)[None, :],
                                     np.arange(P)[:, None] // M == np.arange(H)[None, :] % 2], 1).astype(f32),
        "iota8": np.tile(np.arange(NE, dtype=f32), (P, 1)),
    }


def kernel(**inputs):
    import concourse.bacc as bacc
    from concourse.bass_utils import run_bass_kernel_spmd

    def t(name):
        return np.ascontiguousarray(np.transpose(np.asarray(inputs[name])))

    arrays = {
        "x": inputs["x"],
        "ctxT": np.transpose(np.asarray(inputs["ctx_1024"]), (0, 2, 1)),
        "mask": inputs["mask_Bx1xSxS2_bk0"],
        "Wq": inputs["L0_attn_Wq"], "Wk": inputs["L0_attn_Wk"], "Wv": inputs["L0_attn_Wv"],
        "Ws": inputs["L0_attn_Ws"], "Wg": inputs["L0_attn_Wg"], "Wo": inputs["L0_attn_Wo"],
        "qconv": inputs["L0_attn_qconv_w"], "kconv": inputs["L0_attn_kconv_w"],
        "vconv": inputs["L0_attn_vconv_w"], "gnorm": inputs["L0_attn_gnorm_w"],
        "xWqT": t("L0_xattn_W_q"), "xWkT": t("L0_xattn_W_k"), "xWvT": t("L0_xattn_W_v"),
        "xWpT": t("L0_xattn_W_proj"),
        "xbias": np.broadcast_to(np.asarray(inputs["L0_xattn_b_proj"])[None, :], (P, D)),
        "gate_w": inputs["L0_ffn_gate_w"], "fWu": inputs["L0_ffn_Wu"], "fWv": inputs["L0_ffn_Wv"],
        "fWo": inputs["L0_ffn_Wo"],
    } | constants()
    arrays = {f"in_{n}": np.ascontiguousarray(v) for n, v in arrays.items()}

    nc = bacc.Bacc("TRN2", target_bir_lowering=False, num_devices=1)
    aps = {n[3:]: nc.dram_tensor(n, v.shape, mybir.dt.from_np(v.dtype), kind="ExternalInput").ap()
           for n, v in arrays.items()}
    aps["out"] = nc.dram_tensor("out_0", (B, T, D), F32, kind="ExternalOutput").ap()
    build(nc, aps)
    return run_bass_kernel_spmd(nc, [arrays], core_ids=[0]).results[0]["out_0"]
```
